# Optimizing a Trainium2 kernel written in Bass

```python
import numpy as np
import jax
import jax.numpy as jnp

def _softmax(x, axis=-1):
    return jax.nn.softmax(x, axis=axis)

def _gelu(x):
    return jax.nn.gelu(x, approximate=True)

def _silu(x):
    return jax.nn.silu(x)

def _sigmoid(x):
    return jax.nn.sigmoid(x)

def _layernorm(x, axis=-1, eps=1e-05):
    m = jnp.mean(x, axis=axis, keepdims=True)
    v = jnp.var(x, axis=axis, keepdims=True)
    return (x - m) / jnp.sqrt(v + eps)

def _scatter_add(tgt, idx, src, axis=0):
    return tgt.at[idx].add(src)

def _segment_sum(src, seg, n):
    return jax.ops.segment_sum(src, seg, n)
kernel_name = 'mk_decoder_postln_d1_seqx_r8_a140e9'

def setup_inputs(seed: int=0):
    np.random.seed(seed)
    _w = jnp.asarray

    def _rec_inputs():
        import jax
        import jax.numpy as jnp
        _rk = jax.random.key(seed)
        x = -0.0002928 + 1 * jax.random.normal(jax.random.fold_in(_rk, 1), (32, 100, 128), jnp.float32)
        _lenS = 100 - jax.random.randint(jax.random.fold_in(_rk, 7), (32,), 0, max(1, 100 // 4) + 1, jnp.int32)
        _lenS2 = 1444 - jax.random.randint(jax.random.fold_in(_rk, 8), (32,), 0, max(1, 1444 // 4) + 1, jnp.int32)
        _ctx_1024P = jax.random.normal(jax.random.fold_in(_rk, 11), (32, 16, 128), jnp.float32)
        _ctx_1024c = jax.random.dirichlet(jax.random.fold_in(_rk, 511), 0.3 * jnp.ones((16,), jnp.float32), (32, 1444))
        _ctx_1024t = jnp.einsum('bsk,bkd->bsd', _ctx_1024c, _ctx_1024P)
        _ctx_1024t = _ctx_1024t * jax.lax.rsqrt(jnp.mean(jnp.square(_ctx_1024t)) + 1e-12) * 0.953939
        ctx_1024 = -1.39393e-06 + 0.999914 * (_ctx_1024t + 0.3 * jax.random.normal(jax.random.fold_in(_rk, 611), (32, 1444, 128), jnp.float32))
        return (x, ctx_1024)
    x, ctx_1024 = _rec_inputs()

    def _L0_attn_setup():
        import jax, jax.numpy as jnp
        import numpy as np
        import math
        B, T, C = (8, 256, 128)
        H, D = (16, 64)

        def _l2norm(v, axis=-1, eps=1e-12):
            n = jnp.sqrt(jnp.sum(v * v, axis=axis, keepdims=True))
            return v / jnp.maximum(n, eps)

        def _reference_tuple_inner(x, W_r, b_r, W_k, b_k, W_v, b_v, W_g, b_g, W_o, b_o, decay, eta, time_mix_r, time_mix_k, time_mix_v, time_mix_g, gn_weight, gn_bias):
            Bx, Tx, Cx = x.shape
            Hh = decay.shape[0]
            Dd = Cx // Hh
            x_shift = jnp.concatenate([jnp.zeros_like(x[:, :1]), x[:, :-1]], axis=1)
            x_r = x * time_mix_r + x_shift * (1 - time_mix_r)
            x_k = x * time_mix_k + x_shift * (1 - time_mix_k)
            x_v = x * time_mix_v + x_shift * (1 - time_mix_v)
            x_g = x * time_mix_g + x_shift * (1 - time_mix_g)
            r = jax.nn.sigmoid(x_r @ W_r.T + b_r).reshape(Bx, Tx, Hh, Dd)
            k = (x_k @ W_k.T + b_k).reshape(Bx, Tx, Hh, Dd)
            v = (x_v @ W_v.T + b_v).reshape(Bx, Tx, Hh, Dd)
            g = jax.nn.silu(x_g @ W_g.T + b_g)
            k = _l2norm(k)
            v = _l2norm(v)
            dec = jax.nn.sigmoid(decay)
            et = jax.nn.sigmoid(eta)
            max_norm = math.sqrt(Dd) * 2.0
            rs = jnp.transpose(r, (1, 0, 2, 3))
            ks_ = jnp.transpose(k, (1, 0, 2, 3))
            vs = jnp.transpose(v, (1, 0, 2, 3))

            def step(state, rkv):
                r_t, k_t, v_t = rkv
                pred = jnp.einsum('bhij,bhj->bhi', state, k_t)
                err = pred - v_t
                state = dec * state - et * (err[..., :, None] * k_t[..., None, :])
                n = jnp.maximum(jnp.sqrt(jnp.sum(state * state, axis=(-2, -1), keepdims=True)), 1e-08)
                state = state * jnp.where(n > max_norm, max_norm / n, 1.0)
                wkv = jnp.einsum('bhij,bhj->bhi', state, r_t)
                return (state, wkv)
            state0 = jnp.zeros((Bx, Hh, Dd, Dd), jnp.float32)
            state, wkv = jax.lax.scan(step, state0, (rs, ks_, vs))
            wkv = jnp.transpose(wkv, (1, 0, 2, 3))
            mean = jnp.mean(wkv, axis=(1, 3), keepdims=True)
            var = jnp.mean(jnp.square(wkv - mean), axis=(1, 3), keepdims=True)
            wkv_n = ((wkv - mean) / jnp.sqrt(var + 1e-05)).reshape(Bx, Tx, Cx)
            wkv_n = wkv_n * gn_weight + gn_bias
            out = (wkv_n @ W_o.T + b_o) * g
            last_x = x[:, -1:, :]
            return (out, state, last_x)
        key = jax.random.key(seed)
        ks = jax.random.split(key, 20)
        s = 1.0 / math.sqrt(C)
        inp = {'x': jax.random.normal(ks[0], (B, T, C), dtype=jnp.float32), 'W_r': jax.random.normal(ks[1], (C, C), dtype=jnp.float32) * s, 'b_r': jnp.zeros((C,), jnp.float32), 'W_k': jax.random.normal(ks[2], (C, C), dtype=jnp.float32) * s, 'b_k': jnp.zeros((C,), jnp.float32), 'W_v': jax.random.normal(ks[3], (C, C), dtype=jnp.float32) * s, 'b_v': jnp.zeros((C,), jnp.float32), 'W_g': jax.random.normal(ks[4], (C, C), dtype=jnp.float32) * s, 'b_g': jnp.zeros((C,), jnp.float32), 'W_o': jax.random.normal(ks[5], (C, C), dtype=jnp.float32) * s, 'b_o': jnp.zeros((C,), jnp.float32), 'decay': jax.random.uniform(ks[6], (H, 1, 1), jnp.float32, 2.0, 4.0), 'eta': jax.random.uniform(ks[7], (H, 1, 1), jnp.float32, -3.0, -1.0), 'time_mix_r': jnp.full((1, 1, C), 0.5, jnp.float32), 'time_mix_k': jnp.full((1, 1, C), 0.5, jnp.float32), 'time_mix_v': jnp.full((1, 1, C), 0.5, jnp.float32), 'time_mix_g': jnp.full((1, 1, C), 0.5, jnp.float32), 'gn_weight': jnp.ones((C,), jnp.float32), 'gn_bias': jnp.zeros((C,), jnp.float32)}
        return inp
    _L0_attn_all = _L0_attn_setup()
    _L0_attn_in = {k: v for k, v in _L0_attn_all.items() if k in ('W_r', 'b_r', 'W_k', 'b_k', 'W_v', 'b_v', 'W_g', 'b_g', 'W_o', 'b_o', 'decay', 'eta', 'time_mix_r', 'time_mix_k', 'time_mix_v', 'time_mix_g', 'gn_weight', 'gn_bias')}
    del _L0_attn_all

    def _L0_xattn_setup():
        import jax, jax.numpy as jnp
        import numpy as np
        N_HEADS = 16
        HIDDEN = 128
        HEAD = HIDDEN // N_HEADS
        key = jax.random.key(seed)
        ks = jax.random.split(key, 11)
        B, S, H = (2, 256, HIDDEN)
        s = 1.0 / np.sqrt(H)
        return {'query': jax.random.normal(ks[0], (B, S, H), jnp.float32), 'key': jax.random.normal(ks[1], (B, S, H), jnp.float32), 'value': jax.random.normal(ks[2], (B, S, H), jnp.float32), 'Wq': jax.random.normal(ks[3], (H, H), jnp.float32) * s, 'bq': jnp.zeros((H,), jnp.float32), 'Wk': jax.random.normal(ks[4], (H, H), jnp.float32) * s, 'bk': jnp.zeros((H,), jnp.float32), 'Wv': jax.random.normal(ks[5], (H, H), jnp.float32) * s, 'bv': jnp.zeros((H,), jnp.float32), 'Wo': jax.random.normal(ks[6], (H, H), jnp.float32) * s, 'bo': jnp.zeros((H,), jnp.float32)}
    _L0_xattn_all = _L0_xattn_setup()
    _L0_xattn_in = {k: v for k, v in _L0_xattn_all.items() if k in ('Wq', 'bq', 'Wk', 'bk', 'Wv', 'bv', 'Wo', 'bo')}
    del _L0_xattn_all

    def _L0_ffn_setup():
        import jax, jax.numpy as jnp
        import numpy as np
        B, S, D, O, E, K = (2, 256, 128, 128, 8, 2)
        key = jax.random.key(seed)
        ks = jax.random.split(key, 6)

        def w(k, shape, fan_in):
            return jax.random.normal(k, shape, jnp.float32) * fan_in ** (-0.5)
        return {'x': jax.random.normal(ks[0], (B, S, D), jnp.float32), 'gate_w': w(ks[1], (E, D), D), 'gate_b': jnp.zeros((E,), jnp.float32), 'w1': w(ks[2], (E, D, O), D), 'b1': jnp.zeros((E, O), jnp.float32), 'w2': w(ks[3], (E, O, O), O), 'b2': jnp.zeros((E, O), jnp.float32), 'w3': w(ks[4], (E, O, O), O), 'b3': jnp.zeros((E, O), jnp.float32)}
    _L0_ffn_all = _L0_ffn_setup()
    _L0_ffn_in = {k: v for k, v in _L0_ffn_all.items() if k in ('gate_w', 'gate_b', 'w1', 'b1', 'w2', 'b2', 'w3', 'b3')}
    del _L0_ffn_all
    return {'x': x, 'ctx_1024': ctx_1024, 'L0_attn_W_r': _L0_attn_in['W_r'], 'L0_attn_b_r': _L0_attn_in['b_r'], 'L0_attn_W_k': _L0_attn_in['W_k'], 'L0_attn_b_k': _L0_attn_in['b_k'], 'L0_attn_W_v': _L0_attn_in['W_v'], 'L0_attn_b_v': _L0_attn_in['b_v'], 'L0_attn_W_g': _L0_attn_in['W_g'], 'L0_attn_b_g': _L0_attn_in['b_g'], 'L0_attn_W_o': _L0_attn_in['W_o'], 'L0_attn_b_o': _L0_attn_in['b_o'], 'L0_attn_decay': _L0_attn_in['decay'], 'L0_attn_eta': _L0_attn_in['eta'], 'L0_attn_time_mix_r': _L0_attn_in['time_mix_r'], 'L0_attn_time_mix_k': _L0_attn_in['time_mix_k'], 'L0_attn_time_mix_v': _L0_attn_in['time_mix_v'], 'L0_attn_time_mix_g': _L0_attn_in['time_mix_g'], 'L0_attn_gn_weight': _L0_attn_in['gn_weight'], 'L0_attn_gn_bias': _L0_attn_in['gn_bias'], 'L0_xattn_Wq': _L0_xattn_in['Wq'], 'L0_xattn_bq': _L0_xattn_in['bq'], 'L0_xattn_Wk': _L0_xattn_in['Wk'], 'L0_xattn_bk': _L0_xattn_in['bk'], 'L0_xattn_Wv': _L0_xattn_in['Wv'], 'L0_xattn_bv': _L0_xattn_in['bv'], 'L0_xattn_Wo': _L0_xattn_in['Wo'], 'L0_xattn_bo': _L0_xattn_in['bo'], 'L0_ffn_gate_w': _L0_ffn_in['gate_w'], 'L0_ffn_gate_b': _L0_ffn_in['gate_b'], 'L0_ffn_w1': _L0_ffn_in['w1'], 'L0_ffn_b1': _L0_ffn_in['b1'], 'L0_ffn_w2': _L0_ffn_in['w2'], 'L0_ffn_b2': _L0_ffn_in['b2'], 'L0_ffn_w3': _L0_ffn_in['w3'], 'L0_ffn_b3': _L0_ffn_in['b3']}

def reference(x, ctx_1024, L0_attn_W_r, L0_attn_b_r, L0_attn_W_k, L0_attn_b_k, L0_attn_W_v, L0_attn_b_v, L0_attn_W_g, L0_attn_b_g, L0_attn_W_o, L0_attn_b_o, L0_attn_decay, L0_attn_eta, L0_attn_time_mix_r, L0_attn_time_mix_k, L0_attn_time_mix_v, L0_attn_time_mix_g, L0_attn_gn_weight, L0_attn_gn_bias, L0_xattn_Wq, L0_xattn_bq, L0_xattn_Wk, L0_xattn_bk, L0_xattn_Wv, L0_xattn_bv, L0_xattn_Wo, L0_xattn_bo, L0_ffn_gate_w, L0_ffn_gate_b, L0_ffn_w1, L0_ffn_b1, L0_ffn_w2, L0_ffn_b2, L0_ffn_w3, L0_ffn_b3):
    import jax
    import jax.numpy as jnp

    def _L0_attn_ref(x, W_r, b_r, W_k, b_k, W_v, b_v, W_g, b_g, W_o, b_o, decay, eta, time_mix_r, time_mix_k, time_mix_v, time_mix_g, gn_weight, gn_bias):
        import jax, jax.numpy as jnp
        import numpy as np
        import math
        B, T, C = (8, 256, 128)
        H, D = (16, 64)

        def _l2norm(v, axis=-1, eps=1e-12):
            n = jnp.sqrt(jnp.sum(v * v, axis=axis, keepdims=True))
            return v / jnp.maximum(n, eps)

        def _reference_tuple_inner(x, W_r, b_r, W_k, b_k, W_v, b_v, W_g, b_g, W_o, b_o, decay, eta, time_mix_r, time_mix_k, time_mix_v, time_mix_g, gn_weight, gn_bias):
            Bx, Tx, Cx = x.shape
            Hh = decay.shape[0]
            Dd = Cx // Hh
            x_shift = jnp.concatenate([jnp.zeros_like(x[:, :1]), x[:, :-1]], axis=1)
            x_r = x * time_mix_r + x_shift * (1 - time_mix_r)
            x_k = x * time_mix_k + x_shift * (1 - time_mix_k)
            x_v = x * time_mix_v + x_shift * (1 - time_mix_v)
            x_g = x * time_mix_g + x_shift * (1 - time_mix_g)
            r = jax.nn.sigmoid(x_r @ W_r.T + b_r).reshape(Bx, Tx, Hh, Dd)
            k = (x_k @ W_k.T + b_k).reshape(Bx, Tx, Hh, Dd)
            v = (x_v @ W_v.T + b_v).reshape(Bx, Tx, Hh, Dd)
            g = jax.nn.silu(x_g @ W_g.T + b_g)
            k = _l2norm(k)
            v = _l2norm(v)
            dec = jax.nn.sigmoid(decay)
            et = jax.nn.sigmoid(eta)
            max_norm = math.sqrt(Dd) * 2.0
            rs = jnp.transpose(r, (1, 0, 2, 3))
            ks_ = jnp.transpose(k, (1, 0, 2, 3))
            vs = jnp.transpose(v, (1, 0, 2, 3))

            def step(state, rkv):
                r_t, k_t, v_t = rkv
                pred = jnp.einsum('bhij,bhj->bhi', state, k_t)
                err = pred - v_t
                state = dec * state - et * (err[..., :, None] * k_t[..., None, :])
                n = jnp.maximum(jnp.sqrt(jnp.sum(state * state, axis=(-2, -1), keepdims=True)), 1e-08)
                state = state * jnp.where(n > max_norm, max_norm / n, 1.0)
                wkv = jnp.einsum('bhij,bhj->bhi', state, r_t)
                return (state, wkv)
            state0 = jnp.zeros((Bx, Hh, Dd, Dd), jnp.float32)
            state, wkv = jax.lax.scan(step, state0, (rs, ks_, vs))
            wkv = jnp.transpose(wkv, (1, 0, 2, 3))
            mean = jnp.mean(wkv, axis=(1, 3), keepdims=True)
            var = jnp.mean(jnp.square(wkv - mean), axis=(1, 3), keepdims=True)
            wkv_n = ((wkv - mean) / jnp.sqrt(var + 1e-05)).reshape(Bx, Tx, Cx)
            wkv_n = wkv_n * gn_weight + gn_bias
            out = (wkv_n @ W_o.T + b_o) * g
            last_x = x[:, -1:, :]
            return (out, state, last_x)
        return _reference_tuple_inner(x, W_r, b_r, W_k, b_k, W_v, b_v, W_g, b_g, W_o, b_o, decay, eta, time_mix_r, time_mix_k, time_mix_v, time_mix_g, gn_weight, gn_bias)[0]

    def _L0_xattn_ref(query, key, value, Wq, bq, Wk, bk, Wv, bv, Wo, bo):
        import jax, jax.numpy as jnp
        import numpy as np
        N_HEADS = 16
        HIDDEN = 128
        HEAD = HIDDEN // N_HEADS
        B, Sq, H = query.shape
        Sk = key.shape[1]
        q = (query @ Wq + bq).reshape(B, Sq, N_HEADS, HEAD).transpose(0, 2, 1, 3)
        k = (key @ Wk + bk).reshape(B, Sk, N_HEADS, HEAD).transpose(0, 2, 1, 3)
        v = (value @ Wv + bv).reshape(B, Sk, N_HEADS, HEAD).transpose(0, 2, 1, 3)
        scores = jnp.einsum('bhqd,bhkd->bhqk', q, k) / np.sqrt(HEAD).astype(np.float32)
        attn = jax.nn.softmax(scores, axis=-1)
        out = jnp.einsum('bhqk,bhkd->bhqd', attn, v)
        out = out.transpose(0, 2, 1, 3).reshape(B, Sq, H)
        return out @ Wo + bo

    def _L0_ffn_ref(x, gate_w, gate_b, w1, b1, w2, b2, w3, b3):
        import jax, jax.numpy as jnp
        import numpy as np
        B, S, D, O, E, K = (2, 256, 128, 128, 8, 2)
        probs = jax.nn.softmax(x @ gate_w.T + gate_b, axis=-1)
        _, topi = jax.lax.top_k(probs, K)
        onehot = jax.nn.one_hot(topi, E, dtype=probs.dtype)
        cw = jnp.einsum('bske,bsk->bse', onehot, probs[..., :K])
        out = jnp.zeros(x.shape[:2] + (O,), x.dtype)
        for e in range(E):
            h = jax.nn.relu(x @ w1[e] + b1[e])
            h = jax.nn.relu(h @ w2[e] + b2[e])
            h = h @ w3[e] + b3[e]
            out = out + cw[..., e:e + 1] * h
        return out
    x = _layernorm(x + _L0_attn_ref(x, L0_attn_W_r, L0_attn_b_r, L0_attn_W_k, L0_attn_b_k, L0_attn_W_v, L0_attn_b_v, L0_attn_W_g, L0_attn_b_g, L0_attn_W_o, L0_attn_b_o, L0_attn_decay, L0_attn_eta, L0_attn_time_mix_r, L0_attn_time_mix_k, L0_attn_time_mix_v, L0_attn_time_mix_g, L0_attn_gn_weight, L0_attn_gn_bias), axis=-1)
    x = _layernorm(x + _L0_xattn_ref(x, ctx_1024, ctx_1024, L0_xattn_Wq, L0_xattn_bq, L0_xattn_Wk, L0_xattn_bk, L0_xattn_Wv, L0_xattn_bv, L0_xattn_Wo, L0_xattn_bo), axis=-1)
    x = _layernorm(x + _L0_ffn_ref(x, L0_ffn_gate_w, L0_ffn_gate_b, L0_ffn_w1, L0_ffn_b1, L0_ffn_w2, L0_ffn_b2, L0_ffn_w3, L0_ffn_b3), axis=-1)
    return x

_drawn_inputs = setup_inputs


def setup_inputs(seed=0):
    import zlib

    import numpy as np

    out = dict(_drawn_inputs(seed))
    spreads = {'L0_attn_b_r': (0.0, 0.319),
     'L0_attn_b_k': (0.0, 0.1),
     'L0_attn_b_v': (0.0, 0.1),
     'L0_attn_b_g': (0.0, 0.1),
     'L0_attn_b_o': (0.0, 0.1),
     'L0_attn_time_mix_r': (0.5, 0.2),
     'L0_attn_time_mix_k': (0.5, 0.2),
     'L0_attn_time_mix_v': (0.5, 0.2),
     'L0_attn_time_mix_g': (0.5, 0.2),
     'L0_attn_gn_weight': (1.0, 0.2),
     'L0_attn_gn_bias': (0.0, 0.1),
     'L0_xattn_bq': (0.0, 0.1),
     'L0_xattn_bk': (0.0, 0.8),
     'L0_xattn_bv': (0.0, 0.1),
     'L0_xattn_bo': (0.0, 0.1),
     'L0_ffn_gate_b': (0.0, 0.1),
     'L0_ffn_b1': (0.0, 0.664),
     'L0_ffn_b2': (0.0, 0.455),
     'L0_ffn_b3': (0.0, 0.313)}
    factors = {}
    for name, (base, spread) in spreads.items():
        noise = np.random.default_rng([zlib.crc32(name.encode()), seed]).standard_normal(out[name].shape)
        drawn = base * np.exp(spread * noise) if base else spread * noise
        out[name] = jnp.asarray(drawn.astype(out[name].dtype))
    for name, factor in factors.items():
        out[name] = (out[name] * factor).astype(out[name].dtype)
    return out
```

```python
from contextlib import ExitStack

import concourse.bass as bass
from concourse import mybir

F32 = mybir.dt.float32
BF16 = mybir.dt.bfloat16
U32 = mybir.dt.uint32
ALU = mybir.AluOpType
ACT = mybir.ActivationFunctionType
AX = mybir.AxisListType
RMAX = bass.bass_isa.ReduceOp.max

B, T, C = 32, 100, 128
H, D = 16, 8
S = 1444
E, TOPK = 8, 2
G = 4
NG = B // G
GT = G * T
Q4 = 4
NQ = H // Q4
KT = (S + 127) // 128
LAST = S - (KT - 1) * 128
PAIRS = H // 2
SLOTS = 6
K_PART = (0, 0, 0, 1, 1, 2)
Q_PART = (0, 1, 2, 0, 1, 0)
ROWS = SLOTS * 16
UNITS = 2
UC = 4 * 2 * T
KPC = (482, 482, 480)
MAXN = (D ** 0.5) * 2.0


def rows_of(t):
    return LAST if t == KT - 1 else 128


def build(nc, xT, xn, ctxT, Wrkvg, brkvg, mix, WoT, vec_c, bias_t, dec_in, eta_in,
          Wq, Wk, Wv, Wxo, gate_wT, gate_b, w1, w2, w3, b12, b3, ident_in, iota_in, out):
    with ExitStack() as ctx:
        def sb(name, shape, dt=F32):
            return ctx.enter_context(nc.sbuf_tensor(name, shape, dt))

        def sem(name):
            return ctx.enter_context(nc.semaphore(name))

        rkv_d = nc.dram_tensor("rkv_d", (B, T, 3 * C), F32).ap()
        wkv_d = nc.dram_tensor("wkv_d", (B, T, C), F32).ap()
        qparts_d = nc.dram_tensor("qparts_d", (3, C, B * T), BF16).ap()
        kparts_d = nc.dram_tensor("kparts_d", (2, 3, C, S), BF16).ap()

        ident = sb("ident", [128, 128])
        iota = sb("iota", [128, E])
        wrkvg = sb("wrkvg", [C, 4, C])
        w_now = sb("w_now", [C, 4, C])
        w_prev = sb("w_prev", [C, 4, C])
        b_rkvg = sb("b_rkvg", [T, 4 * C])
        mix_s = sb("mix_s", [C, 4])
        mixc_s = sb("mixc_s", [C, 4])
        wo_s = sb("wo_s", [C, C])
        vecc = sb("vecc", [C, 4])
        bias_s = sb("bias_s", [T, 4, C])
        dec = sb("dec", [128, Q4])
        eta = sb("eta", [128, Q4])
        wq_s = sb("wq_s", [C, C])
        wk_s = sb("wk_s", [C, C])
        wv_s = sb("wv_s", [C, C])
        wxo_s = sb("wxo_s", [C, C])
        gw_s = sb("gw_s", [C, E])
        gb_s = sb("gb_s", [T, E])
        eps_s = sb("eps_s", [128, 1])
        x1 = sb("x1", [T, B, C])
        gate = sb("gate", [T, B, C])
        arena = sb("arena", [128, 38000])

        def view(off, n, shape=None, dt=F32, rows=128, **dims):
            v = arena[0:rows, off:off + n]
            if dt != F32:
                v = v.bitcast(dt)
            return v

        at = [0]

        def carve(n):
            o = at[0]
            at[0] += n
            assert at[0] <= 38000, at[0]
            return o

        xg = [view(carve(G * (T + 1)), G * (T + 1)).rearrange("p (b t) -> p b t", b=G) for _ in range(2)]
        nat = [view(carve(G * 512), G * 512, rows=T).rearrange("p (b n) -> p b n", b=G) for _ in range(2)]
        gsig = view(carve(G * C), G * C, rows=T).rearrange("p (b n) -> p b n", b=G)
        rkv = view(carve(T * 96), T * 96).rearrange("p (t n) -> p t n", n=96)
        ke = view(carve(T * 32), T * 32).rearrange("p (t n) -> p t n", n=32)
        wkv = view(carve(T * 32), T * 32).rearrange("p (t n) -> p t n", n=32)
        sq = view(carve(T * 64), T * 64).rearrange("p (t n) -> p t n", n=64)
        nrm = view(carve(T * 8), T * 8).rearrange("p (t n) -> p t n", n=8)
        state = view(carve(256), 256)
        prod = view(carve(256), 256)
        upd = view(carve(256), 256)
        dst8 = view(carve(256), 256)
        small = view(carve(128), 128)
        s1_end = at[0]
        at[0] = 0
        natw = [view(carve(GT * 0 + G * C), G * C, rows=T).rearrange("p (b n) -> p b n", b=G) for _ in range(2)]
        xin = [view(carve(G * C), G * C, rows=T).rearrange("p (b n) -> p b n", b=G) for _ in range(2)]
        attT = view(carve(GT), GT)
        osum = view(carve(G * C), G * C, rows=T).rearrange("p (b n) -> p b n", b=G)
        x1T = view(carve(GT), GT)
        qres = view(carve(GT), GT)
        qpart = view(carve(3 * GT // 2), 3 * GT // 2, dt=BF16).rearrange("p (s n) -> p s n", s=3)
        bst = view(carve(64), 64)
        at[0] = 0
        ctx_s = [view(carve(S), S) for _ in range(2)]
        kres = view(carve(S), S)
        kpart = [view(carve(3 * S // 2), 3 * S // 2, dt=BF16).rearrange("p (s n) -> p s n", s=3) for _ in range(1)]
        kst = [view(carve(PAIRS * S // 2), PAIRS * S // 2, dt=BF16, rows=ROWS).rearrange("p (h n) -> p h n", h=PAIRS)
               for _ in range(2)]
        qst = [view(carve(PAIRS * 2 * T // 2), PAIRS * T, dt=BF16, rows=ROWS).rearrange(
            "p (h e t) -> p h e t", h=PAIRS, e=2) for _ in range(2)]
        vst = [view(carve(KT * 256), KT * 256).rearrange("p (k h n) -> p k h n", k=KT, h=PAIRS) for _ in range(2)]
        pexp = [view(carve(UC), UC) for _ in range(2)]
        dif = [view(carve(UC), UC) for _ in range(2)]
        rmax = view(carve(2 * UC), 2 * UC)
        amax = view(carve(2 * UC), 2 * UC)
        acc_s = view(carve(4 * T), 4 * T)
        rden = view(carve(H), H, rows=T)
        attn = view(carve(C), C, rows=T)
        attnT = view(carve(T), T)
        at[0] = 0
        wexp = [view(carve(E * C), E * C).rearrange("p (e n) -> p e n", e=E) for _ in range(3)]
        b12_s = view(carve(2 * E), 2 * E).rearrange("p (l e) -> p l e", l=2)
        b3_s = view(carve(E * C), E * C, rows=T).rearrange("p (e n) -> p e n", e=E)
        x2 = view(carve(G * C), G * C, rows=T).rearrange("p (b n) -> p b n", b=G)
        x2T = view(carve(GT), GT)
        h1 = [view(carve(GT), GT) for _ in range(2)]
        h2 = [view(carve(GT), GT) for _ in range(2)]
        lg = view(carve(G * E), G * E, rows=T).rearrange("p (b e) -> p b e", b=G)
        pr = view(carve(G * E), G * E, rows=T).rearrange("p (b e) -> p b e", b=G)
        top = view(carve(G * 8), G * 8, rows=T).rearrange("p (b e) -> p b e", b=G)
        topi = view(carve(G * 8), G * 8, rows=T, dt=U32).rearrange("p (b e) -> p b e", b=G)
        topf = view(carve(G * 8), G * 8, rows=T).rearrange("p (b e) -> p b e", b=G)
        oh = view(carve(G * E), G * E, rows=T).rearrange("p (b e) -> p b e", b=G)
        cw = view(carve(G * E), G * E, rows=T).rearrange("p (b e) -> p b e", b=G)
        h3 = view(carve(G * C), G * C, rows=T).rearrange("p (b n) -> p b n", b=G)
        fin = [view(carve(G * C), G * C, rows=T).rearrange("p (b n) -> p b n", b=G) for _ in range(2)]
        sm3 = view(carve(64), 64)

        ps = ctx.enter_context(nc.psum_tensor("ps", [128, 8, 512], F32))

        consts_in = sem("consts_in")
        experts_in = sem("experts_in")
        mixed_w = sem("mixed_w")
        xg_zero = sem("xg_zero")
        xg_in = [sem(f"xg_in{i}") for i in range(2)]
        proj_done = sem("proj_done")
        bias_done = sem("bias_done")
        sig_done = sem("sig_done")
        gated = sem("gated")
        rkv_out = sem("rkv_out")
        rkv_in = sem("rkv_in")
        sq_done = sem("sq_done")
        sqrt_done = sem("sqrt_done")
        chain = sem("chain")
        step_ss = sem("step_ss")
        step_n = sem("step_n")
        wkv_ready = sem("wkv_ready")
        wkv_out = sem("wkv_out")
        var_ready = sem("var_ready")
        std_ready = sem("std_ready")
        natw_in = [sem(f"natw_in{i}") for i in range(2)]
        natw_used = sem("natw_used")
        xin_used = sem("xin_used")
        pe_c = sem("pe_c")
        dve_c = sem("dve_c")
        qpart_ready = sem("qpart_ready")
        q_out = sem("q_out")
        ctx_in = [sem(f"ctx_in{i}") for i in range(2)]
        kproj_done = sem("kproj_done")
        kpart_ready = sem("kpart_ready")
        kpart_out = sem("kpart_out")
        kst_in = [sem(f"kst_in{i}") for i in range(2)]
        kproj_read = sem("kproj_read")
        vproj_done = sem("vproj_done")
        v_ready = sem("v_ready")
        attn_done = sem("attn_done")
        score1 = sem("score1")
        score1_read = sem("score1_read")
        rmax_ready = sem("rmax_ready")
        amax_ready = sem("amax_ready")
        score2 = sem("score2")
        dif_ready = sem("dif_ready")
        exp_done = sem("exp_done")
        pv_done = sem("pv_done")
        acc_copied = sem("acc_copied")
        acc_T = sem("acc_T")
        attn_ready = sem("attn_ready")
        attn_T = sem("attn_T")
        attnT_ready = sem("attnT_ready")
        xo_done = sem("xo_done")
        y_ready = sem("y_ready")
        pe3 = sem("pe3")
        dve3 = sem("dve3")
        act3 = sem("act3")
        h2_used = sem("h2_used")
        out_done = sem("out_done")

        D3, A3, P3 = 3 + E, 1 + 2 * E, 2 + 3 * E
        out_ready = sem("out_ready")
        waits_passed = sem("waits_passed")
        ch3 = sem("ch3")
        var3 = sem("var3")
        std3 = sem("std3")

        block = ctx.enter_context(nc.Block())

        NCONST = 19

        def passed(eng):
            eng.sem_inc(waits_passed, 1)

        def chained(eng, sm, base):
            n = [0]

            def link(ins):
                n[0] += 1
                ins.then_inc(sm, 1)
                eng.wait_ge(sm, base + n[0])
            return link, n

        N_PRE, N_STEP = 9, 13
        CH_STEP = N_PRE
        CH_NORM = CH_STEP + T * N_STEP

        @block.sync
        def _(sp):
            for dst, src in ((ident, ident_in), (iota, iota_in), (wrkvg, Wrkvg), (b_rkvg, brkvg), (mix_s, mix),
                             (wo_s, WoT), (vecc, vec_c), (bias_s, bias_t), (dec, dec_in),
                             (eta, eta_in), (wq_s, Wq), (wk_s, Wk), (wv_s, Wv), (wxo_s, Wxo), (gw_s, gate_wT),
                             (gb_s, gate_b)):
                sp.dma_start(dst[:], src).then_inc(consts_in, 16)
            sp.wait_ge(xg_zero, 1)
            with sp.Fori(0, NG // 2) as gg:
                for u in range(2):
                    g = gg * 2 + u
                    sp.wait_ge(proj_done, g + 1)
                    passed(sp)
                    sp.dma_start(xg[u][:, :, 1:T + 1], xT[:, bass.ds(g * G, G), :]).then_inc(xg_in[u], 16)
                    sp.wait_ge(gated, g + 2)
                    passed(sp)
                    sp.dma_start(rkv_d[bass.ds(g * G, G)].rearrange("b t n -> t b n"),
                                 nat[u][:, :, 0:3 * C]).then_inc(rkv_out, 16)
            sp.wait_ge(rkv_out, 16 * NG + 16)
            for w in range(3):
                for q in range(NQ):
                    sp.dma_start(rkv[32 * q:32 * q + 32, :, 32 * w:32 * w + 32],
                                 rkv_d[:, :, w * C + 32 * q:w * C + 32 * q + 32]).then_inc(rkv_in, 16)
            sp.wait_ge(wkv_ready, 1)
            for q in range(NQ):
                sp.dma_start(wkv_d[:, :, 32 * q:32 * q + 32], wkv[32 * q:32 * q + 32, :, :]).then_inc(wkv_out, 16)
            sp.wait_ge(wkv_out, 16 * NQ)
            with sp.Fori(0, NG // 2) as gg:
                for u in range(2):
                    g = gg * 2 + u
                    sp.wait_ge(qpart_ready, g + 1)
                    passed(sp)
                    sp.dma_start(natw[u][:, :, :], wkv_d[bass.ds(g * G, G)].rearrange("b t n -> t b n")
                                 ).then_inc(natw_in[u], 16)
                    sp.dma_start(xin[u][:, :, :], xn[bass.ds(g * G, G)].rearrange("b t n -> t b n")
                                 ).then_inc(natw_in[u], 16)
                    sp.wait_ge(qpart_ready, g + 2)
                    passed(sp)
                    sp.dma_start(qparts_d[:, :, bass.ds(g * GT, GT)].rearrange("s c n -> c s n"),
                                 qpart[:, :, :]).then_inc(q_out, 16)
                    sp.wait_ge(q_out, 16 * (g + 1) + 16)
                    passed(sp)

            def prep(b, u, first):
                if not first:
                    sp.wait_ge(v_ready, b - 1)
                    passed(sp)
                sp.dma_start(ctx_s[u][:, :], ctxT[bass.ds(b, 1)].rearrange("o c n -> (o c) n")
                             ).then_inc(ctx_in[u], 16)
                sp.wait_ge(kpart_ready, b + 1)
                passed(sp)
                sp.dma_start(kparts_d[u].rearrange("s c n -> c s n"), kpart[0][:, :, :]).then_inc(kpart_out, 16)
                sp.wait_ge(kpart_out, 16 * (b + 1))
                passed(sp)
                if not first:
                    sp.wait_ge(pv_done, (b - 1) * KT * UNITS)
                    passed(sp)
                for s in range(SLOTS):
                    sp.dma_start(kst[u][16 * s:16 * s + 16, :, :],
                                 kparts_d[u, K_PART[s]].rearrange("(h p) n -> p h n", p=16)).then_inc(kst_in[u], 16)
                    for e in range(2):
                        sp.dma_start(qst[u][16 * s + 8 * e:16 * s + 8 * e + 8, :, e, :],
                                     qparts_d[Q_PART[s], :, bass.ds(b * T, T)].rearrange(
                                         "(h e p) n -> e p h n", e=2, p=8)[e]).then_inc(kst_in[u], 16)

            sp.wait_ge(xg_zero, 2)
            prep(0, 0, True)
            prep(1, 1, True)
            with sp.Fori(1, B // 2) as i:
                prep(2 * i, 0, False)
                prep(2 * i + 1, 1, False)
            sp.wait_ge(y_ready, B)
            for dst, src in zip(wexp, (w1, w2, w3)):
                sp.dma_start(dst[:, :, :], src.rearrange("e d o -> d e o")).then_inc(experts_in, 16)
            sp.dma_start(b12_s[:, :, :], b12).then_inc(experts_in, 16)
            sp.dma_start(b3_s[:, :, :], b3).then_inc(experts_in, 16)
            with sp.Fori(0, NG // 2) as gg:
                for u in range(2):
                    g = gg * 2 + u
                    sp.wait_ge(out_ready, g + 1)
                    passed(sp)
                    sp.dma_start(out[bass.ds(g * G, G)].rearrange("b t n -> t b n"), fin[u][:, :, :]
                                 ).then_inc(out_done, 16)
            sp.wait_ge(out_done, 16 * NG + 16)

        @block.tensor
        def _(pe):
            pe.wait_ge(mixed_w, 2)
            with pe.Fori(0, NG // 2) as gg:
                for u in range(2):
                    g = gg * 2 + u
                    pe.wait_ge(xg_in[u], 16 * (gg + 1))
                    pe.wait_ge(bias_done, g + 1)
                    for b in range(G):
                        o = ps[0:T, 4 * u + b, :]
                        nc.tensor.matmul(o, xg[u][:, b, 1:T + 1], w_now[:, :, :], start=True, stop=False)
                        last = nc.tensor.matmul(o, xg[u][:, b, 0:T], w_prev[:, :, :], start=False, stop=True)
                    last.then_inc(proj_done, 1)
            with pe.Fori(0, NG // 2) as gg:
                for u in range(2):
                    g = gg * 2 + u
                    pe.wait_ge(natw_in[u], 32 * (gg + 1))
                    pe.wait_ge(dve_c, g * 4 + 1)
                    for b in range(G):
                        last = nc.tensor.transpose(ps[:, 0, b * T:(b + 1) * T], natw[u][:, b, :], ident[0:T, 0:T])
                    last.then_inc(pe_c, 1)
                    pe.wait_ge(dve_c, g * 4 + 2)
                    for b in range(G):
                        last = nc.tensor.matmul(ps[0:T, 1, b * C:(b + 1) * C], attT[:, b * T:(b + 1) * T], wo_s[:],
                                                start=True, stop=True)
                    last.then_inc(pe_c, 1)
                    pe.wait_ge(dve_c, g * 4 + 3)
                    for b in range(G):
                        last = nc.tensor.transpose(ps[:, 2, b * T:(b + 1) * T], osum[:, b, :], ident[0:T, 0:T])
                    last.then_inc(pe_c, 1)
                    pe.wait_ge(dve_c, g * 4 + 4)
                    nc.tensor.matmul(ps[:, 3, 0:GT], wq_s[:], x1T[:, :], start=True, stop=True).then_inc(pe_c, 1)

            def prep(b, u):
                pe.wait_ge(ctx_in[u], 16 * ((b - u) // 2 + 1) if isinstance(b, int) else ctx_val(b, u))
                o = 0
                for i, n in enumerate(KPC):
                    last = nc.tensor.matmul(ps[:, 5 + i, 0:n], wk_s[:], ctx_s[u][:, o:o + n], start=True, stop=True)
                    o += n
                last.then_inc(kproj_done, 1)
                pe.wait_ge(kproj_read, b + 1)
                for t in range(KT):
                    m = rows_of(t)
                    last = nc.tensor.matmul(ps[0:m, 5 + t // 4, t % 4 * C:(t % 4 + 1) * C],
                                            ctx_s[u][:, t * 128:t * 128 + m], wv_s[:], start=True, stop=True)
                last.then_inc(vproj_done, 1)
                pe.wait_ge(v_ready, b + 1)

            def scores(u, t, un):
                m = rows_of(t)
                slot = un % 2
                for j in range(4):
                    p = (un % UNITS) * 4 + j
                    last = nc.tensor.matmul(ps[0:m, 2 * slot + j // 2, j % 2 * 200:j % 2 * 200 + 200],
                                            kst[u][:, p, t * 128:t * 128 + m], qst[u][:, p, :, :],
                                            start=True, stop=True)
                return last

            def attention(b, u, half):
                pe.wait_ge(kst_in[u], half)
                n0 = b * (KT * UNITS)
                for n in range(KT * UNITS):
                    if n >= 2:
                        pe.wait_ge(score1_read, n0 + n - 1)
                    scores(u, n // 2, n).then_inc(score1, 1)
                pe.wait_ge(score1_read, n0 + KT * UNITS)

                def pv(n):
                    t, un = n // 2, n % 2
                    m = rows_of(t)
                    pe.wait_ge(exp_done, n0 + n + 1)
                    if m < 128:
                        passed(pe)
                    for j in range(4):
                        last = nc.tensor.matmul(ps[32 * j:32 * j + 32, 4, un * 200:un * 200 + 200],
                                                vst[u][0:m, t, un * 4 + j, :],
                                                pexp[un][0:m, j * 200:j * 200 + 200],
                                                start=(t == 0 and un == 0), stop=(t == KT - 1), skip_group_check=True)
                    last.then_inc(pv_done, 1)

                for n in range(KT * UNITS):
                    if n >= 2:
                        pe.wait_ge(dif_ready, n0 + n - 1)
                    scores(u, n // 2, n).then_inc(score2, 1)
                    if n >= 1:
                        pv(n - 1)
                pv(KT * UNITS - 1)
                pe.wait_ge(acc_copied, b + 1)
                for s in range(2):
                    for e in range(2):
                        i = s * 2 + e
                        last = nc.tensor.transpose(ps[0:T, 5, i * 128:(i + 1) * 128],
                                                   acc_s[:, s * 200 + e * 100:s * 200 + e * 100 + 100], ident[:])
                last.then_inc(acc_T, 1)
                pe.wait_ge(attn_ready, b + 1)
                nc.tensor.transpose(ps[:, 6, 0:T], attn[:, :], ident[0:T, 0:T]).then_inc(attn_T, 1)
                pe.wait_ge(attnT_ready, b + 1)
                nc.tensor.matmul(ps[0:T, 7, 0:C], attnT[:, :], wxo_s[:], start=True, stop=True).then_inc(xo_done, 1)
                pe.wait_ge(y_ready, b + 1)

            def ctx_val(b, u):
                return 8 * (b - u) + 16

            per = 16 * SLOTS * 3
            prep(0, 0)
            with pe.Fori(0, B // 2 - 1) as i:
                prep(2 * i + 1, 1)
                attention(2 * i, 0, (i + 1) * per)
                prep(2 * i + 2, 0)
                attention(2 * i + 1, 1, (i + 1) * per)
            prep(B - 1, 1)
            attention(B - 2, 0, B // 2 * per)
            attention(B - 1, 1, B // 2 * per)

            pe.wait_ge(experts_in, 16 * 5)
            with pe.Fori(0, NG) as g:
                pe.wait_ge(dve3, g * D3 + 1)
                for b in range(G):
                    last = nc.tensor.transpose(ps[:, 0, b * T:(b + 1) * T], x2[:, b, :], ident[0:T, 0:T])
                last.then_inc(pe3, 1)
                pe.wait_ge(dve3, g * D3 + 2)
                for b in range(G):
                    last = nc.tensor.matmul(ps[0:T, 1, b * E:(b + 1) * E], x2T[:, b * T:(b + 1) * T], gw_s[:],
                                            start=True, stop=True)
                last.then_inc(pe3, 1)
                for e in range(E):
                    k = e % 2
                    nc.tensor.matmul(ps[:, 2 + k, 0:GT], wexp[0][:, e, :], x2T[:, :], start=True,
                                     stop=True).then_inc(pe3, 1)
                    pe.wait_ge(act3, g * A3 + 2 + 2 * e)
                    nc.tensor.matmul(ps[:, 4 + k, 0:GT], wexp[1][:, e, :], h1[k][:, :], start=True,
                                     stop=True).then_inc(pe3, 1)
                    pe.wait_ge(act3, g * A3 + 3 + 2 * e)
                    if e >= 2:
                        pe.wait_ge(dve3, g * D3 + 3 + e - 1)
                    for b in range(G):
                        last = nc.tensor.matmul(ps[0:T, 6 + k, b * C:(b + 1) * C], h2[k][:, b * T:(b + 1) * T],
                                                wexp[2][:, e, :], start=True, stop=True)
                    last.then_inc(pe3, 1)

        @block.scalar
        def _(act):
            act.wait_ge(consts_in, 16 * 16)
            nc.scalar.activation(dec[:], dec[:], ACT.Sigmoid).then_inc(sig_done, 1)
            nc.scalar.activation(eta[:], eta[:], ACT.Sigmoid).then_inc(sig_done, 1)
            with act.Fori(0, NG // 2) as gg:
                for u in range(2):
                    g = gg * 2 + u
                    act.wait_ge(bias_done, g + 2)
                    act.wait_ge(gated, g + 1)
                    nc.scalar.activation(nat[u][:, :, 0:C], nat[u][:, :, 0:C], ACT.Sigmoid).then_inc(sig_done, 1)
                    nc.scalar.activation(gsig[:, :, :], nat[u][:, :, 3 * C:4 * C], ACT.Sigmoid).then_inc(sig_done, 1)
            act.wait_ge(sq_done, 1)
            nc.scalar.activation(nrm[:, :, :], nrm[:, :, :], ACT.Sqrt).then_inc(sqrt_done, 1)
            with act.Fori(0, T) as t:
                act.wait_ge(step_ss, t + 1)
                nc.scalar.activation(small[:, 8:12], small[:, 4:8], ACT.Sqrt, scale=1.0 / MAXN ** 2
                                     ).then_inc(step_n, 1)
            act.wait_ge(var_ready, 1)
            nc.scalar.activation(small[:, 80:84], small[:, 64:72].rearrange("p (h n) -> p h n", n=2)[:, :, 1],
                                 ACT.Sqrt, bias=eps_s[:]).then_inc(std_ready, 1)
            with act.Fori(0, NG) as g:
                act.wait_ge(var_ready, g + 2)
                nc.scalar.activation(bst[0:T, 40:44], bst[0:T, 32:40].rearrange("p (h n) -> p h n", n=2)[:, :, 1],
                                     ACT.Sqrt, bias=eps_s[0:T]).then_inc(std_ready, 1)
            with act.Fori(0, B) as b:
                for n in range(KT * UNITS):
                    m = rows_of(n // 2)
                    act.wait_ge(dif_ready, b * (KT * UNITS) + n + 1)
                    if n >= 2:
                        act.wait_ge(pv_done, b * (KT * UNITS) + n - 1)
                    nc.scalar.activation(pexp[n % 2][0:m, :], dif[n % 2][0:m, :], ACT.Exp,
                                         scale=float(D) ** -0.5).then_inc(exp_done, 1)
            with act.Fori(0, NG) as g:
                act.wait_ge(var3, 2 * g + 1)
                nc.scalar.activation(sm3[0:T, 40:44], sm3[0:T, 32:40].rearrange("p (h n) -> p h n", n=2)[:, :, 1],
                                     ACT.Sqrt, bias=eps_s[0:T]).then_inc(std3, 1)
                act.wait_ge(dve3, g * D3 + 3)
                nc.scalar.activation(pr[:, :, :], lg[:, :, :], ACT.Exp).then_inc(act3, 1)
                for e in range(E):
                    k = e % 2
                    act.wait_ge(pe3, g * P3 + 3 + 3 * e)
                    nc.scalar.activation(h1[k][:, :], ps[:, 2 + k, 0:GT], ACT.Relu, bias=b12_s[:, 0, e:e + 1]
                                         ).then_inc(act3, 1)
                    act.wait_ge(pe3, g * P3 + 4 + 3 * e)
                    nc.scalar.activation(h2[k][:, :], ps[:, 4 + k, 0:GT], ACT.Relu, bias=b12_s[:, 1, e:e + 1]
                                         ).then_inc(act3, 1)
                act.wait_ge(var3, 2 * g + 2)
                nc.scalar.activation(sm3[0:T, 44:48], sm3[0:T, 32:40].rearrange("p (h n) -> p h n", n=2)[:, :, 1],
                                     ACT.Sqrt, bias=eps_s[0:T]).then_inc(std3, 1)

        @block.gpsimd
        def _(pool):
            with pool.Fori(0, B) as b:
                pool.wait_ge(rmax_ready, b + 1)
                passed(pool)
                nc.gpsimd.partition_all_reduce(amax[:, :], rmax[:, :], 128, RMAX).then_inc(amax_ready, 1)

        @block.vector
        def _(dve):
            V = nc.vector
            for freed in (proj_done, qpart_ready, bias_done, dve_c, gated):
                dve.sem_inc(freed, 1)
            for stored in (rkv_out, q_out, out_done):
                dve.sem_inc(stored, 16)
            link, n = chained(dve, chain, 0)
            for u in range(2):
                link(V.memset(xg[u][:, :, 0:1], 0.0))
            link(V.memset(eps_s[:], 1e-5))
            V.memset(state[:, :], 0.0).then_inc(xg_zero, 1)
            dve.wait_ge(consts_in, 16 * 16)
            link(V.tensor_scalar(mixc_s[:], mix_s[:], -1.0, 1.0, ALU.mult, ALU.add))
            V.tensor_tensor(w_now[:, :, :], wrkvg[:, :, :], mix_s[:].unsqueeze(2).broadcast_to([C, 4, C]),
                            ALU.mult).then_inc(mixed_w, 1)
            V.tensor_tensor(w_prev[:, :, :], wrkvg[:, :, :], mixc_s[:].unsqueeze(2).broadcast_to([C, 4, C]),
                            ALU.mult).then_inc(mixed_w, 1)
            with dve.Fori(0, NG // 2) as gg:
                for u in range(2):
                    g = gg * 2 + u
                    dve.wait_ge(proj_done, g + 2)
                    dve.wait_ge(rkv_out, 16 * g + 16)
                    V.tensor_tensor(nat[u][:, :, :], ps[0:T, 4 * u:4 * u + 4, :],
                                    b_rkvg[:].unsqueeze(1).broadcast_to([T, G, 512]), ALU.add).then_inc(bias_done, 1)
                    dve.wait_ge(sig_done, 2 * g + 4)
                    V.tensor_tensor(gate[:, bass.ds(g * G, G), :], nat[u][:, :, 3 * C:4 * C], gsig[:, :, :],
                                    ALU.mult).then_inc(gated, 1)
            dve.wait_ge(rkv_in, 16 * 12)
            kv = rkv[:, :, 32:96]
            kv8 = kv.rearrange("p t (h d) -> p t h d", d=D)
            link(V.tensor_tensor(sq[:, :, :], kv, kv, ALU.mult))
            V.tensor_reduce(nrm[:, :, :], sq[:, :, :].rearrange("p t (h d) -> p t h d", d=D), AX.X,
                            ALU.add).then_inc(sq_done, 1)
            dve.wait_ge(sqrt_done, 1)
            link(V.tensor_scalar_max(nrm[:, :, :], nrm[:, :, :], 1e-12))
            link(V.reciprocal(nrm[:, :, :], nrm[:, :, :]))
            link(V.tensor_tensor(kv8, kv8, nrm[:, :, :].unsqueeze(3).broadcast_to([128, T, 8, D]), ALU.mult))
            link(V.tensor_tensor(ke[:, :, :].rearrange("p t (h d) -> p t h d", d=D), kv8[:, :, 0:4, :],
                                 eta[:].unsqueeze(1).unsqueeze(3).broadcast_to([128, T, 4, D]), ALU.mult))
            assert n[0] == N_PRE, n

            st4 = state.rearrange("p (h i j) -> p h i j", h=4, i=D)
            pr4 = prod.rearrange("p (h i j) -> p h i j", h=4, i=D)
            up4 = upd.rearrange("p (h i j) -> p h i j", h=4, i=D)
            pred = small[:, 16:48].rearrange("p (h i) -> p h i", h=4)

            def vec_of(tile, t, o):
                return tile[:, bass.ds(t, 1), o:o + 32].rearrange("p o (h d) -> p (o h) d", d=D)

            def over_i(v):
                return v.unsqueeze(2).broadcast_to([128, 4, D, D])

            def over_j(v):
                return v.unsqueeze(3).broadcast_to([128, 4, D, D])

            def head(v):
                return v.unsqueeze(2).broadcast_to([128, 4, D * D])

            sth = state.rearrange("p (h n) -> p h n", h=4)
            with dve.Fori(0, T) as t:
                link, n = chained(dve, chain, t * N_STEP + CH_STEP)
                link(V.tensor_tensor(pr4, st4, over_i(vec_of(rkv, t, 32)), ALU.mult))
                link(V.tensor_reduce(pred, pr4, AX.X, ALU.add))
                link(V.tensor_tensor(pred, pred, vec_of(rkv, t, 64), ALU.subtract))
                link(V.tensor_tensor(sth, sth, head(dec[:]), ALU.mult))
                link(V.tensor_tensor(up4, over_j(pred), over_i(vec_of(ke, t, 0)), ALU.mult))
                link(V.tensor_tensor(state[:, :], state[:, :], upd[:, :], ALU.subtract))
                link(V.tensor_tensor(prod[:, :], state[:, :], state[:, :], ALU.mult))
                link(V.tensor_reduce(small[:, 4:8], prod.rearrange("p (h n) -> p h n", h=4), AX.X, ALU.add))
                dve.sem_inc(step_ss, 1)
                dve.wait_ge(step_n, t + 1)
                link(V.tensor_scalar_max(small[:, 12:16], small[:, 8:12], 1.0))
                link(V.reciprocal(small[:, 0:4], small[:, 12:16]))
                link(V.tensor_tensor(sth, sth, head(small[:, 0:4]), ALU.mult))
                link(V.tensor_tensor(pr4, st4, over_i(vec_of(rkv, t, 0)), ALU.mult))
                link(V.tensor_reduce(vec_of(wkv, t, 0), pr4, AX.X, ALU.add))
                assert n[0] == N_STEP, n
            link, n = chained(dve, chain, CH_NORM)
            bns = upd[:, 0:48].rearrange("p (h c n) -> p h c n", h=4, c=2)
            for h in range(4):
                for c in range(2):
                    last = V.bn_stats(bns[:, h, c, :], wkv[:, 50 * c:50 * c + 50, 8 * h:8 * h + 8])
            link(last)
            for h in range(4):
                last = V.bn_aggr(small[:, 64 + 2 * h:66 + 2 * h], bns[:, h, :, :].rearrange("p c n -> p (c n)"))
                if h < 3:
                    link(last)
            last.then_inc(var_ready, 1)
            dve.wait_ge(std_ready, 1)
            link(V.reciprocal(small[:, 84:88], small[:, 80:84]))
            for h in range(4):
                w = wkv[:, :, 8 * h:8 * h + 8]
                last = V.tensor_scalar(w, w, small[:, 64 + 2 * h:65 + 2 * h], small[:, 84 + h:85 + h],
                                       ALU.subtract, ALU.mult)
            last.then_inc(wkv_ready, 1)
            n_norm = n[0]

            n_c = 11
            with dve.Fori(0, NG // 2) as gg:
                for u in range(2):
                    g = gg * 2 + u
                    link, n = chained(dve, chain, g * n_c + CH_NORM + n_norm)
                    dve.wait_ge(pe_c, g * 4 + 1)
                    V.tensor_scalar(attT[:, :], ps[:, 0, 0:GT], vecc[:, 0:1], vecc[:, 1:2], ALU.mult,
                                    ALU.add).then_inc(dve_c, 1)
                    dve.wait_ge(pe_c, g * 4 + 2)
                    link(V.tensor_tensor(osum[:, :, :], ps[0:T, 1, :].rearrange("p (b n) -> p b n", b=G),
                                         bias_s[:, 0, :].unsqueeze(1).broadcast_to([T, G, C]), ALU.add))
                    link(V.tensor_tensor(osum[:, :, :], osum[:, :, :], gate[:, bass.ds(g * G, G), :], ALU.mult))
                    link(V.tensor_tensor(osum[:, :, :], osum[:, :, :], xin[u][:, :, :], ALU.add))
                    for b in range(G):
                        last = V.bn_stats(bst[0:T, 6 * b:6 * b + 6], osum[:, b, :])
                    link(last)
                    passed(dve)
                    for b in range(G):
                        last = V.bn_aggr(bst[0:T, 32 + 2 * b:34 + 2 * b], bst[0:T, 6 * b:6 * b + 6])
                    last.then_inc(var_ready, 1)
                    dve.wait_ge(std_ready, g + 2)
                    link(V.reciprocal(bst[0:T, 44:48], bst[0:T, 40:44]))
                    for b in range(G):
                        last = V.tensor_scalar(osum[:, b, :], osum[:, b, :], bst[0:T, 32 + 2 * b:33 + 2 * b],
                                               bst[0:T, 44 + b:45 + b], ALU.subtract, ALU.mult)
                    last.then_inc(dve_c, 1)
                    dve.wait_ge(dve_c, g * 4 + 3)
                    link(V.tensor_tensor(x1[:, bass.ds(g * G, G), :], osum[:, :, :],
                                         bias_s[:, 2, :].unsqueeze(1).broadcast_to([T, G, C]), ALU.add))
                    dve.wait_ge(pe_c, g * 4 + 3)
                    V.tensor_copy(x1T[:, :], ps[:, 2, 0:GT]).then_inc(dve_c, 1)
                    dve.wait_ge(pe_c, g * 4 + 4)
                    dve.wait_ge(q_out, 16 * g + 16)
                    link(V.tensor_scalar(qpart[:, 0, :], ps[:, 3, 0:GT], vecc[:, 2:3], None, ALU.add))
                    link(V.scalar_tensor_tensor(qres[:, :], ps[:, 3, 0:GT], vecc[:, 2:3], qpart[:, 0, :], ALU.add,
                                                ALU.subtract))
                    link(V.tensor_copy(qpart[:, 1, :], qres[:, :]))
                    link(V.tensor_tensor(qpart[:, 2, :], qres[:, :], qpart[:, 1, :], ALU.subtract))
                    link(V.memset(bst[:, 60:61], 0.0))
                    dve.sem_inc(qpart_ready, 1)
                    dve.sem_inc(dve_c, 1)
                    assert n[0] == n_c, n
            base2 = CH_NORM + n_norm + NG * n_c

            link, n = chained(dve, chain, base2)
            for u in range(2):
                link(V.memset(qst[u][:, :, :, :], 0.0))
                link(V.memset(vst[u][:, :, :, :], 0.0))
                for e in range(2):
                    link(V.memset(vst[u][:, :, :, 9 * e + 8:9 * e + 9], 1.0))
            base2 += n[0]
            dve.sem_inc(xg_zero, 1)
            n_kp, n_at = 3, 5
            n_b = n_kp + n_at

            def prep(b, u, base):
                link, n = chained(dve, chain, base)
                dve.wait_ge(kproj_done, b + 1)
                if not isinstance(b, int) or b > 0:
                    dve.wait_ge(kpart_out, 16 * b)
                o = 0
                for i, w in enumerate(KPC):
                    last = V.tensor_scalar(kpart[0][:, 0, o:o + w], ps[:, 5 + i, 0:w], vecc[:, 3:4], None, ALU.add)
                    o += w
                link(last)
                o = 0
                for i, w in enumerate(KPC):
                    last = V.scalar_tensor_tensor(kres[:, o:o + w], ps[:, 5 + i, 0:w], vecc[:, 3:4],
                                                  kpart[0][:, 0, o:o + w], ALU.add, ALU.subtract)
                    o += w
                last.then_inc(kproj_read, 1)
                dve.wait_ge(kproj_read, b + 1)
                link(V.tensor_copy(kpart[0][:, 1, :], kres[:, :]))
                link(V.tensor_tensor(kpart[0][:, 2, :], kres[:, :], kpart[0][:, 1, :], ALU.subtract))
                dve.sem_inc(kpart_ready, 1)
                dve.wait_ge(vproj_done, b + 1)
                for t in range(KT):
                    m = rows_of(t)
                    last = V.tensor_copy(
                        vst[u][0:m, t, :, 0:18].rearrange("p h (e n) -> p h e n", n=9)[:, :, :, 0:8],
                        ps[0:m, 5 + t // 4, t % 4 * C:(t % 4 + 1) * C].rearrange("p (h e n) -> p h e n", e=2, n=8))
                last.then_inc(v_ready, 1)
                assert n[0] == n_kp, n

            def attention(b, u, base):
                link, n = chained(dve, chain, base)
                n0 = b * (KT * UNITS)
                for k in range(KT * UNITS):
                    t, un = k // 2, k % 2
                    m = rows_of(t)
                    dve.wait_ge(score1, n0 + k + 1)
                    src = ps[0:m, 2 * un:2 * un + 2, 0:400]
                    dst = rmax[0:m, un * UC:(un + 1) * UC].rearrange("p (a n) -> p a n", a=2)
                    if t == 0:
                        V.tensor_copy(dst, src).then_inc(score1_read, 1)
                    else:
                        dve.wait_ge(score1_read, n0 + k - 1)
                        V.tensor_tensor(dst, src, dst, ALU.max).then_inc(score1_read, 1)
                dve.wait_ge(score1_read, n0 + KT * UNITS)
                dve.sem_inc(rmax_ready, 1)
                dve.wait_ge(amax_ready, b + 1)
                for k in range(KT * UNITS):
                    t, un = k // 2, k % 2
                    m = rows_of(t)
                    dve.wait_ge(score2, n0 + k + 1)
                    if k >= 2:
                        dve.wait_ge(exp_done, n0 + k - 1)
                    V.tensor_tensor(dif[un][0:m, :].rearrange("p (a n) -> p a n", a=2),
                                    ps[0:m, 2 * un:2 * un + 2, 0:400],
                                    amax[0:m, un * UC:(un + 1) * UC].rearrange("p (a n) -> p a n", a=2),
                                    ALU.subtract).then_inc(dif_ready, 1)
                dve.wait_ge(pv_done, n0 + KT * UNITS)
                V.tensor_copy(acc_s[:, :], ps[:, 4, 0:400]).then_inc(acc_copied, 1)
                dve.wait_ge(acc_T, b + 1)
                for s in range(2):
                    for e in range(2):
                        o = 256 * s + 137 * e
                        last = V.reciprocal(rden[:, :].rearrange("p (s g e) -> p s g e", s=2, e=2)[:, s, :, e],
                                            ps[0:T, 5, o + 8:o + 105:32])
                link(last)
                for s in range(2):
                    for e in range(2):
                        o = 256 * s + 137 * e
                        for gq in range(4):
                            h = (s * 4 + gq) * 2 + e
                            last = V.tensor_scalar(attn[:, 8 * h:8 * h + 8], ps[0:T, 5, o + 32 * gq:o + 32 * gq + 8],
                                                   rden[:, h:h + 1], None, ALU.mult)
                link(last)
                link(V.tensor_tensor(attn[:, :], attn[:, :], bias_s[:, 1, :], ALU.add))
                dve.sem_inc(attn_ready, 1)
                dve.wait_ge(attn_T, b + 1)
                link(V.tensor_copy(attnT[:, :], ps[:, 6, 0:T]))
                dve.sem_inc(attnT_ready, 1)
                dve.wait_ge(xo_done, b + 1)
                xb = x1[:, bass.ds(b, 1), :].rearrange("p o n -> p (o n)")
                link(V.tensor_tensor(xb, ps[0:T, 7, 0:C], xb, ALU.add))
                dve.sem_inc(y_ready, 1)
                assert n[0] == n_at, n

            prep(0, 0, base2)
            base2 += n_kp
            with dve.Fori(0, B // 2 - 1) as i:
                bb = i * (2 * n_b) + base2
                prep(2 * i + 1, 1, bb)
                attention(2 * i, 0, bb + n_kp)
                prep(2 * i + 2, 0, bb + n_b)
                attention(2 * i + 1, 1, bb + n_b + n_kp)
            base2 += (B // 2 - 1) * 2 * n_b
            prep(B - 1, 1, base2)
            attention(B - 2, 0, base2 + n_kp)
            attention(B - 1, 1, base2 + n_b)

            def layernorm(link, src, dst, k, g, col):
                for b in range(G):
                    last = V.bn_stats(sm3[0:T, 6 * b:6 * b + 6], src[:, b, :])
                link(last)
                passed(dve)
                for b in range(G):
                    last = V.bn_aggr(sm3[0:T, 32 + 2 * b:34 + 2 * b], sm3[0:T, 6 * b:6 * b + 6])
                last.then_inc(var3, 1)
                dve.wait_ge(std3, 2 * g + k)
                link(V.reciprocal(sm3[0:T, 48:52], sm3[0:T, col:col + 4]))
                for b in range(G):
                    last = V.tensor_scalar(dst[:, b, :], src[:, b, :], sm3[0:T, 32 + 2 * b:33 + 2 * b],
                                           sm3[0:T, 48 + b:49 + b], ALU.subtract, ALU.mult)
                return last

            n_3 = 26
            dve.wait_ge(experts_in, 16 * 5)
            with dve.Fori(0, NG // 2) as gg:
                for u in range(2):
                    g = gg * 2 + u
                    link, n = chained(dve, ch3, g * n_3)
                    link(V.tensor_copy(h3[:, :, :], x1[:, bass.ds(g * G, G), :]))
                    layernorm(link, h3, x2, 1, g, 40).then_inc(dve3, 1)
                    dve.wait_ge(pe3, g * P3 + 1)
                    V.tensor_copy(x2T[:, :], ps[:, 0, 0:GT]).then_inc(dve3, 1)
                    dve.wait_ge(pe3, g * P3 + 2)
                    link(V.tensor_tensor(lg[:, :, :], ps[0:T, 1, 0:G * E].rearrange("p (b e) -> p b e", b=G),
                                         gb_s[:].unsqueeze(1).broadcast_to([T, G, E]), ALU.add))
                    link(V.tensor_reduce(sm3[0:T, 52:56], lg[:, :, :], AX.X, ALU.max))
                    V.tensor_tensor(lg[:, :, :], lg[:, :, :], sm3[0:T, 52:56].unsqueeze(2).broadcast_to([T, G, E]),
                                    ALU.subtract).then_inc(dve3, 1)
                    dve.wait_ge(act3, g * A3 + 1)
                    link(V.tensor_reduce(sm3[0:T, 52:56], pr[:, :, :], AX.X, ALU.add))
                    link(V.reciprocal(sm3[0:T, 56:60], sm3[0:T, 52:56]))
                    link(V.tensor_tensor(pr[:, :, :], pr[:, :, :],
                                         sm3[0:T, 56:60].unsqueeze(2).broadcast_to([T, G, E]), ALU.mult))
                    passed(dve)
                    for b in range(G):
                        last = V.max(top[:, b, :], pr[:, b, :])
                    link(last)
                    passed(dve)
                    for b in range(G):
                        last = V.max_index(topi[:, b, :], top[:, b, :], pr[:, b, :])
                    link(last)
                    link(V.tensor_copy(topf[:, :, :], topi[:, :, :]))
                    iob = iota[0:T, :].unsqueeze(1).broadcast_to([T, G, E])
                    for k in range(TOPK):
                        dst = cw if k == 0 else oh
                        link(V.tensor_tensor(dst[:, :, :], topf[:, :, k:k + 1].broadcast_to([T, G, E]), iob,
                                             ALU.is_equal))
                        link(V.tensor_tensor(dst[:, :, :], dst[:, :, :], pr[:, :, k:k + 1].broadcast_to([T, G, E]),
                                             ALU.mult))
                    link(V.tensor_tensor(cw[:, :, :], cw[:, :, :], oh[:, :, :], ALU.add))
                    for e in range(E):
                        k = e % 2
                        dve.wait_ge(pe3, g * P3 + 5 + 3 * e)
                        link(V.tensor_tensor(h3[:, :, :], ps[0:T, 6 + k, :].rearrange("p (b n) -> p b n", b=G),
                                             b3_s[:, e, :].unsqueeze(1).broadcast_to([T, G, C]), ALU.add))
                        for b in range(G):
                            last = V.scalar_tensor_tensor(x2[:, b, :], h3[:, b, :], cw[:, b, e:e + 1], x2[:, b, :],
                                                          ALU.mult, ALU.add)
                        last.then_inc(dve3, 1)
                        dve.wait_ge(dve3, g * D3 + 4 + e)
                    dve.wait_ge(out_done, 16 * g + 16)
                    layernorm(link, x2, fin[u], 2, g, 44).then_inc(out_ready, 1)
                    dve.wait_ge(out_ready, g + 1)
                    assert n[0] == n_3, n


def kernel(**inputs):
    import numpy as np
    import concourse.bacc as bacc
    from concourse.bass_utils import run_bass_kernel_spmd

    a = {k: np.asarray(v) for k, v in inputs.items()}
    A, X, F = "L0_attn_", "L0_xattn_", "L0_ffn_"

    def wide(v, n):
        return np.ascontiguousarray(np.broadcast_to(v, (n,) + v.shape))

    tm = np.stack([a[A + "time_mix_" + c].reshape(C) for c in "rkvg"], 1)
    arrays = {
        "xT": np.ascontiguousarray(a["x"].transpose(2, 0, 1)),
        "xn": a["x"],
        "ctxT": np.ascontiguousarray(a["ctx_1024"].transpose(0, 2, 1)),
        "Wrkvg": np.stack([a[A + "W_" + c].T for c in "rkvg"], 1),
        "brkvg": wide(np.concatenate([a[A + "b_" + c] for c in "rkvg"]), T),
        "mix": tm,
        "WoT": np.ascontiguousarray(a[A + "W_o"].T),
        "vec_c": np.stack([a[A + "gn_weight"], a[A + "gn_bias"], a[X + "bq"], a[X + "bk"]], 1),
        "bias_t": wide(np.stack([a[A + "b_o"], a[X + "bv"], a[X + "bo"], a[X + "bo"]]), T),
        "dec_in": np.repeat(a[A + "decay"].reshape(NQ, Q4), B, 0),
        "eta_in": np.repeat(a[A + "eta"].reshape(NQ, Q4), B, 0),
        "Wq": a[X + "Wq"], "Wk": a[X + "Wk"], "Wv": a[X + "Wv"], "Wxo": a[X + "Wo"],
        "gate_wT": np.ascontiguousarray(a[F + "gate_w"].T),
        "gate_b": wide(a[F + "gate_b"], T),
        "w1": a[F + "w1"], "w2": a[F + "w2"], "w3": a[F + "w3"],
        "b12": np.ascontiguousarray(np.stack([a[F + "b1"], a[F + "b2"]]).transpose(2, 0, 1)),
        "b3": wide(a[F + "b3"], T),
        "ident_in": np.eye(128, dtype=np.float32),
        "iota_in": wide(np.arange(E, dtype=np.float32), 128),
    }
    nc = bacc.Bacc("TRN2", target_bir_lowering=False, num_devices=1)
    args = [nc.dram_tensor(n + "_dram", v.shape, mybir.dt.from_np(v.dtype), kind="ExternalInput").ap()
            for n, v in arrays.items()]
    args.append(nc.dram_tensor("out_dram", (B, T, C), F32, kind="ExternalOutput").ap())
    build(nc, *args)
    r = run_bass_kernel_spmd(nc, [{n + "_dram": v for n, v in arrays.items()}], core_ids=[0])
    return r.results[0]["out_dram"]
```

```python
from contextlib import ExitStack

import concourse.bass as bass
from concourse import mybir

F32 = mybir.dt.float32
BF16 = mybir.dt.bfloat16
I32 = mybir.dt.int32
U32 = mybir.dt.uint32
ALU = mybir.AluOpType
ACT = mybir.ActivationFunctionType
AX = mybir.AxisListType
RMAX = bass.bass_isa.ReduceOp.max

B, T, C = 32, 100, 128
H, D = 16, 8
S = 1444
E, TOPK = 8, 2
G = 4
NG = B // G
GT = G * T
Q4 = 4
NQ = H // Q4
KT = (S + 127) // 128
LAST = S - (KT - 1) * 128
PAIRS = H // 2
SLOTS = 6
K_PART = (0, 0, 0, 1, 1, 2)
Q_PART = (0, 1, 2, 0, 1, 0)
ROWS = SLOTS * 16
UNITS = 2
UC = 4 * 2 * T
KC = (482, 482, 480)
NU = KT * UNITS
SS = 3
MAXN = (D ** 0.5) * 2.0
SCORE_BOUND = 64.0
STEPS = 5
CHORES = ((1, "k0"), (4, "k1"), (7, "k2"), (9, "bound"), (11, "v0"), (13, "v1"), (15, "v2"), (17, "sums"),
          (19, "attn"), (21, "out"))
NCH = len(CHORES)
CHORE = {name: i for i, (_, name) in enumerate(CHORES)}


def rows_of(t):
    return LAST if t == KT - 1 else 128


def build(nc, xT, xn, ctxT, Wrkvg, brkvg, mix, WoT, vec_c, bias_t, dec_in, eta_in,
          Wq, Wk, Wv, Wxo, gate_wT, gate_b, dec_all_in, headsel_in, w1, w2, w3, b12, b3, ident_in, iota_in, out):
    with ExitStack() as ctx:
        def sb(name, shape, dt=F32):
            return ctx.enter_context(nc.sbuf_tensor(name, shape, dt))

        def sem(name):
            return ctx.enter_context(nc.semaphore(name))

        rkv_d = nc.dram_tensor("rkv_d", (B, T, 3 * C), F32).ap()
        wkv_d = nc.dram_tensor("wkv_d", (B, T, C), F32).ap()
        qparts_d = nc.dram_tensor("qparts_d", (3, C, B * T), BF16).ap()
        kparts_d = nc.dram_tensor("kparts_d", (2, 3, C, S), BF16).ap()

        ident = sb("ident", [128, 128])
        iota = sb("iota", [128, E])
        wrkvg = sb("wrkvg", [C, 4, C])
        w_now = sb("w_now", [C, 4, C])
        w_prev = sb("w_prev", [C, 4, C])
        b_rkvg = sb("b_rkvg", [T, 4 * C])
        mix_s = sb("mix_s", [C, 4])
        mixc_s = sb("mixc_s", [C, 4])
        wo_s = sb("wo_s", [C, C])
        vecc = sb("vecc", [C, 4])
        bias_s = sb("bias_s", [T, 4, C])
        dec = sb("dec", [128, Q4])
        eta = sb("eta", [128, Q4])
        wq_s = sb("wq_s", [C, C])
        wk_s = sb("wk_s", [C, C])
        wv_s = sb("wv_s", [C, C])
        wxo_s = sb("wxo_s", [C, C])
        gw_s = sb("gw_s", [C, E])
        gb_s = sb("gb_s", [T, E])
        eps_s = sb("eps_s", [128, 1])
        x1 = sb("x1", [T, B + 1, C])
        dec_all = sb("dec_all", [1, 2, H])
        clip_test = sb("clip_test", [1, 4, H])
        flags = sb("flags", [1, 4], I32)
        headsel = sb("headsel", [C, H])
        qabs = sb("qabs", [C, B + 1])
        kabs = sb("kabs", [C, 4])
        kbound = sb("kbound", [C, 1])
        gate = sb("gate", [T, B, C])
        arena = sb("arena", [128, 39000])

        def view(off, n, shape=None, dt=F32, rows=128, **dims):
            v = arena[0:rows, off:off + n]
            if dt != F32:
                v = v.bitcast(dt)
            return v

        at = [0]

        def carve(n):
            o = at[0]
            at[0] += n
            assert at[0] <= 39000, at[0]
            return o

        xg = [view(carve(G * (T + 1)), G * (T + 1)).rearrange("p (b t) -> p b t", b=G) for _ in range(2)]
        nat = [view(carve(G * 512), G * 512, rows=T).rearrange("p (b n) -> p b n", b=G) for _ in range(2)]
        gsig = view(carve(G * C), G * C, rows=T).rearrange("p (b n) -> p b n", b=G)
        rkv = view(carve((T + 1) * 96), (T + 1) * 96).rearrange("p (t n) -> p t n", n=96)
        ke = view(carve(T * 32), T * 32).rearrange("p (t n) -> p t n", n=32)
        wkv = view(carve((T + 1) * 32), (T + 1) * 32).rearrange("p (t n) -> p t n", n=32)
        sq = view(carve(T * 64), T * 64).rearrange("p (t n) -> p t n", n=64)
        nrm = view(carve(T * 8), T * 8).rearrange("p (t n) -> p t n", n=8)
        state = [view(carve(256), 256) for _ in range(2)]
        decayed = view(carve(256), 256)
        prod = [view(carve(288), 288).rearrange("p (h i j) -> p h i j", h=4, i=D) for _ in range(2)]
        upd = view(carve(256), 256)
        rprod = view(carve(256), 256)
        small = view(carve(128), 128)
        s1_end = at[0]
        at[0] = 0
        natw = [view(carve(GT * 0 + G * C), G * C, rows=T).rearrange("p (b n) -> p b n", b=G) for _ in range(2)]
        xin = [view(carve(G * C), G * C, rows=T).rearrange("p (b n) -> p b n", b=G) for _ in range(2)]
        attT = view(carve(GT), GT)
        osum = view(carve(G * C), G * C, rows=T).rearrange("p (b n) -> p b n", b=G)
        x1T = view(carve(GT), GT)
        qres = view(carve(GT), GT)
        qpart = view(carve(3 * GT // 2), 3 * GT // 2, dt=BF16).rearrange("p (s n) -> p s n", s=3)
        bst = view(carve(64), 64)
        at[0] = 0
        ctx_s = [view(carve(S), S) for _ in range(2)]
        kres = view(carve(KC[0]), KC[0])
        kpart = view(carve(3 * S // 2), 3 * S // 2, dt=BF16).rearrange("p (s n) -> p s n", s=3)
        kst = [view(carve(PAIRS * S // 2), PAIRS * S // 2, dt=BF16, rows=ROWS).rearrange("p (h n) -> p h n", h=PAIRS)
               for _ in range(2)]
        qst = [view(carve(PAIRS * T), PAIRS * T, dt=BF16, rows=ROWS).rearrange(
            "p (h e t) -> p h e t", h=PAIRS, e=2) for _ in range(2)]
        vst = [view(carve(KT * 256), KT * 256).rearrange("p (k h n) -> p k h n", k=KT, h=PAIRS) for _ in range(2)]
        pexp = [view(carve(UC), UC) for _ in range(SS)]
        dif = [view(carve(UC), UC) for _ in range(2)]
        rmax = view(carve(2 * UC), 2 * UC)
        amax = view(carve(2 * UC), 2 * UC)
        acc_s = view(carve(4 * T), 4 * T)
        rden = view(carve(H), H, rows=T)
        attn = view(carve(C), C, rows=T).rearrange("p (h d) -> p h d", h=H)
        attnT = view(carve(T), T)
        at[0] = 0
        wexp = [view(carve(E * C), E * C).rearrange("p (e n) -> p e n", e=E) for _ in range(3)]
        b12_s = view(carve(2 * E), 2 * E).rearrange("p (l e) -> p l e", l=2)
        b3_s = view(carve(E * C), E * C, rows=T).rearrange("p (e n) -> p e n", e=E)
        x2 = view(carve(G * C), G * C, rows=T).rearrange("p (b n) -> p b n", b=G)
        x2T = view(carve(GT), GT)
        h1 = [view(carve(GT), GT) for _ in range(2)]
        h2 = [view(carve(GT), GT) for _ in range(2)]
        lg = view(carve(G * E), G * E, rows=T).rearrange("p (b e) -> p b e", b=G)
        pr = view(carve(G * E), G * E, rows=T).rearrange("p (b e) -> p b e", b=G)
        top = view(carve(G * 8), G * 8, rows=T).rearrange("p (b e) -> p b e", b=G)
        topi = view(carve(G * 8), G * 8, rows=T, dt=U32).rearrange("p (b e) -> p b e", b=G)
        topf = view(carve(G * 8), G * 8, rows=T).rearrange("p (b e) -> p b e", b=G)
        oh = view(carve(G * E), G * E, rows=T).rearrange("p (b e) -> p b e", b=G)
        cw = view(carve(G * E), G * E, rows=T).rearrange("p (b e) -> p b e", b=G)
        h3 = view(carve(G * C), G * C, rows=T).rearrange("p (b n) -> p b n", b=G)
        fin = [view(carve(G * C), G * C, rows=T).rearrange("p (b n) -> p b n", b=G) for _ in range(2)]
        sm3 = view(carve(64), 64)

        ps = ctx.enter_context(nc.psum_tensor("ps", [128, 8, 512], F32))

        consts_in = sem("consts_in")
        experts_in = sem("experts_in")
        mixed_w = sem("mixed_w")
        xg_zero = sem("xg_zero")
        xg_in = [sem(f"xg_in{i}") for i in range(2)]
        proj_done = sem("proj_done")
        bias_done = sem("bias_done")
        sig_done = sem("sig_done")
        gated = sem("gated")
        rkv_out = sem("rkv_out")
        rkv_in = sem("rkv_in")
        sq_done = sem("sq_done")
        sqrt_done = sem("sqrt_done")
        chain = sem("chain")
        step_ss = sem("step_ss")
        step_n = sem("step_n")
        recur = sem("recur")
        act_recur = sem("act_recur")
        rprod_ready = sem("rprod_ready")
        clip_sig = sem("clip_sig")
        clip_flag = sem("clip_flag")
        wkv_ready = sem("wkv_ready")
        wkv_out = sem("wkv_out")
        var_ready = sem("var_ready")
        std_ready = sem("std_ready")
        natw_in = [sem(f"natw_in{i}") for i in range(2)]
        natw_used = sem("natw_used")
        xin_used = sem("xin_used")
        pe_c = sem("pe_c")
        dve_c = sem("dve_c")
        qpart_ready = sem("qpart_ready")
        q_out = sem("q_out")
        ctx_in = [sem(f"ctx_in{i}") for i in range(2)]
        kpart_ready = sem("kpart_ready")
        kpart_out = sem("kpart_out")
        kst_in = [sem(f"kst_in{i}") for i in range(2)]
        chore_posted = sem("chore_posted")
        chore_taken = sem("chore_taken")
        score1 = sem("score1")
        score1_read = sem("score1_read")
        rmax_ready = sem("rmax_ready")
        amax_ready = sem("amax_ready")
        scored = sem("scored")
        dif_ready = sem("dif_ready")
        exp_done = sem("exp_done")
        pv_done = sem("pv_done")
        stage2_set = sem("stage2_set")
        acc_copied = sem("acc_copied")
        kbound_ready = sem("kbound_ready")
        flag_ready = sem("flag_ready")
        y_ready = sem("y_ready")
        pe3 = sem("pe3")
        dve3 = sem("dve3")
        act3 = sem("act3")
        h2_used = sem("h2_used")
        out_done = sem("out_done")

        PRO = 7
        D3, A3, P3 = 3 + E, 1 + 2 * E, 2 + 3 * E
        out_ready = sem("out_ready")
        waits_passed = sem("waits_passed")
        ch3 = sem("ch3")
        var3 = sem("var3")
        std3 = sem("std3")

        block = ctx.enter_context(nc.Block())

        NCONST = 19

        def passed(eng):
            eng.sem_inc(waits_passed, 1)

        def chained(eng, sm, base):
            n = [0]

            def link(ins):
                n[0] += 1
                ins.then_inc(sm, 1)
                eng.wait_ge(sm, base + n[0])
            return link, n

        N_STEP = 13

        @block.sync
        def _(sp):
            for dst, src in ((ident, ident_in), (iota, iota_in), (wrkvg, Wrkvg), (b_rkvg, brkvg), (mix_s, mix),
                             (wo_s, WoT), (vecc, vec_c), (bias_s, bias_t), (dec, dec_in),
                             (eta, eta_in), (wq_s, Wq), (wk_s, Wk), (wv_s, Wv), (wxo_s, Wxo), (gw_s, gate_wT),
                             (gb_s, gate_b), (dec_all, dec_all_in), (headsel, headsel_in)):
                sp.dma_start(dst[:], src).then_inc(consts_in, 16)
            sp.wait_ge(xg_zero, 1)
            with sp.Fori(0, NG // 2) as gg:
                for u in range(2):
                    g = gg * 2 + u
                    sp.wait_ge(proj_done, g + 1)
                    passed(sp)
                    sp.dma_start(xg[u][:, :, 1:T + 1], xT[:, bass.ds(g * G, G), :]).then_inc(xg_in[u], 16)
                    sp.wait_ge(gated, g + 2)
                    passed(sp)
                    sp.dma_start(rkv_d[bass.ds(g * G, G)].rearrange("b t n -> t b n"),
                                 nat[u][:, :, 0:3 * C]).then_inc(rkv_out, 16)
            sp.wait_ge(rkv_out, 16 * NG + 16)
            for w in range(3):
                for q in range(NQ):
                    sp.dma_start(rkv[32 * q:32 * q + 32, 0:T, 32 * w:32 * w + 32],
                                 rkv_d[:, :, w * C + 32 * q:w * C + 32 * q + 32]).then_inc(rkv_in, 16)
            sp.wait_ge(wkv_ready, 1)
            for q in range(NQ):
                sp.dma_start(wkv_d[:, :, 32 * q:32 * q + 32], wkv[32 * q:32 * q + 32, 1:T + 1, :]).then_inc(wkv_out, 16)
            sp.wait_ge(wkv_out, 16 * NQ)
            with sp.Fori(0, NG // 2) as gg:
                for u in range(2):
                    g = gg * 2 + u
                    sp.wait_ge(qpart_ready, g + 1)
                    passed(sp)
                    sp.dma_start(natw[u][:, :, :], wkv_d[bass.ds(g * G, G)].rearrange("b t n -> t b n")
                                 ).then_inc(natw_in[u], 16)
                    sp.dma_start(xin[u][:, :, :], xn[bass.ds(g * G, G)].rearrange("b t n -> t b n")
                                 ).then_inc(natw_in[u], 16)
                    sp.wait_ge(qpart_ready, g + 2)
                    passed(sp)
                    sp.dma_start(qparts_d[:, :, bass.ds(g * GT, GT)].rearrange("s c n -> c s n"),
                                 qpart[:, :, :]).then_inc(q_out, 16)
                    sp.wait_ge(q_out, 16 * (g + 1) + 16)
                    passed(sp)

            def load_ctx(b, u):
                sp.dma_start(ctx_s[u][:, :], ctxT[bass.ds(b, 1)].rearrange("o c n -> (o c) n")
                             ).then_inc(ctx_in[u], 16)

            def move_parts(b, src, u):
                o = 0
                for i, w in enumerate(KC):
                    sp.wait_ge(kpart_ready, b * 3 + i + 1)
                    passed(sp)
                    sp.dma_start(kparts_d[u, :, :, o:o + w].rearrange("s c n -> c s n"), kpart[:, :, o:o + w]
                                 ).then_inc(kpart_out, 16)
                    o += w
                for s in range(SLOTS):
                    for e in range(2):
                        sp.dma_start(qst[u][16 * s + 8 * e:16 * s + 8 * e + 8, :, e, :],
                                     qparts_d[Q_PART[s], :, bass.ds(src * T, T)].rearrange(
                                         "(h e p) n -> e p h n", e=2, p=8)[e]).then_inc(kst_in[u], 16)
                sp.wait_ge(kpart_out, 16 * 3 * (b + 1))
                passed(sp)
                for s in range(SLOTS):
                    sp.dma_start(kst[u][16 * s:16 * s + 16, :, :],
                                 kparts_d[u, K_PART[s]].rearrange("(h p) n -> p h n", p=16)).then_inc(kst_in[u], 16)

            sp.wait_ge(stage2_set, 1)
            load_ctx(0, 0)
            load_ctx(1, 1)
            move_parts(0, 0, 0)

            def around(b, u, nxt, src):
                if nxt is not None:
                    sp.wait_ge(chore_posted, PRO + NCH * b)
                    passed(sp)
                    load_ctx(nxt, u)
                sp.wait_ge(scored, NU * b + 1)
                passed(sp)
                move_parts(b + 1, src, 1 - u)

            with sp.Fori(0, B // 2 - 1) as i:
                around(2 * i, 0, 2 * i + 2, 2 * i + 1)
                around(2 * i + 1, 1, 2 * i + 3, 2 * i + 2)
            around(B - 2, 0, 0, B - 1)
            around(B - 1, 1, None, 0)
            sp.wait_ge(kst_in[0], 16 * 3 * SLOTS * (B // 2 + 1))
            sp.wait_ge(y_ready, B)
            for dst, src in zip(wexp, (w1, w2, w3)):
                sp.dma_start(dst[:, :, :], src.rearrange("e d o -> d e o")).then_inc(experts_in, 16)
            sp.dma_start(b12_s[:, :, :], b12).then_inc(experts_in, 16)
            sp.dma_start(b3_s[:, :, :], b3).then_inc(experts_in, 16)
            with sp.Fori(0, NG // 2) as gg:
                for u in range(2):
                    g = gg * 2 + u
                    sp.wait_ge(out_ready, g + 1)
                    passed(sp)
                    sp.dma_start(out[bass.ds(g * G, G)].rearrange("b t n -> t b n"), fin[u][:, :, :]
                                 ).then_inc(out_done, 16)
            sp.wait_ge(out_done, 16 * NG + 16)

        @block.tensor
        def _(pe):
            pe.wait_ge(mixed_w, 2)
            with pe.Fori(0, NG // 2) as gg:
                for u in range(2):
                    g = gg * 2 + u
                    pe.wait_ge(xg_in[u], 16 * (gg + 1))
                    pe.wait_ge(bias_done, g + 1)
                    for b in range(G):
                        o = ps[0:T, 4 * u + b, :]
                        nc.tensor.matmul(o, xg[u][:, b, 1:T + 1], w_now[:, :, :], start=True, stop=False)
                        last = nc.tensor.matmul(o, xg[u][:, b, 0:T], w_prev[:, :, :], start=False, stop=True)
                    last.then_inc(proj_done, 1)
            with pe.Fori(0, NG // 2) as gg:
                for u in range(2):
                    g = gg * 2 + u
                    pe.wait_ge(natw_in[u], 32 * (gg + 1))
                    pe.wait_ge(dve_c, g * 4 + 1)
                    for b in range(G):
                        last = nc.tensor.transpose(ps[:, 0, b * T:(b + 1) * T], natw[u][:, b, :], ident[0:T, 0:T])
                    last.then_inc(pe_c, 1)
                    pe.wait_ge(dve_c, g * 4 + 2)
                    for b in range(G):
                        last = nc.tensor.matmul(ps[0:T, 1, b * C:(b + 1) * C], attT[:, b * T:(b + 1) * T], wo_s[:],
                                                start=True, stop=True)
                    last.then_inc(pe_c, 1)
                    pe.wait_ge(dve_c, g * 4 + 3)
                    for b in range(G):
                        last = nc.tensor.transpose(ps[:, 2, b * T:(b + 1) * T], osum[:, b, :], ident[0:T, 0:T])
                    last.then_inc(pe_c, 1)
                    pe.wait_ge(dve_c, g * 4 + 4)
                    nc.tensor.matmul(ps[:, 3, 0:GT], wq_s[:], x1T[:, :], start=True, stop=True).then_inc(pe_c, 1)

            def project_k(u, i):
                o = sum(KC[:i])
                return nc.tensor.matmul(ps[:, 7, 0:KC[i]], wk_s[:], ctx_s[u][:, o:o + KC[i]], start=True, stop=True)

            def project_v(u, i):
                for t in range(4 * i, 4 * i + 4):
                    m = rows_of(t)
                    last = nc.tensor.matmul(ps[0:m, 7, t % 4 * C:(t % 4 + 1) * C],
                                            ctx_s[u][:, t * 128:t * 128 + m], wv_s[:], start=True, stop=True)
                return last

            def bound():
                return nc.tensor.matmul(ps[0:1, 7, 0:H], kbound[:], headsel[:], start=True, stop=True)

            def sums():
                for s in range(2):
                    for e in range(2):
                        last = nc.tensor.transpose(ps[0:T, 7, s * 256 + e * 112:s * 256 + e * 112 + 128],
                                                   acc_s[:, s * 200 + e * 100:s * 200 + e * 100 + 100], ident[:])
                return last

            def scores(u, n):
                t, slot = n // 2, n % SS
                m = rows_of(t)
                for j in range(4):
                    last = nc.tensor.matmul(ps[0:m, 2 * slot + j // 2, j % 2 * 200:j % 2 * 200 + 200],
                                            kst[u][:, n % 2 * 4 + j, t * 128:t * 128 + m],
                                            qst[u][:, n % 2 * 4 + j, :, :], start=True, stop=True)
                return last

            def pv(u, n, slot, t):
                m, un = rows_of(t), n % 2
                for j in range(4):
                    last = nc.tensor.matmul(ps[32 * j:32 * j + 32, 6, un * 200:un * 200 + 200],
                                            vst[u][0:m, t, un * 4 + j, :],
                                            pexp[slot][0:m, j * 200:j * 200 + 200],
                                            start=(n == 0), stop=(n >= NU - 2), skip_group_check=True)
                return last

            def pv_unit(b, u, n):
                if n == 0:
                    pe.wait_ge(acc_copied, b + 1)
                pe.wait_ge(exp_done, NU * (b + 1) + n + 1)
                if n >= NU - 2:
                    passed(pe)
                pv(u, n, n % SS, n // 2).then_inc(pv_done, 1)

            def chore(b, u, name):
                c = CHORE[name]
                pe.wait_ge(chore_taken, PRO + NCH * b + c)
                if name[0] in "kv":
                    i = int(name[1])
                    if name == "k0":
                        pe.wait_ge(ctx_in[1 - u], 8 * (b + 1 - (1 - u)) + 16)
                    last = (project_k if name[0] == "k" else project_v)(1 - u, i)
                elif name == "bound":
                    pe.wait_ge(kbound_ready, b + 2)
                    last = bound()
                elif name == "sums":
                    last = sums()
                elif name == "attn":
                    last = nc.tensor.transpose(ps[:, 7, 0:T], attn[:, :, :], ident[0:T, 0:T])
                else:
                    last = nc.tensor.matmul(ps[0:T, 7, 0:C], attnT[:, :], wxo_s[:], start=True, stop=True)
                last.then_inc(chore_posted, 1)

            def attention(b, u):
                pe.wait_ge(flag_ready, b + 1)
                passed(pe)
                flag = pe.value_load(flags[0:1, 1 + u:2 + u], min_val=0, max_val=1)
                pe.wait_ge(kst_in[u], (8 * (b - u) + 16) * 3 * SLOTS)
                with pe.If(flag):
                    for n in (NU - 2, NU - 1):
                        pv_unit(b - 1, 1 - u, n)
                    for n in range(NU):
                        if n < SS:
                            pe.wait_ge(exp_done, NU * (b + 1) - SS + n + 1)
                        else:
                            pe.wait_ge(score1_read, NU * b + n - SS + 1)
                        scores(u, n).then_inc(score1, 1)
                    for n in range(NU):
                        if n < SS:
                            pe.wait_ge(score1_read, NU * b + NU - SS + n + 1)
                        else:
                            pe.wait_ge(dif_ready, NU * b + n - SS + 1)
                        scores(u, n).then_inc(scored, 1)
                        if n >= 2:
                            pv_unit(b, u, n - 2)
                        for at, name in CHORES:
                            if at == n:
                                chore(b, u, name)
                with pe.Else():
                    pe.sem_inc(score1, NU)
                    for n in range(NU):
                        pe.wait_ge(exp_done, NU * (b + 1) + n - SS + 1)
                        scores(u, n).then_inc(scored, 1)
                        if n < 2:
                            pv_unit(b - 1, 1 - u, NU - 2 + n)
                        else:
                            pv_unit(b, u, n - 2)
                        for at, name in CHORES:
                            if at == n:
                                chore(b, u, name)

            pe.wait_ge(stage2_set, 2)
            for n in range(2):
                pv(1, n, 1, 0)
            pe.wait_ge(ctx_in[0], 16)
            for i, name in enumerate(("k0", "k1", "k2", "bound", "v0", "v1", "v2")):
                if i:
                    pe.wait_ge(chore_taken, i)
                if name == "bound":
                    pe.wait_ge(kbound_ready, 1)
                    last = bound()
                else:
                    last = (project_k if name[0] == "k" else project_v)(0, int(name[1]))
                last.then_inc(chore_posted, 1)
            with pe.Fori(0, B // 2) as i:
                attention(2 * i, 0)
                attention(2 * i + 1, 1)
            for n in (NU - 2, NU - 1):
                pv_unit(B - 1, 1, n)
            for name in ("sums", "attn", "out"):
                i = CHORE[name] - CHORE["sums"]
                if i == 0:
                    pe.wait_ge(acc_copied, B + 1)
                pe.wait_ge(chore_taken, PRO + NCH * B + i)
                if name == "sums":
                    last = sums()
                elif name == "attn":
                    last = nc.tensor.transpose(ps[:, 7, 0:T], attn[:, :, :], ident[0:T, 0:T])
                else:
                    last = nc.tensor.matmul(ps[0:T, 7, 0:C], attnT[:, :], wxo_s[:], start=True, stop=True)
                last.then_inc(chore_posted, 1)

            pe.wait_ge(experts_in, 16 * 5)
            with pe.Fori(0, NG) as g:
                pe.wait_ge(dve3, g * D3 + 1)
                for b in range(G):
                    last = nc.tensor.transpose(ps[:, 0, b * T:(b + 1) * T], x2[:, b, :], ident[0:T, 0:T])
                last.then_inc(pe3, 1)
                pe.wait_ge(dve3, g * D3 + 2)
                for b in range(G):
                    last = nc.tensor.matmul(ps[0:T, 1, b * E:(b + 1) * E], x2T[:, b * T:(b + 1) * T], gw_s[:],
                                            start=True, stop=True)
                last.then_inc(pe3, 1)
                for e in range(E):
                    k = e % 2
                    nc.tensor.matmul(ps[:, 2 + k, 0:GT], wexp[0][:, e, :], x2T[:, :], start=True,
                                     stop=True).then_inc(pe3, 1)
                    pe.wait_ge(act3, g * A3 + 2 + 2 * e)
                    nc.tensor.matmul(ps[:, 4 + k, 0:GT], wexp[1][:, e, :], h1[k][:, :], start=True,
                                     stop=True).then_inc(pe3, 1)
                    pe.wait_ge(act3, g * A3 + 3 + 2 * e)
                    if e >= 2:
                        pe.wait_ge(dve3, g * D3 + 3 + e - 1)
                    for b in range(G):
                        last = nc.tensor.matmul(ps[0:T, 6 + k, b * C:(b + 1) * C], h2[k][:, b * T:(b + 1) * T],
                                                wexp[2][:, e, :], start=True, stop=True)
                    last.then_inc(pe3, 1)

        @block.scalar
        def _(act):
            act.wait_ge(consts_in, 16 * 18)
            nc.scalar.activation(dec[:], dec[:], ACT.Sigmoid).then_inc(sig_done, 1)
            nc.scalar.activation(eta[:], eta[:], ACT.Sigmoid).then_inc(sig_done, 1)
            nc.scalar.activation(dec_all[:], dec_all[:], ACT.Sigmoid).then_inc(clip_sig, 1)
            with act.Fori(0, NG // 2) as gg:
                for u in range(2):
                    g = gg * 2 + u
                    act.wait_ge(bias_done, g + 2)
                    act.wait_ge(gated, g + 1)
                    nc.scalar.activation(nat[u][:, :, 0:C], nat[u][:, :, 0:C], ACT.Sigmoid).then_inc(sig_done, 1)
                    nc.scalar.activation(gsig[:, :, :], nat[u][:, :, 3 * C:4 * C], ACT.Sigmoid).then_inc(sig_done, 1)
            act.wait_ge(sq_done, 1)
            nc.scalar.activation(nrm[:, :, :], nrm[:, :, :], ACT.Sqrt).then_inc(sqrt_done, 1)
            act.wait_ge(clip_flag, 1)
            may_clip = act.value_load(flags[0:1, 0:1], min_val=0, max_val=1)
            with act.If(may_clip):
                with act.Fori(0, T) as t:
                    act.wait_ge(step_ss, t + 1)
                    nc.scalar.activation(small[:, 8:12], small[:, 4:8], ACT.Sqrt, scale=1.0 / MAXN ** 2
                                         ).then_inc(step_n, 1)
            with act.Else():
                def minus_v(t, u):
                    nc.scalar.activation(prod[u][:, :, :, D], rkv[:, bass.ds(t, 1), 64:96].rearrange(
                        "p o (h d) -> p (o h) d", d=D), ACT.Copy, scale=-1.0).then_inc(act_recur, 1)

                act.wait_ge(recur, 1)
                minus_v(0, 0)
                with act.Fori(0, T // 2) as i:
                    for u in range(2):
                        t = 2 * i + u
                        act.wait_ge(recur, t * STEPS + 1)
                        for h in range(Q4):
                            last = nc.scalar.activation(decayed[:, 64 * h:64 * h + 64],
                                                        state[u][:, 64 * h:64 * h + 64], ACT.Copy,
                                                        scale=dec[:, h:h + 1])
                        last.then_inc(act_recur, 1)
                        minus_v(t + 1, 1 - u)
            act.wait_ge(var_ready, 1)
            nc.scalar.activation(small[:, 80:84], small[:, 64:72].rearrange("p (h n) -> p h n", n=2)[:, :, 1],
                                 ACT.Sqrt, bias=eps_s[:]).then_inc(std_ready, 1)
            with act.Fori(0, NG) as g:
                act.wait_ge(var_ready, g + 2)
                nc.scalar.activation(bst[0:T, 40:44], bst[0:T, 32:40].rearrange("p (h n) -> p h n", n=2)[:, :, 1],
                                     ACT.Sqrt, bias=eps_s[0:T]).then_inc(std_ready, 1)
            def exps(b, u):
                act.wait_ge(flag_ready, b + 1)
                passed(act)
                flag = act.value_load(flags[0:1, 1 + u:2 + u], min_val=0, max_val=1)
                with act.If(flag):
                    for n in range(NU):
                        m = rows_of(n // 2)
                        act.wait_ge(dif_ready, NU * b + n + 1)
                        act.wait_ge(pv_done, NU * b + n + 1)
                        nc.scalar.activation(pexp[n % SS][0:m, :], dif[n % 2][0:m, :], ACT.Exp,
                                             scale=float(D) ** -0.5).then_inc(exp_done, 1)
                with act.Else():
                    for n in range(NU):
                        m = rows_of(n // 2)
                        act.wait_ge(pv_done, NU * b + n + 1)
                        act.wait_ge(scored, NU * b + n + 1)
                        nc.scalar.activation(pexp[n % SS][0:m, :].rearrange("p (a n) -> p a n", a=2),
                                             ps[0:m, 2 * (n % SS):2 * (n % SS) + 2, 0:400], ACT.Exp,
                                             scale=float(D) ** -0.5).then_inc(exp_done, 1)

            with act.Fori(0, B // 2) as i:
                exps(2 * i, 0)
                exps(2 * i + 1, 1)
            with act.Fori(0, NG) as g:
                act.wait_ge(var3, 2 * g + 1)
                nc.scalar.activation(sm3[0:T, 40:44], sm3[0:T, 32:40].rearrange("p (h n) -> p h n", n=2)[:, :, 1],
                                     ACT.Sqrt, bias=eps_s[0:T]).then_inc(std3, 1)
                act.wait_ge(dve3, g * D3 + 3)
                nc.scalar.activation(pr[:, :, :], lg[:, :, :], ACT.Exp).then_inc(act3, 1)
                for e in range(E):
                    k = e % 2
                    act.wait_ge(pe3, g * P3 + 3 + 3 * e)
                    nc.scalar.activation(h1[k][:, :], ps[:, 2 + k, 0:GT], ACT.Relu, bias=b12_s[:, 0, e:e + 1]
                                         ).then_inc(act3, 1)
                    act.wait_ge(pe3, g * P3 + 4 + 3 * e)
                    nc.scalar.activation(h2[k][:, :], ps[:, 4 + k, 0:GT], ACT.Relu, bias=b12_s[:, 1, e:e + 1]
                                         ).then_inc(act3, 1)
                act.wait_ge(var3, 2 * g + 2)
                nc.scalar.activation(sm3[0:T, 44:48], sm3[0:T, 32:40].rearrange("p (h n) -> p h n", n=2)[:, :, 1],
                                     ACT.Sqrt, bias=eps_s[0:T]).then_inc(std3, 1)

        @block.gpsimd
        def _(pool):
            pool.wait_ge(clip_flag, 1)
            may_clip = pool.value_load(flags[0:1, 0:1], min_val=0, max_val=1)
            with pool.If(may_clip):
                pool.sem_inc(rprod_ready, 1)
            with pool.Else():
                with pool.Fori(0, T // 2) as i:
                    for u in range(2):
                        t = 2 * i + u
                        pool.wait_ge(recur, (t + 1) * STEPS + 1)
                        nc.gpsimd.tensor_tensor(
                            rprod.rearrange("p (h i j) -> p h i j", h=4, i=D),
                            state[1 - u].rearrange("p (h i j) -> p h i j", h=4, i=D),
                            rkv[:, bass.ds(t, 1), 0:32].rearrange("p o (h d) -> p (o h) d", d=D).unsqueeze(
                                2).broadcast_to([128, 4, D, D]), ALU.mult).then_inc(rprod_ready, 1)

            def maxima(b, u):
                pool.wait_ge(flag_ready, b + 1)
                passed(pool)
                flag = pool.value_load(flags[0:1, 1 + u:2 + u], min_val=0, max_val=1)
                with pool.If(flag):
                    pool.wait_ge(rmax_ready, b + 1)
                    passed(pool)
                    nc.gpsimd.partition_all_reduce(amax[:, :], rmax[:, :], 128, RMAX).then_inc(amax_ready, 1)
                with pool.Else():
                    pool.sem_inc(amax_ready, 1)

            with pool.Fori(0, B // 2) as i:
                maxima(2 * i, 0)
                maxima(2 * i + 1, 1)

        @block.vector
        def _(dve):
            V = nc.vector
            for freed in (proj_done, qpart_ready, bias_done, dve_c, gated):
                dve.sem_inc(freed, 1)
            for stored in (rkv_out, q_out, out_done):
                dve.sem_inc(stored, 16)
            for freed in (pv_done, amax_ready, rprod_ready):
                dve.sem_inc(freed, 1)
            dve.sem_inc(exp_done, NU)
            link, n = chained(dve, chain, 0)
            for u in range(2):
                link(V.memset(xg[u][:, :, 0:1], 0.0))
            link(V.memset(eps_s[:], 1e-5))
            link(V.memset(rkv[:, T:T + 1, :], 0.0))
            link(V.memset(rprod[:, :], 0.0))
            link(V.memset(x1[:, 0, :], 0.0))
            link(V.memset(qabs[:, B:B + 1], 0.0))
            V.memset(state[0][:, :], 0.0).then_inc(xg_zero, 1)
            dve.wait_ge(consts_in, 16 * 18)
            link(V.tensor_scalar(mixc_s[:], mix_s[:], -1.0, 1.0, ALU.mult, ALU.add))
            V.tensor_tensor(w_now[:, :, :], wrkvg[:, :, :], mix_s[:].unsqueeze(2).broadcast_to([C, 4, C]),
                            ALU.mult).then_inc(mixed_w, 1)
            V.tensor_tensor(w_prev[:, :, :], wrkvg[:, :, :], mixc_s[:].unsqueeze(2).broadcast_to([C, 4, C]),
                            ALU.mult).then_inc(mixed_w, 1)
            with dve.Fori(0, NG // 2) as gg:
                for u in range(2):
                    g = gg * 2 + u
                    dve.wait_ge(proj_done, g + 2)
                    dve.wait_ge(rkv_out, 16 * g + 16)
                    V.tensor_tensor(nat[u][:, :, :], ps[0:T, 4 * u:4 * u + 4, :],
                                    b_rkvg[:].unsqueeze(1).broadcast_to([T, G, 512]), ALU.add).then_inc(bias_done, 1)
                    dve.wait_ge(sig_done, 2 * g + 4)
                    V.tensor_tensor(gate[:, bass.ds(g * G, G), :], nat[u][:, :, 3 * C:4 * C], gsig[:, :, :],
                                    ALU.mult).then_inc(gated, 1)
            dve.wait_ge(clip_sig, 1)
            hd, he = dec_all[:, 0, :], dec_all[:, 1, :]
            link(V.scalar_tensor_tensor(clip_test[:, 0, :], hd, 2.0, he, ALU.mult, ALU.subtract))
            link(V.tensor_tensor(clip_test[:, 1, :], hd, hd, ALU.mult))
            link(V.tensor_scalar(clip_test[:, 2, :], clip_test[:, 1, :], -1.0, 1.0, ALU.mult, ALU.add))
            link(V.tensor_tensor(clip_test[:, 2, :], clip_test[:, 2, :], clip_test[:, 0, :], ALU.mult))
            link(V.tensor_tensor(clip_test[:, 1, :], clip_test[:, 1, :], he, ALU.mult))
            link(V.scalar_tensor_tensor(clip_test[:, 3, :], clip_test[:, 2, :], 28.0, clip_test[:, 1, :], ALU.mult,
                                        ALU.subtract))
            link(V.tensor_reduce(clip_test[:, 0, 0:1], clip_test[:, 3, :], AX.X, ALU.min))
            V.tensor_scalar(flags[0:1, 0:1], clip_test[:, 0, 0:1], 0.0, None, ALU.is_lt).then_inc(clip_flag, 1)
            dve.wait_ge(rkv_in, 16 * 12)
            kv = rkv[:, 0:T, 32:96]
            kv8 = kv.rearrange("p t (h d) -> p t h d", d=D)
            link(V.tensor_tensor(sq[:, :, :], kv, kv, ALU.mult))
            V.tensor_reduce(nrm[:, :, :], sq[:, :, :].rearrange("p t (h d) -> p t h d", d=D), AX.X,
                            ALU.add).then_inc(sq_done, 1)
            dve.wait_ge(sqrt_done, 1)
            link(V.tensor_scalar_max(nrm[:, :, :], nrm[:, :, :], 1e-12))
            link(V.reciprocal(nrm[:, :, :], nrm[:, :, :]))
            link(V.tensor_tensor(kv8, kv8, nrm[:, :, :].unsqueeze(3).broadcast_to([128, T, 8, D]), ALU.mult))
            link(V.tensor_tensor(ke[:, :, :].rearrange("p t (h d) -> p t h d", d=D), kv8[:, :, 0:4, :],
                                 eta[:].unsqueeze(1).unsqueeze(3).broadcast_to([128, T, 4, D]), ALU.mult))
            n_pre = n[0]

            def vec_of(tile, t, o):
                return tile[:, bass.ds(t, 1), o:o + 32].rearrange("p o (h d) -> p (o h) d", d=D)

            def over_i(v):
                return v.unsqueeze(2).broadcast_to([128, 4, D, D])

            def over_j(v):
                return v.unsqueeze(3).broadcast_to([128, 4, D, D])

            def head(v):
                return v.unsqueeze(2).broadcast_to([128, 4, D * D])

            st4 = [x.rearrange("p (h i j) -> p h i j", h=4, i=D) for x in state]
            sth = state[0].rearrange("p (h n) -> p h n", h=4)
            up4 = upd.rearrange("p (h i j) -> p h i j", h=4, i=D)
            pred = small[:, 16:48].rearrange("p (h i) -> p h i", h=4)
            dve.sem_inc(recur, 1)
            dve.wait_ge(clip_flag, 1)
            may_clip = dve.value_load(flags[0:1, 0:1], min_val=0, max_val=1)
            with dve.If(may_clip):
                pr4 = prod[0][:, :, :, 0:D]
                with dve.Fori(0, T) as t:
                    link, n = chained(dve, recur, t * N_STEP + 1)
                    link(V.tensor_tensor(pr4, st4[0], over_i(vec_of(rkv, t, 32)), ALU.mult))
                    link(V.tensor_reduce(pred, pr4, AX.X, ALU.add))
                    link(V.tensor_tensor(pred, pred, vec_of(rkv, t, 64), ALU.subtract))
                    link(V.tensor_tensor(sth, sth, head(dec[:]), ALU.mult))
                    link(V.tensor_tensor(up4, over_j(pred), over_i(vec_of(ke, t, 0)), ALU.mult))
                    link(V.tensor_tensor(state[0][:, :], state[0][:, :], upd[:, :], ALU.subtract))
                    link(V.tensor_tensor(upd[:, :], state[0][:, :], state[0][:, :], ALU.mult))
                    link(V.tensor_reduce(small[:, 4:8], upd.rearrange("p (h n) -> p h n", h=4), AX.X, ALU.add))
                    dve.sem_inc(step_ss, 1)
                    dve.wait_ge(step_n, t + 1)
                    link(V.tensor_scalar_max(small[:, 12:16], small[:, 8:12], 1.0))
                    link(V.reciprocal(small[:, 0:4], small[:, 12:16]))
                    link(V.tensor_tensor(sth, sth, head(small[:, 0:4]), ALU.mult))
                    link(V.tensor_tensor(pr4, st4[0], over_i(vec_of(rkv, t, 0)), ALU.mult))
                    link(V.tensor_reduce(vec_of(wkv, t + 1, 0), pr4, AX.X, ALU.add))
                    assert n[0] == N_STEP, n
            with dve.Else():
                def read_out(t):
                    return V.tensor_reduce(vec_of(wkv, t, 0), rprod.rearrange("p (h i j) -> p h i j", h=4, i=D),
                                           AX.X, ALU.add).then_inc(recur, 1)

                with dve.Fori(0, T // 2) as i:
                    for u in range(2):
                        t = 2 * i + u
                        at_step = t * STEPS + 1
                        dve.wait_ge(recur, at_step)
                        V.tensor_tensor(prod[u][:, :, :, 0:D], st4[u], over_i(vec_of(rkv, t, 32)),
                                        ALU.mult).then_inc(recur, 1)
                        dve.wait_ge(act_recur, 2 * t + 1)
                        dve.wait_ge(recur, at_step + 1)
                        V.tensor_reduce(pred, prod[u][:, :, :, :], AX.X, ALU.add).then_inc(recur, 1)
                        dve.wait_ge(recur, at_step + 2)
                        V.tensor_tensor(up4, over_j(pred), over_i(vec_of(ke, t, 0)), ALU.mult).then_inc(recur, 1)
                        dve.wait_ge(rprod_ready, t + 1)
                        read_out(t)
                        dve.wait_ge(act_recur, 2 * t + 2)
                        dve.wait_ge(recur, at_step + 3)
                        V.tensor_tensor(state[1 - u][:, :], decayed[:, :], upd[:, :], ALU.subtract).then_inc(recur, 1)
                dve.wait_ge(rprod_ready, T + 1)
                read_out(T)
                dve.wait_ge(recur, T * STEPS + 2)
            link, n = chained(dve, chain, n_pre)
            bns = upd[:, 0:48].rearrange("p (h c n) -> p h c n", h=4, c=2)
            for h in range(4):
                for c in range(2):
                    last = V.bn_stats(bns[:, h, c, :], wkv[:, 50 * c + 1:50 * c + 51, 8 * h:8 * h + 8])
            link(last)
            for h in range(4):
                last = V.bn_aggr(small[:, 64 + 2 * h:66 + 2 * h], bns[:, h, :, :].rearrange("p c n -> p (c n)"))
                if h < 3:
                    link(last)
            last.then_inc(var_ready, 1)
            dve.wait_ge(std_ready, 1)
            link(V.reciprocal(small[:, 84:88], small[:, 80:84]))
            for h in range(4):
                w = wkv[:, 1:T + 1, 8 * h:8 * h + 8]
                last = V.tensor_scalar(w, w, small[:, 64 + 2 * h:65 + 2 * h], small[:, 84 + h:85 + h],
                                       ALU.subtract, ALU.mult)
            last.then_inc(wkv_ready, 1)
            n_norm = n[0]

            n_c = 11
            with dve.Fori(0, NG // 2) as gg:
                for u in range(2):
                    g = gg * 2 + u
                    link, n = chained(dve, chain, g * n_c + n_pre + n_norm)
                    dve.wait_ge(pe_c, g * 4 + 1)
                    V.tensor_scalar(attT[:, :], ps[:, 0, 0:GT], vecc[:, 0:1], vecc[:, 1:2], ALU.mult,
                                    ALU.add).then_inc(dve_c, 1)
                    dve.wait_ge(pe_c, g * 4 + 2)
                    link(V.tensor_tensor(osum[:, :, :], ps[0:T, 1, :].rearrange("p (b n) -> p b n", b=G),
                                         bias_s[:, 0, :].unsqueeze(1).broadcast_to([T, G, C]), ALU.add))
                    link(V.tensor_tensor(osum[:, :, :], osum[:, :, :], gate[:, bass.ds(g * G, G), :], ALU.mult))
                    link(V.tensor_tensor(osum[:, :, :], osum[:, :, :], xin[u][:, :, :], ALU.add))
                    for b in range(G):
                        last = V.bn_stats(bst[0:T, 6 * b:6 * b + 6], osum[:, b, :])
                    link(last)
                    passed(dve)
                    for b in range(G):
                        last = V.bn_aggr(bst[0:T, 32 + 2 * b:34 + 2 * b], bst[0:T, 6 * b:6 * b + 6])
                    last.then_inc(var_ready, 1)
                    dve.wait_ge(std_ready, g + 2)
                    link(V.reciprocal(bst[0:T, 44:48], bst[0:T, 40:44]))
                    for b in range(G):
                        last = V.tensor_scalar(osum[:, b, :], osum[:, b, :], bst[0:T, 32 + 2 * b:33 + 2 * b],
                                               bst[0:T, 44 + b:45 + b], ALU.subtract, ALU.mult)
                    last.then_inc(dve_c, 1)
                    dve.wait_ge(dve_c, g * 4 + 3)
                    link(V.tensor_tensor(x1[:, bass.ds(g * G + 1, G), :], osum[:, :, :],
                                         bias_s[:, 2, :].unsqueeze(1).broadcast_to([T, G, C]), ALU.add))
                    dve.wait_ge(pe_c, g * 4 + 3)
                    V.tensor_copy(x1T[:, :], ps[:, 2, 0:GT]).then_inc(dve_c, 1)
                    dve.wait_ge(pe_c, g * 4 + 4)
                    dve.wait_ge(q_out, 16 * g + 16)
                    link(V.tensor_scalar(qpart[:, 0, :], ps[:, 3, 0:GT], vecc[:, 2:3], None, ALU.add))
                    link(V.scalar_tensor_tensor(qres[:, :], ps[:, 3, 0:GT], vecc[:, 2:3], qpart[:, 0, :], ALU.add,
                                                ALU.subtract))
                    link(V.tensor_copy(qpart[:, 1, :], qres[:, :]))
                    link(V.tensor_tensor(qpart[:, 2, :], qres[:, :], qpart[:, 1, :], ALU.subtract))
                    link(V.tensor_reduce(qabs[:, bass.ds(g * G, G)], qpart[:, 0, :].rearrange(
                        "p (b t) -> p b t", b=G), AX.X, ALU.max, apply_absolute_value=True))
                    dve.sem_inc(qpart_ready, 1)
                    dve.sem_inc(dve_c, 1)
                    assert n[0] == n_c, n
            base2 = n_pre + n_norm + NG * n_c

            link, n = chained(dve, chain, base2)
            for u in range(2):
                link(V.memset(qst[u][:, :, :, :], 0.0))
                link(V.memset(vst[u][:, :, :, :], 0.0))
                for e in range(2):
                    link(V.memset(vst[u][:, :, :, 16 * e + D:16 * e + D + 1], 1.0))
            link(V.memset(pexp[1][:, :], 1.0))
            link(V.memset(pexp[2][:, :], 1.0))
            base2 += n[0]
            dve.sem_inc(stage2_set, 2)
            n_k, n_bound, n_sums = 3, 1, 2

            def take_k(b, i, posted, base):
                link, n = chained(dve, chain, base)
                o, w = sum(KC[:i]), KC[i]
                p = ps[:, 7, 0:w]
                hi, mid, lo = (kpart[:, j, o:o + w] for j in range(3))
                if not isinstance(b, int):
                    dve.wait_ge(kpart_out, 16 * (3 * b + i - 2))
                dve.wait_ge(chore_posted, posted)
                link(V.tensor_scalar(hi, p, vecc[:, 3:4], None, ALU.add))
                V.scalar_tensor_tensor(kres[:, 0:w], p, vecc[:, 3:4], hi, ALU.add, ALU.subtract
                                       ).then_inc(chore_taken, 1)
                link(V.tensor_reduce(kabs[:, i:i + 1], hi, AX.X, ALU.max, apply_absolute_value=True))
                dve.wait_ge(chore_taken, posted)
                link(V.tensor_copy(mid, kres[:, 0:w]))
                V.tensor_tensor(lo, kres[:, 0:w], mid, ALU.subtract).then_inc(kpart_ready, 1)
                dve.wait_ge(kpart_ready, b * 3 + i + 1)
                assert n[0] == n_k
                if i == 2:
                    V.tensor_reduce(kabs[:, 3:4], kabs[:, 0:3], AX.X, ALU.max).then_inc(chain, 1)
                    dve.wait_ge(chain, base + n_k + 1)
                    V.tensor_tensor(kbound[:], kabs[:, 3:4], qabs[:, bass.ds(b, 1)], ALU.mult
                                    ).then_inc(kbound_ready, 1)

            def take_bound(b, u, posted, base):
                dve.wait_ge(chore_posted, posted)
                V.tensor_reduce(clip_test[0:1, 0, 0:1], ps[0:1, 7, 0:H], AX.X, ALU.max).then_inc(chain, 1)
                dve.wait_ge(chain, base + 1)
                if not isinstance(b, int):
                    dve.wait_ge(amax_ready, b)
                V.tensor_scalar(flags[0:1, 1 + u:2 + u], clip_test[0:1, 0, 0:1], SCORE_BOUND * float(D) ** 0.5,
                                None, ALU.is_gt).then_inc(flag_ready, 1)
                dve.wait_ge(flag_ready, b + 1)
                dve.sem_inc(chore_taken, 1)

            def take_v(b, u, i, posted):
                dve.wait_ge(chore_posted, posted)
                if not isinstance(b, int):
                    dve.wait_ge(pv_done, NU * (b - 1) + 4)
                dst = vst[u].rearrange("p k h (e n) -> p (k h e) n", e=2)
                src = ps[:, 7, :].rearrange("p (k n) -> p k n", n=D)
                if i < 2:
                    V.tensor_copy(dst[:, 64 * i:64 * i + 64, 0:D], src).then_inc(chore_taken, 1)
                else:
                    V.tensor_copy(dst[:, 128:176, 0:D], src[:, 0:48, :])
                    V.tensor_copy(dst[0:LAST, 176:192, 0:D], src[0:LAST, 48:64, :]).then_inc(chore_taken, 1)

            def copy_sums(b):
                dve.wait_ge(pv_done, NU * b + 3)
                V.tensor_copy(acc_s[:, :], ps[:, 6, 0:4 * T]).then_inc(acc_copied, 1)

            def take_sums(posted, base):
                link, n = chained(dve, chain, base)
                dve.wait_ge(chore_posted, posted)
                v = ps[0:T, 7, :].rearrange("p (h n) -> p h n", n=32)
                link(V.reciprocal(rden[:, :], v[:, :, D]))
                link(V.tensor_tensor(attn[:, :, :], v[:, :, 0:D], rden[:, :].unsqueeze(2).broadcast_to([T, H, D]),
                                     ALU.mult))
                assert n[0] == n_sums
                V.tensor_tensor(attn[:, :, :], attn[:, :, :], bias_s[:, 1, :].rearrange("p (h d) -> p h d", d=D),
                                ALU.add).then_inc(chore_taken, 1)

            def take_attn(posted):
                dve.wait_ge(chore_posted, posted)
                V.tensor_copy(attnT[:, :], ps[:, 7, 0:T]).then_inc(chore_taken, 1)

            def take_out(b, posted):
                dve.wait_ge(chore_posted, posted)
                xb = x1[:, bass.ds(b, 1), :].rearrange("p o n -> p (o n)")
                V.tensor_tensor(xb, ps[0:T, 7, 0:C], xb, ALU.add).then_inc(chore_taken, 1)

            n_b = 3 * n_k + 1 + n_bound + n_sums

            def chore(b, u, name, base):
                posted = PRO + NCH * b + CHORE[name] + 1
                if name[0] == "k":
                    take_k(b + 1, int(name[1]), posted, base + n_k * int(name[1]))
                elif name == "bound":
                    take_bound(b + 1, 1 - u, posted, base + 3 * n_k + 1)
                elif name[0] == "v":
                    take_v(b + 1, 1 - u, int(name[1]), posted)
                elif name == "sums":
                    take_sums(posted, base + 3 * n_k + 1 + n_bound)
                elif name == "attn":
                    take_attn(posted)
                else:
                    take_out(b, posted)

            def attention(b, u, base):
                copy_sums(b)
                dve.wait_ge(flag_ready, b + 1)
                passed(dve)
                flag = dve.value_load(flags[0:1, 1 + u:2 + u], min_val=0, max_val=1)
                with dve.If(flag):
                    for n in range(NU):
                        un, m = n % 2, rows_of(n // 2)
                        dve.wait_ge(score1, NU * b + n + 1)
                        src = ps[0:m, 2 * (n % SS):2 * (n % SS) + 2, 0:400]
                        dst = rmax[0:m, un * UC:(un + 1) * UC].rearrange("p (a n) -> p a n", a=2)
                        if n < UNITS:
                            V.tensor_copy(dst, src).then_inc(score1_read, 1)
                        else:
                            dve.wait_ge(score1_read, NU * b + n - 1)
                            V.tensor_tensor(dst, src, dst, ALU.max).then_inc(score1_read, 1)
                    dve.wait_ge(score1_read, NU * (b + 1))
                    dve.sem_inc(rmax_ready, 1)
                    dve.wait_ge(amax_ready, b + 2)
                    for n in range(NU):
                        un, m = n % 2, rows_of(n // 2)
                        dve.wait_ge(scored, NU * b + n + 1)
                        dve.wait_ge(exp_done, NU * (b + 1) + n - 1)
                        V.tensor_tensor(dif[un][0:m, :].rearrange("p (a n) -> p a n", a=2),
                                        ps[0:m, 2 * (n % SS):2 * (n % SS) + 2, 0:400],
                                        amax[0:m, un * UC:(un + 1) * UC].rearrange("p (a n) -> p a n", a=2),
                                        ALU.subtract).then_inc(dif_ready, 1)
                        for at, name in CHORES:
                            if at == n:
                                chore(b, u, name, base)
                with dve.Else():
                    dve.sem_inc(score1_read, NU)
                    dve.sem_inc(rmax_ready, 1)
                    dve.sem_inc(dif_ready, NU)
                    for _, name in CHORES:
                        chore(b, u, name, base)

            for i in range(3):
                take_k(0, i, i + 1, base2 + n_k * i)
            take_bound(0, 0, 4, base2 + 3 * n_k + 1)
            for i in range(3):
                take_v(0, 0, i, 5 + i)
            base2 += 3 * n_k + 1 + n_bound
            with dve.Fori(0, B // 2) as i:
                attention(2 * i, 0, i * (2 * n_b) + base2)
                attention(2 * i + 1, 1, i * (2 * n_b) + base2 + n_b)
            base2 += B * n_b
            copy_sums(B)
            take_sums(PRO + NCH * B + 1, base2)
            take_attn(PRO + NCH * B + 2)
            take_out(B, PRO + NCH * B + 3)
            dve.wait_ge(chore_taken, PRO + NCH * B + 3)
            dve.sem_inc(y_ready, B)

            def layernorm(link, src, dst, k, g, col):
                for b in range(G):
                    last = V.bn_stats(sm3[0:T, 6 * b:6 * b + 6], src[:, b, :])
                link(last)
                passed(dve)
                for b in range(G):
                    last = V.bn_aggr(sm3[0:T, 32 + 2 * b:34 + 2 * b], sm3[0:T, 6 * b:6 * b + 6])
                last.then_inc(var3, 1)
                dve.wait_ge(std3, 2 * g + k)
                link(V.reciprocal(sm3[0:T, 48:52], sm3[0:T, col:col + 4]))
                for b in range(G):
                    last = V.tensor_scalar(dst[:, b, :], src[:, b, :], sm3[0:T, 32 + 2 * b:33 + 2 * b],
                                           sm3[0:T, 48 + b:49 + b], ALU.subtract, ALU.mult)
                return last

            n_3 = 26
            dve.wait_ge(experts_in, 16 * 5)
            with dve.Fori(0, NG // 2) as gg:
                for u in range(2):
                    g = gg * 2 + u
                    link, n = chained(dve, ch3, g * n_3)
                    link(V.tensor_copy(h3[:, :, :], x1[:, bass.ds(g * G + 1, G), :]))
                    layernorm(link, h3, x2, 1, g, 40).then_inc(dve3, 1)
                    dve.wait_ge(pe3, g * P3 + 1)
                    V.tensor_copy(x2T[:, :], ps[:, 0, 0:GT]).then_inc(dve3, 1)
                    dve.wait_ge(pe3, g * P3 + 2)
                    link(V.tensor_tensor(lg[:, :, :], ps[0:T, 1, 0:G * E].rearrange("p (b e) -> p b e", b=G),
                                         gb_s[:].unsqueeze(1).broadcast_to([T, G, E]), ALU.add))
                    link(V.tensor_reduce(sm3[0:T, 52:56], lg[:, :, :], AX.X, ALU.max))
                    V.tensor_tensor(lg[:, :, :], lg[:, :, :], sm3[0:T, 52:56].unsqueeze(2).broadcast_to([T, G, E]),
                                    ALU.subtract).then_inc(dve3, 1)
                    dve.wait_ge(act3, g * A3 + 1)
                    link(V.tensor_reduce(sm3[0:T, 52:56], pr[:, :, :], AX.X, ALU.add))
                    link(V.reciprocal(sm3[0:T, 56:60], sm3[0:T, 52:56]))
                    link(V.tensor_tensor(pr[:, :, :], pr[:, :, :],
                                         sm3[0:T, 56:60].unsqueeze(2).broadcast_to([T, G, E]), ALU.mult))
                    passed(dve)
                    for b in range(G):
                        last = V.max(top[:, b, :], pr[:, b, :])
                    link(last)
                    passed(dve)
                    for b in range(G):
                        last = V.max_index(topi[:, b, :], top[:, b, :], pr[:, b, :])
                    link(last)
                    link(V.tensor_copy(topf[:, :, :], topi[:, :, :]))
                    iob = iota[0:T, :].unsqueeze(1).broadcast_to([T, G, E])
                    for k in range(TOPK):
                        dst = cw if k == 0 else oh
                        link(V.tensor_tensor(dst[:, :, :], topf[:, :, k:k + 1].broadcast_to([T, G, E]), iob,
                                             ALU.is_equal))
                        link(V.tensor_tensor(dst[:, :, :], dst[:, :, :], pr[:, :, k:k + 1].broadcast_to([T, G, E]),
                                             ALU.mult))
                    link(V.tensor_tensor(cw[:, :, :], cw[:, :, :], oh[:, :, :], ALU.add))
                    for e in range(E):
                        k = e % 2
                        dve.wait_ge(pe3, g * P3 + 5 + 3 * e)
                        link(V.tensor_tensor(h3[:, :, :], ps[0:T, 6 + k, :].rearrange("p (b n) -> p b n", b=G),
                                             b3_s[:, e, :].unsqueeze(1).broadcast_to([T, G, C]), ALU.add))
                        for b in range(G):
                            last = V.scalar_tensor_tensor(x2[:, b, :], h3[:, b, :], cw[:, b, e:e + 1], x2[:, b, :],
                                                          ALU.mult, ALU.add)
                        last.then_inc(dve3, 1)
                        dve.wait_ge(dve3, g * D3 + 4 + e)
                    dve.wait_ge(out_done, 16 * g + 16)
                    layernorm(link, x2, fin[u], 2, g, 44).then_inc(out_ready, 1)
                    dve.wait_ge(out_ready, g + 1)
                    assert n[0] == n_3, n


def kernel(**inputs):
    import numpy as np
    import concourse.bacc as bacc
    from concourse.bass_utils import run_bass_kernel_spmd

    a = {k: np.asarray(v) for k, v in inputs.items()}
    A, X, F = "L0_attn_", "L0_xattn_", "L0_ffn_"

    def wide(v, n):
        return np.ascontiguousarray(np.broadcast_to(v, (n,) + v.shape))

    order = (2 * (4 * np.arange(2)[:, None, None] + np.arange(4)) + np.arange(2)[:, None]).reshape(H)
    by_head = (D * order[:, None] + np.arange(D)).reshape(C)
    tm = np.stack([a[A + "time_mix_" + c].reshape(C) for c in "rkvg"], 1)
    arrays = {
        "xT": np.ascontiguousarray(a["x"].transpose(2, 0, 1)),
        "xn": a["x"],
        "ctxT": np.ascontiguousarray(a["ctx_1024"].transpose(0, 2, 1)),
        "Wrkvg": np.stack([a[A + "W_" + c].T for c in "rkvg"], 1),
        "brkvg": wide(np.concatenate([a[A + "b_" + c] for c in "rkvg"]), T),
        "mix": tm,
        "WoT": np.ascontiguousarray(a[A + "W_o"].T),
        "vec_c": np.stack([a[A + "gn_weight"], a[A + "gn_bias"], a[X + "bq"], a[X + "bk"]], 1),
        "bias_t": wide(np.stack([a[A + "b_o"], a[X + "bv"][by_head], a[X + "bo"], a[X + "bo"]]), T),
        "dec_in": np.repeat(a[A + "decay"].reshape(NQ, Q4), B, 0),
        "eta_in": np.repeat(a[A + "eta"].reshape(NQ, Q4), B, 0),
        "Wq": a[X + "Wq"], "Wk": a[X + "Wk"], "Wv": a[X + "Wv"], "Wxo": a[X + "Wo"][by_head],
        "gate_wT": np.ascontiguousarray(a[F + "gate_w"].T),
        "gate_b": wide(a[F + "gate_b"], T),
        "dec_all_in": np.stack([a[A + "decay"].reshape(H), a[A + "eta"].reshape(H)])[None],
        "headsel_in": np.repeat(np.eye(H, dtype=np.float32), D, 0),
        "w1": a[F + "w1"], "w2": a[F + "w2"], "w3": a[F + "w3"],
        "b12": np.ascontiguousarray(np.stack([a[F + "b1"], a[F + "b2"]]).transpose(2, 0, 1)),
        "b3": wide(a[F + "b3"], T),
        "ident_in": np.eye(128, dtype=np.float32),
        "iota_in": wide(np.arange(E, dtype=np.float32), 128),
    }
    nc = bacc.Bacc("TRN2", target_bir_lowering=False, num_devices=1)
    args = [nc.dram_tensor(n + "_dram", v.shape, mybir.dt.from_np(v.dtype), kind="ExternalInput").ap()
            for n, v in arrays.items()]
    args.append(nc.dram_tensor("out_dram", (B, T, C), F32, kind="ExternalOutput").ap())
    build(nc, *args)
    r = run_bass_kernel_spmd(nc, [{n + "_dram": v for n, v in arrays.items()}], core_ids=[0])
    return r.results[0]["out_dram"]
```

```python
from contextlib import ExitStack

import concourse.bass as bass
from concourse import mybir

F32 = mybir.dt.float32
BF16 = mybir.dt.bfloat16
I32 = mybir.dt.int32
U32 = mybir.dt.uint32
ALU = mybir.AluOpType
ACT = mybir.ActivationFunctionType
AX = mybir.AxisListType
RMAX = bass.bass_isa.ReduceOp.max

B, T, C = 32, 100, 128
H, D = 16, 8
S = 1444
E = 8
G = 4
NG = B // G
GT = G * T
Q4 = 4
NQ = H // Q4
KT = (S + 127) // 128
LAST = S - (KT - 1) * 128
PAIRS = H // 2
ARENA = 42000
SLOTS = 6
K_PART = (0, 0, 0, 1, 1, 2)
Q_PART = (0, 1, 2, 0, 1, 0)
ROWS = SLOTS * 16
UNITS = 2
UC = 4 * 2 * T
KC = (482, 482, 480)
NU = KT * UNITS
SS = 3
MAXN = (D ** 0.5) * 2.0
SCORE_BOUND = 64.0
UNROLL = 4
STEPS = 6
CHORES = ((1, "k0"), (5, "k1"), (9, "k2"), (17, "bound"), (19, "sums"), (21, "attn"), (23, "out"))
SPREADS = ((11, "v0"), (12, "v1"), (13, "v2"))
NCH = len(CHORES)
CHORE = {name: i for i, (_, name) in enumerate(CHORES)}


def rows_of(t):
    return LAST if t == KT - 1 else 128


def build(nc, xT, xn, ctxT, Wrkvg, brkvg, mix, WoT, vec_c, bias_t, dec_in, eta_in,
          Wq, Wk, Wv, Wxo, gate_wT, gate_b, dec_all_in, headsel_in, w1, w2, w3, b12, b3, ident_in, iota_in, out):
    with ExitStack() as ctx:
        def sb(name, shape, dt=F32):
            return ctx.enter_context(nc.sbuf_tensor(name, shape, dt))

        def sem(name):
            return ctx.enter_context(nc.semaphore(name))

        v_d = nc.dram_tensor("v_d", (B, 128, KT * C), F32).ap()
        rkv_d = nc.dram_tensor("rkv_d", (B, T, 3 * C), F32).ap()
        wkv_d = nc.dram_tensor("wkv_d", (B, T, C), F32).ap()
        qparts_d = nc.dram_tensor("qparts_d", (3, C, B * T), BF16).ap()
        kparts_d = nc.dram_tensor("kparts_d", (2, 3, C, S), BF16).ap()

        ident = sb("ident", [128, 128])
        iota = sb("iota", [128, E])
        w_now = sb("w_now", [C, 4, C])
        w_prev = sb("w_prev", [C, 4, C])
        mix_s = sb("mix_s", [C, 4])
        mixc_s = sb("mixc_s", [C, 4])
        wo_s = sb("wo_s", [C, C])
        vecc = sb("vecc", [C, 4])
        bias_s = sb("bias_s", [T, 4, C])
        dec = sb("dec", [128, Q4])
        root_eta = sb("root_eta", [T, 2 * H])
        wq_s = sb("wq_s", [C, C])
        wk_s = sb("wk_s", [C, C])
        wv_s = sb("wv_s", [C, C])
        wxo_s = sb("wxo_s", [C, C])
        gw_s = sb("gw_s", [C, E])
        gb_s = sb("gb_s", [T, E])
        eps_s = sb("eps_s", [128, 1])
        x1 = sb("x1", [T, B + 1, C])
        dec_all = sb("dec_all", [1, 2, H])
        clip_test = sb("clip_test", [1, 4, H])
        flags = sb("flags", [1, 4], I32)
        headsel = sb("headsel", [C, H])
        qabs = sb("qabs", [C, B + 2])
        kabs = sb("kabs", [C, 2])
        kbound = sb("kbound", [C, 1])
        gate = sb("gate", [T, B, C])
        arena = sb("arena", [128, ARENA])

        def view(off, n, dt=F32, rows=128):
            v = arena[0:rows, off:off + n]
            if dt != F32:
                v = v.bitcast(dt)
            return v

        at = [0]

        def carve(n):
            o = at[0]
            at[0] += n
            assert at[0] <= ARENA, at[0]
            return o

        def per_batch(v):
            return v.rearrange("p (b n) -> p b n", b=G)

        rkv = view(carve((T + 1) * 96), (T + 1) * 96).rearrange("p (t n) -> p t n", n=96)
        over_wkv = at[0]
        wkv = view(carve((T + 1) * 32), (T + 1) * 32).rearrange("p (t n) -> p t n", n=32)
        state = [view(carve(256), 256) for _ in range(2)]
        decayed = view(carve(256), 256)
        prod = [view(carve(320), 320).rearrange("p (h i j) -> p h i j", h=4, i=D) for _ in range(2)]
        upd = view(carve(256), 256)
        rprod = view(carve(256), 256)
        small = view(carve(128), 128)
        stage2 = at[0]
        at[0] = over_wkv
        xg = [per_batch(view(carve(G * (T + 1)), G * (T + 1))) for _ in range(2)]
        gsig = per_batch(view(carve(G * C), G * C, rows=T))
        kv_sq = per_batch(view(carve(G * 2 * C), G * 2 * C, rows=T))
        nrm = per_batch(view(carve(G * 2 * H), G * 2 * H, rows=T))
        assert at[0] <= over_wkv + (T + 1) * 32
        at[0] = stage2
        kst0 = carve(PAIRS * S // 2)
        kres = view(carve(KC[0]), KC[0])
        kpart = view(carve(3 * S // 2), 3 * S // 2, dt=BF16).rearrange("p (s n) -> p s n", s=3)
        over_k = at[0]
        ctx_s = [view(carve(S), S) for _ in range(2)]
        qst = [view(carve(PAIRS * T), PAIRS * T, dt=BF16, rows=ROWS).rearrange(
            "p (h e t) -> p h e t", h=PAIRS, e=2) for _ in range(2)]
        over_vst1 = at[0] + KT * 256
        vst = [view(carve(KT * 256), KT * 256).rearrange("p (k h n) -> p k h n", k=KT, h=PAIRS) for _ in range(2)]
        over_pexp = at[0]
        pexp = [view(carve(UC), UC) for _ in range(SS)]
        vbuf = [view(carve(KT * C), KT * C) for _ in range(2)]
        over_acc = at[0]
        acc_s = view(carve(4 * T), 4 * T)
        rden = view(carve(H), H, rows=T)
        attn = view(carve(C), C, rows=T).rearrange("p (h d) -> p h d", h=H)
        attnT = view(carve(T), T)
        at[0] = kst0
        rkv_nat = [per_batch(view(carve(G * 3 * C), G * 3 * C, rows=T)) for _ in range(2)]
        nat = [per_batch(view(carve(G * 512), G * 512, rows=T)) for _ in range(2)]
        assert at[0] <= over_k
        b_rkvg = view(over_pexp, 4 * C, rows=T)
        wrkvg = view(over_acc, 4 * C).rearrange("p (w n) -> p w n", w=4)
        dk = view(over_vst1, (T + 1) * 32).rearrange("p (t n) -> p t n", n=32)
        kk = view(over_acc, T * Q4).rearrange("p (t h) -> p t h", h=Q4)
        assert over_vst1 + (T + 1) * 32 <= over_pexp + UC
        at[0] = 0
        natw = [per_batch(view(carve(G * C), G * C, rows=T)) for _ in range(2)]
        xin = [per_batch(view(carve(G * C), G * C, rows=T)) for _ in range(2)]
        osum = [per_batch(view(carve(G * C), G * C, rows=T)) for _ in range(2)]
        attT = [view(carve(GT), GT) for _ in range(2)]
        x1T = [view(carve(GT), GT) for _ in range(2)]
        qpart = [view(carve(3 * GT // 2), 3 * GT // 2, dt=BF16).rearrange("p (s n) -> p s n", s=3) for _ in range(2)]
        qres = view(carve(GT), GT)
        bst = view(carve(64), 64)
        assert at[0] <= over_wkv
        at[0] = 0
        kst = [view(o, PAIRS * S // 2, dt=BF16, rows=ROWS).rearrange("p (h n) -> p h n", h=PAIRS)
               for o in (kst0, carve(PAIRS * S // 2))]
        dif = [view(carve(UC), UC) for _ in range(2)]
        rmax = view(carve(2 * UC), 2 * UC)
        amax = view(carve(2 * UC), 2 * UC)
        wexp = [view(carve(E * C), E * C).rearrange("p (e n) -> p e n", e=E) for _ in range(3)]
        b12_s = view(carve(2 * E), 2 * E).rearrange("p (l e) -> p l e", l=2)
        b3_s = view(carve(C), C, rows=E)
        assert at[0] <= stage2
        at[0] = stage2
        x2, fin, pr, cw = ([view(carve(G * k), G * k, rows=T).rearrange("p (b n) -> p b n", b=G) for _ in range(2)]
                           for k in (C, C, E, E))
        x2T, h1, h2 = ([view(carve(GT), GT) for _ in range(2)] for _ in range(3))
        cwT = [view(carve(GT), GT, rows=E) for _ in range(2)]
        lg, top, topf, oh = (view(carve(G * E), G * E, rows=T).rearrange("p (b e) -> p b e", b=G) for _ in range(4))
        topi = view(carve(G * 8), G * 8, rows=T, dt=U32).rearrange("p (b e) -> p b e", b=G)
        sm3 = view(carve(128), 128, rows=T)

        ps = ctx.enter_context(nc.psum_tensor("ps", [128, 8, 512], F32))

        wrkvg_in = sem("wrkvg_in")
        consts_in = sem("consts_in")
        experts_in = sem("experts_in")
        mixed_w = sem("mixed_w")
        xg_zero = sem("xg_zero")
        xg_in = [sem(f"xg_in{i}") for i in range(2)]
        proj_done = sem("proj_done")
        bias_done = sem("bias_done")
        sig_done = sem("sig_done")
        gated = sem("gated")
        kv_squared = sem("kv_squared")
        norm2_ready = sem("norm2_ready")
        norm_ready = sem("norm_ready")
        rkv_ready = sem("rkv_ready")
        rkv_out = [sem(f"rkv_out{i}") for i in range(2)]
        rkv_in = sem("rkv_in")
        chain = sem("chain")
        step_ss = sem("step_ss")
        step_n = sem("step_n")
        recur = sem("recur")
        act_recur = sem("act_recur")
        rprod_ready = sem("rprod_ready")
        dk_ready = sem("dk_ready")
        vbuf_set = sem("vbuf_set")
        v_posted = sem("v_posted")
        v_copied = sem("v_copied")
        v_out = [sem(f"v_out{i}") for i in range(2)]
        v_in = [sem(f"v_in{i}") for i in range(2)]
        v_spread = sem("v_spread")
        clip_sig = sem("clip_sig")
        clip_flag = sem("clip_flag")
        wkv_ready = sem("wkv_ready")
        wkv_out = [sem(f"wkv_out{i}") for i in range(2)]
        var_ready = sem("var_ready")
        std_ready = sem("std_ready")
        natw_in = [sem(f"natw_in{i}") for i in range(2)]
        wkvT_posted = sem("wkvT_posted")
        attT_ready = sem("attT_ready")
        o_posted = sem("o_posted")
        x_added = sem("x_added")
        x1_ready = sem("x1_ready")
        x1T_posted = sem("x1T_posted")
        x1T_ready = sem("x1T_ready")
        q_posted = sem("q_posted")
        q_high = sem("q_high")
        qpart_ready = sem("qpart_ready")
        q_out = [sem(f"q_out{i}") for i in range(2)]
        ctx_in = [sem(f"ctx_in{i}") for i in range(2)]
        kpart_ready = sem("kpart_ready")
        kpart_out = [sem(f"kpart_out{i}") for i in range(3)]
        kst_in = [sem(f"kst_in{i}") for i in range(2)]
        chore_posted = sem("chore_posted")
        chore_taken = sem("chore_taken")
        score1 = sem("score1")
        score1_read = sem("score1_read")
        rmax_ready = sem("rmax_ready")
        amax_ready = sem("amax_ready")
        scored = sem("scored")
        dif_ready = sem("dif_ready")
        exp_done = sem("exp_done")
        pv_done = sem("pv_done")
        pool_set = sem("pool_set")
        vst_set = sem("vst_set")
        acc_copied = sem("acc_copied")
        kbound_ready = sem("kbound_ready")
        flag_ready = sem("flag_ready")
        x2_ready = sem("x2_ready")
        x2T_posted = sem("x2T_posted")
        x2T_ready = sem("x2T_ready")
        logits_posted = sem("logits_posted")
        logits_ready = sem("logits_ready")
        gate_exp = sem("gate_exp")
        cw_ready = sem("cw_ready")
        cwT_posted = sem("cwT_posted")
        cwT_ready = sem("cwT_ready")
        base_posted = sem("base_posted")
        h1_posted = sem("h1_posted")
        h1_ready = sem("h1_ready")
        h2_posted = sem("h2_posted")
        h2_ready = sem("h2_ready")
        h3_posted = sem("h3_posted")
        h3_used = sem("h3_used")
        out_stored = [sem(f"out_stored{i}") for i in range(2)]

        PRE, POST = 0, 64
        PRO = 8
        out_ready = sem("out_ready")
        waits_passed = sem("waits_passed")
        ch3 = sem("ch3")
        var3 = sem("var3")
        std3 = sem("std3")

        block = ctx.enter_context(nc.Block())

        def passed(eng):
            eng.sem_inc(waits_passed, 1)

        def chained(eng, sm, base):
            n = [0]

            def link(ins):
                n[0] += 1
                ins.then_inc(sm, 1)
                eng.wait_ge(sm, base + n[0])
            return link, n

        N_STEP = 13

        @block.sync
        def _(sp):
            def load_x(g):
                sp.dma_start(xg[g % 2][:, :, 1:T + 1], xT[:, g * G:(g + 1) * G, :]).then_inc(xg_in[g % 2], 16)

            def load_ctx(b, u):
                sp.dma_start(ctx_s[u][:, :], ctxT[bass.ds(b, 1)].rearrange("o c n -> (o c) n")
                             ).then_inc(ctx_in[u], 16)

            for dst, src in ((wrkvg, Wrkvg), (mix_s[:], mix)):
                sp.dma_start(dst, src).then_inc(wrkvg_in, 16)
            sp.wait_ge(xg_zero, 1)
            load_x(0)
            load_x(1)
            sp.dma_start(b_rkvg, brkvg).then_inc(consts_in, 16)
            for dst, src in ((ident, ident_in), (iota, iota_in), (wo_s, WoT), (vecc, vec_c), (bias_s, bias_t), (dec, dec_in),
                             (root_eta, eta_in), (wq_s, Wq), (wk_s, Wk), (wv_s, Wv), (wxo_s, Wxo), (gw_s, gate_wT),
                             (gb_s, gate_b), (dec_all, dec_all_in), (headsel, headsel_in)):
                sp.dma_start(dst[:], src).then_inc(consts_in, 16)

            def redistribute(g):
                sp.wait_ge(rkv_out[g % 2], 16 * (g // 2) + 32)
                for q in range(NQ):
                    sp.dma_start(rkv[32 * q + g * G:32 * q + g * G + G, 0:T, :].rearrange("p t (w n) -> p t w n", w=3),
                                 rkv_d[g * G:(g + 1) * G].rearrange("b t (w q n) -> q b t w n", w=3, q=NQ)[q]
                                 ).then_inc(rkv_in, 16)

            load_ctx(0, 0)
            load_ctx(1, 1)
            sp.wait_ge(proj_done, 1 + 1)
            load_x(2)
            for g in range(NG):
                if g + 3 < NG:
                    sp.wait_ge(proj_done, g + 1 + 2)
                    load_x(g + 3)
                sp.wait_ge(rkv_ready, g + 1)
                sp.dma_start(rkv_d[g * G:(g + 1) * G].rearrange("b t n -> t b n"),
                             rkv_nat[g % 2][:, :, :]).then_inc(rkv_out[g % 2], 16)
                if g:
                    redistribute(g - 1)
            redistribute(NG - 1)

            def store_k(b, u):
                o = 0
                for i, w in enumerate(KC):
                    sp.wait_ge(kpart_ready, b * 3 + i + 1)
                    passed(sp)
                    sp.dma_start(kparts_d[u, :, :, o:o + w].rearrange("s c n -> c s n"), kpart[:, :, o:o + w]
                                 ).then_inc(kpart_out[i], 16)
                    o += w

            def stack_k(b, u):
                for i in range(3):
                    sp.wait_ge(kpart_out[i], 16 * (b + 1))
                    passed(sp)
                for s in range(SLOTS):
                    sp.dma_start(kst[u][16 * s:16 * s + 16, :, :],
                                 kparts_d[u, K_PART[s]].rearrange("(h p) n -> p h n", p=16)).then_inc(kst_in[u], 16)

            def move_q(src, u):
                for s in range(SLOTS):
                    for e in range(2):
                        sp.dma_start(qst[u][16 * s + 8 * e:16 * s + 8 * e + 8, :, e, :],
                                     qparts_d[Q_PART[s], :, bass.ds(src * T, T)].rearrange(
                                         "(h e p) n -> e p h n", e=2, p=8)[e]).then_inc(kst_in[u], 16)

            def load_v(b, u):
                sp.dma_start(vbuf[u][:, :], v_d[bass.ds(b, 1)].rearrange("o p n -> (o p) n")).then_inc(v_in[u], 16)

            def v_moves(b, u, nxt):
                sp.wait_ge(v_posted, b + 1)
                passed(sp)
                load_ctx(nxt, u)
                sp.wait_ge(v_copied, b + 1 + 2)
                passed(sp)
                sp.dma_start(v_d[bass.ds(b, 1)].rearrange("o p n -> (o p) n"), vbuf[u][:, :]).then_inc(v_out[u], 16)

            v_moves(0, 0, 2)
            v_moves(1, 1, 3)
            store_k(0, 0)
            stack_k(0, 0)
            with sp.Fori(1, B // 2 - 1) as i:
                v_moves(2 * i, 0, 2 * i + 2)
                v_moves(2 * i + 1, 1, 2 * i + 3)
            v_moves(B - 2, 0, 2)
            v_moves(B - 1, 1, 1)
            for u in range(2):
                sp.wait_ge(v_out[u], 8 * B + 16)
                load_v(u, u)
            sp.wait_ge(wkv_ready, 1)
            for i in range(2):
                for q in range(NQ):
                    lo = i * B // 2
                    sp.dma_start(wkv_d[lo:lo + B // 2, :, 32 * q:32 * q + 32],
                                 wkv[32 * q + lo:32 * q + lo + B // 2, 1:T + 1, :]).then_inc(wkv_out[i], 16)
            def load_group(g, u):
                sp.dma_start(natw[u][:, :, :], wkv_d[bass.ds(g * G, G)].rearrange("b t n -> t b n")
                             ).then_inc(natw_in[u], 16)
                sp.dma_start(xin[u][:, :, :], xn[bass.ds(g * G, G)].rearrange("b t n -> t b n")
                             ).then_inc(natw_in[u], 16)

            def store_q(g, u):
                sp.wait_ge(qpart_ready, g + 1)
                passed(sp)
                sp.dma_start(qparts_d[:, :, bass.ds(g * GT, GT)].rearrange("s c n -> c s n"),
                             qpart[u][:, :, :]).then_inc(q_out[u], 16)

            sp.wait_ge(wkv_out[0], 16 * NQ)
            load_group(0, 0)
            load_group(1, 1)
            store_k(1, 1)
            sp.wait_ge(wkv_out[1], 16 * NQ)
            sp.wait_ge(x_added, 1)
            load_group(2, 0)
            def q_out_x_in(g, u):
                store_q(g, u)
                sp.wait_ge(x_added, g + 2)
                passed(sp)
                load_group(g + 3, 1 - u)

            with sp.Fori(0, NG // 2 - 2) as gg:
                q_out_x_in(gg * 2, 0)
                q_out_x_in(gg * 2 + 1, 1)
            q_out_x_in(NG - 4, 0)
            store_q(NG - 3, 1)
            sp.wait_ge(q_out[0], 32)
            move_q(0, 0)
            store_q(NG - 2, 0)
            store_q(NG - 1, 1)
            for u in range(2):
                sp.wait_ge(q_out[u], 16 * (NG // 2 + 1))
            for dst, src in zip(wexp, (w1, w2, w3)):
                sp.dma_start(dst[:, :, :], src.rearrange("e d o -> d e o")).then_inc(experts_in, 16)
            sp.dma_start(b12_s[:, :, :], b12).then_inc(experts_in, 16)
            sp.dma_start(b3_s[:, :], b3).then_inc(experts_in, 16)

            def around(b, u, next_ctx, next_v, last):
                if next_ctx is not None:
                    sp.wait_ge(chore_posted, PRO + NCH * b)
                    passed(sp)
                    load_ctx(next_ctx, 1 - u)
                if next_v is not None:
                    sp.wait_ge(v_spread, b + 1)
                    passed(sp)
                    load_v(next_v, u)
                if not last:
                    sp.wait_ge(scored, NU * b + 1)
                    passed(sp)
                    move_q(b + 1, 1 - u)
                    stack_k(b + 1, 1 - u)
                store_k(b + 2, u)

            with sp.Fori(0, B // 2 - 2) as i:
                around(2 * i, 0, 2 * i + 3, 2 * i + 2, False)
                around(2 * i + 1, 1, 2 * i + 4, 2 * i + 3, False)
            around(B - 4, 0, B - 1, B - 2, False)
            around(B - 3, 1, 0, B - 1, False)
            around(B - 2, 0, 0, 0, False)
            around(B - 1, 1, None, None, True)
            for i in range(3):
                sp.wait_ge(kpart_out[i], 16 * (B + 2))
            with sp.Fori(0, NG // 2) as gg:
                for u in range(2):
                    g = gg * 2 + u
                    sp.wait_ge(out_ready, g + 1)
                    passed(sp)
                    sp.dma_start(out[bass.ds(g * G, G)].rearrange("b t n -> t b n"), fin[u][:, :, :]
                                 ).then_inc(out_stored[u], 16)
            for u in range(2):
                sp.wait_ge(out_stored[u], 16 * (NG // 2 + 1))

        @block.tensor
        def _(pe):
            def project_k(u, i):
                o = sum(KC[:i])
                return nc.tensor.matmul(ps[:, 7, 0:KC[i]], wk_s[:], ctx_s[u][:, o:o + KC[i]], start=True, stop=True)

            def project_v(b, u):
                pe.wait_ge(ctx_in[u], 8 * (b - u) + 16)
                pe.wait_ge(v_copied, b + 1)
                for t in range(KT):
                    m = rows_of(t)
                    last = nc.tensor.matmul(ps[0:m, 3 * u + t // 4, t % 4 * C:(t % 4 + 1) * C],
                                            ctx_s[u][:, t * 128:t * 128 + m], wv_s[:], start=True, stop=True)
                last.then_inc(v_posted, 1)

            pe.wait_ge(mixed_w, 2)
            with pe.Fori(0, NG // 2) as gg:
                for u in range(2):
                    g = gg * 2 + u
                    pe.wait_ge(xg_in[u], 16 * (gg + 1))
                    pe.wait_ge(bias_done, g + 1)
                    for b in range(G):
                        o = ps[0:T, 4 * u + b, :]
                        nc.tensor.matmul(o, xg[u][:, b, 1:T + 1], w_now[:, :, :], start=True, stop=False)
                        last = nc.tensor.matmul(o, xg[u][:, b, 0:T], w_prev[:, :, :], start=False, stop=True)
                    last.then_inc(proj_done, 1)
            pe.wait_ge(bias_done, NG + 2)
            pe.wait_ge(ctx_in[0], 16)
            for i in range(3):
                if i:
                    pe.wait_ge(chore_taken, i)
                project_k(0, i).then_inc(chore_posted, 1)
            project_v(0, 0)
            project_v(1, 1)
            with pe.Fori(1, B // 2) as i:
                project_v(2 * i, 0)
                project_v(2 * i + 1, 1)
            pe.wait_ge(v_copied, B + 2)
            pe.wait_ge(ctx_in[1], 8 * B + 16)
            for i in range(3):
                pe.wait_ge(chore_taken, 3 + i)
                project_k(1, i).then_inc(chore_posted, 1)

            def output_projection(g, u):
                pe.wait_ge(natw_in[u], 16 * (g - u) + 32)
                for b in range(G):
                    last = nc.tensor.transpose(ps[:, u, b * T:(b + 1) * T], natw[u][:, b, :], ident[0:T, 0:T])
                last.then_inc(wkvT_posted, 1)
                pe.wait_ge(attT_ready, g + 1)
                for b in range(G):
                    last = nc.tensor.matmul(ps[0:T, 2 + u, b * C:(b + 1) * C], attT[u][:, b * T:(b + 1) * T], wo_s[:],
                                            start=True, stop=True)
                last.then_inc(o_posted, 1)

            def q_projection(g, u):
                pe.wait_ge(x1_ready, g + 1)
                for b in range(G):
                    last = nc.tensor.transpose(ps[:, 4 + u, b * T:(b + 1) * T], osum[u][:, b, :], ident[0:T, 0:T])
                last.then_inc(x1T_posted, 1)
                pe.wait_ge(x1T_ready, g + 1)
                nc.tensor.matmul(ps[:, 6 + u, 0:GT], wq_s[:], x1T[u][:, :], start=True, stop=True).then_inc(q_posted, 1)

            output_projection(0, 0)
            with pe.Fori(0, NG // 2 - 1) as gg:
                for u in range(2):
                    output_projection(gg * 2 + u + 1, 1 - u)
                    q_projection(gg * 2 + u, u)
            output_projection(NG - 1, 1)
            q_projection(NG - 2, 0)
            q_projection(NG - 1, 1)

            def bound():
                return nc.tensor.matmul(ps[0:1, 7, 0:H], kbound[:], headsel[:], start=True, stop=True)

            def sums():
                for s in range(2):
                    for e in range(2):
                        last = nc.tensor.transpose(ps[0:T, 7, s * 256 + e * 112:s * 256 + e * 112 + 128],
                                                   acc_s[:, s * 200 + e * 100:s * 200 + e * 100 + 100], ident[:])
                return last

            def scores(u, n):
                t, slot = n // 2, n % SS
                m = rows_of(t)
                for j in range(4):
                    last = nc.tensor.matmul(ps[0:m, 2 * slot + j // 2, j % 2 * 200:j % 2 * 200 + 200],
                                            kst[u][:, n % 2 * 4 + j, t * 128:t * 128 + m],
                                            qst[u][:, n % 2 * 4 + j, :, :], start=True, stop=True)
                return last

            def pv(u, n, slot, t):
                m, un = rows_of(t), n % 2
                for j in range(4):
                    last = nc.tensor.matmul(ps[32 * j:32 * j + 32, 6, un * 200:un * 200 + 200],
                                            vst[u][0:m, t, un * 4 + j, :],
                                            pexp[slot][0:m, j * 200:j * 200 + 200],
                                            start=(n == 0), stop=(n >= NU - 2), skip_group_check=True)
                return last

            def pv_unit(b, u, n):
                if n == 0:
                    pe.wait_ge(acc_copied, b + 1)
                pe.wait_ge(exp_done, NU * (b + 1) + n + 1)
                if n >= NU - 2:
                    passed(pe)
                pv(u, n, n % SS, n // 2).then_inc(pv_done, 1)

            def chore(b, u, name):
                c = CHORE[name]
                pe.wait_ge(chore_taken, PRO + NCH * b + c)
                if name[0] == "k":
                    if name == "k0":
                        pe.wait_ge(ctx_in[u], 8 * (b + u) + 8 * B + 16)
                    last = project_k(u, int(name[1]))
                elif name == "bound":
                    pe.wait_ge(kbound_ready, b + 3)
                    last = bound()
                elif name == "sums":
                    last = sums()
                elif name == "attn":
                    last = nc.tensor.transpose(ps[:, 7, 0:T], attn[:, :, :], ident[0:T, 0:T])
                else:
                    last = nc.tensor.matmul(ps[0:T, 7, 0:C], attnT[:, :], wxo_s[:], start=True, stop=True)
                last.then_inc(chore_posted, 1)

            def attention(b, u):
                pe.wait_ge(flag_ready, b + 1)
                passed(pe)
                flag = pe.value_load(flags[0:1, 1 + u:2 + u], min_val=0, max_val=1)
                pe.wait_ge(kst_in[u], (8 * (b - u) + 16) * 3 * SLOTS)
                pe.wait_ge(v_spread, b + 1)
                with pe.If(flag):
                    for n in (NU - 2, NU - 1):
                        pv_unit(b - 1, 1 - u, n)
                    for n in range(NU):
                        if n < SS:
                            pe.wait_ge(exp_done, NU * (b + 1) - SS + n + 1)
                        else:
                            pe.wait_ge(score1_read, NU * b + n - SS + 1)
                        scores(u, n).then_inc(score1, 1)
                    for n in range(NU):
                        if n < SS:
                            pe.wait_ge(score1_read, NU * b + NU - SS + n + 1)
                        else:
                            pe.wait_ge(dif_ready, NU * b + n - SS + 1)
                        scores(u, n).then_inc(scored, 1)
                        if n >= 2:
                            pv_unit(b, u, n - 2)
                        for at, name in CHORES:
                            if at == n:
                                chore(b, u, name)
                with pe.Else():
                    pe.sem_inc(score1, NU)
                    for n in range(NU):
                        pe.wait_ge(exp_done, NU * (b + 1) + n - SS + 1)
                        scores(u, n).then_inc(scored, 1)
                        if n < 2:
                            pv_unit(b - 1, 1 - u, NU - 2 + n)
                        else:
                            pv_unit(b, u, n - 2)
                        for at, name in CHORES:
                            if at == n:
                                chore(b, u, name)

            pe.wait_ge(vst_set, 2)
            pe.wait_ge(kbound_ready, 1)
            for n in range(2):
                pv(1, n, 1, 0)
            bound().then_inc(chore_posted, 1)
            pe.wait_ge(kbound_ready, 2)
            bound().then_inc(chore_posted, 1)
            with pe.Fori(0, B // 2) as i:
                attention(2 * i, 0)
                attention(2 * i + 1, 1)
            for n in (NU - 2, NU - 1):
                pv_unit(B - 1, 1, n)
            for name in ("sums", "attn", "out"):
                i = CHORE[name] - CHORE["sums"]
                if i == 0:
                    pe.wait_ge(acc_copied, B + 1)
                pe.wait_ge(chore_taken, PRO + NCH * B + i)
                if name == "sums":
                    last = sums()
                elif name == "attn":
                    last = nc.tensor.transpose(ps[:, 7, 0:T], attn[:, :, :], ident[0:T, 0:T])
                else:
                    last = nc.tensor.matmul(ps[0:T, 7, 0:C], attnT[:, :], wxo_s[:], start=True, stop=True)
                last.then_inc(chore_posted, 1)

            def transposed(g, u):
                pe.wait_ge(x2_ready, g + 1)
                for b in range(G):
                    last = nc.tensor.transpose(ps[:, 0, b * T:(b + 1) * T], x2[u][:, b, :], ident[0:T, 0:T])
                last.then_inc(x2T_posted, 1)

            def logits(g, u):
                pe.wait_ge(x2T_ready, g + 1)
                for b in range(G):
                    last = nc.tensor.matmul(ps[0:T, 1, b * E:(b + 1) * E], x2T[u][:, b * T:(b + 1) * T], gw_s[:],
                                            start=True, stop=True)
                last.then_inc(logits_posted, 1)

            def weighted_bias(g, u, part):
                if part == 0:
                    pe.wait_ge(cw_ready, g + 1)
                    for b in range(G):
                        last = nc.tensor.transpose(ps[0:E, 0, b * T:(b + 1) * T], cw[u][:, b, :], ident[0:T, 0:T])
                    last.then_inc(cwT_posted, 1)
                else:
                    pe.wait_ge(cwT_ready, g + 1)
                    passed(pe)
                    for b in range(G):
                        last = nc.tensor.matmul(ps[0:T, 1, b * C:(b + 1) * C], cwT[u][:, b * T:(b + 1) * T],
                                                b3_s[:, :], start=True, stop=True)
                    last.then_inc(base_posted, 1)

            def layer1(g, u, e):
                pe.wait_ge(h1_ready, g * E + e - 1 + 2)
                nc.tensor.matmul(ps[:, 2 + e % 2, 0:GT], wexp[0][:, e, :], x2T[u][:, :], start=True,
                                 stop=True).then_inc(h1_posted, 1)

            def layer2(g, u, e):
                pe.wait_ge(h1_ready, g * E + e + 1 + 2)
                nc.tensor.matmul(ps[:, 4 + e % 2, 0:GT], wexp[1][:, e, :], h1[e % 2][:, :], start=True,
                                 stop=True).then_inc(h2_posted, 1)

            def layer3(g, u, e):
                pe.wait_ge(h2_ready, g * E + e + 1)
                pe.wait_ge(h3_used, g * E + e - 1 + 2)
                for b in range(G):
                    last = nc.tensor.matmul(ps[0:T, 6 + e % 2, b * C:(b + 1) * C], h2[e % 2][:, b * T:(b + 1) * T],
                                            wexp[2][:, e, :], start=True, stop=True)
                last.then_inc(h3_posted, 1)

            def experts(g, u, last):
                for e in range(E + 2):
                    if e < E:
                        layer1(g, u, e)
                    if 1 <= e <= E:
                        layer2(g, u, e - 1)
                    if e >= 2:
                        layer3(g, u, e - 2)
                    if e in (2, 5):
                        weighted_bias(g, u, e // 5)
                    if e == 6 and not last:
                        transposed(g + 1, 1 - u)
                    if e == 7 and not last:
                        logits(g + 1, 1 - u)

            pe.wait_ge(experts_in, 16 * 5)
            transposed(0, 0)
            logits(0, 0)
            with pe.Fori(0, NG // 2 - 1) as gg:
                experts(gg * 2, 0, False)
                experts(gg * 2 + 1, 1, False)
            experts(NG - 2, 0, False)
            experts(NG - 1, 1, True)

        @block.scalar
        def _(act):
            act.wait_ge(consts_in, 16 * 16)
            nc.scalar.activation(dec[:], dec[:], ACT.Sigmoid).then_inc(sig_done, 1)
            nc.scalar.activation(root_eta[:], root_eta[:], ACT.Sigmoid).then_inc(sig_done, 1)
            nc.scalar.activation(dec_all[:], dec_all[:], ACT.Sigmoid).then_inc(clip_sig, 1)
            act.wait_ge(sig_done, 2)
            nc.scalar.activation(root_eta[:], root_eta[:], ACT.Sqrt).then_inc(sig_done, 1)
            with act.Fori(0, NG // 2) as gg:
                for u in range(2):
                    g = gg * 2 + u
                    act.wait_ge(bias_done, g + 3)
                    nc.scalar.activation(kv_sq[:, :, :], nat[u][:, :, C:3 * C], ACT.Square).then_inc(kv_squared, 1)
                    act.wait_ge(gated, g + 1)
                    act.wait_ge(rkv_out[u], 8 * (g - u) + 16)
                    nc.scalar.activation(rkv_nat[u][:, :, 0:C], nat[u][:, :, 0:C], ACT.Sigmoid).then_inc(sig_done, 1)
                    nc.scalar.activation(gsig[:, :, :], nat[u][:, :, 3 * C:4 * C], ACT.Sigmoid).then_inc(sig_done, 1)
                    act.wait_ge(norm2_ready, g + 1)
                    nc.scalar.activation(nrm[:, :, :], nrm[:, :, :], ACT.Sqrt).then_inc(norm_ready, 1)
            def copy_v(b, u, part):
                if part == 0:
                    act.wait_ge(v_posted, b + 1)
                    act.wait_ge(v_out[u], 8 * (b - u) + 16)
                if part < 2:
                    nc.scalar.activation(vbuf[u][:, 512 * part:512 * part + 512], ps[:, 3 * u + part, :], ACT.Copy)
                else:
                    nc.scalar.activation(vbuf[u][:, 1024:1408], ps[:, 3 * u + 2, 0:384], ACT.Copy)
                    nc.scalar.activation(vbuf[u][0:LAST, 1408:1536], ps[0:LAST, 3 * u + 2, 384:512], ACT.Copy
                                         ).then_inc(v_copied, 1)

            act.wait_ge(vbuf_set, 1)
            act.wait_ge(clip_flag, 1)
            may_clip = act.value_load(flags[0:1, 0:1], min_val=0, max_val=1)
            with act.If(may_clip):
                with act.Fori(0, T) as t:
                    act.wait_ge(step_ss, t + 1)
                    nc.scalar.activation(small[:, 8:12], small[:, 4:8], ACT.Sqrt, scale=1.0 / MAXN ** 2
                                         ).then_inc(step_n, 1)
                with act.Fori(0, B // 2) as i:
                    for u in range(2):
                        for part in range(3):
                            copy_v(2 * i + u, u, part)
            with act.Else():
                def minus_v(t, u):
                    nc.scalar.activation(prod[u][:, :, :, D], rkv[:, bass.ds(t, 1), 64:96].rearrange(
                        "p o (h d) -> p (o h) d", d=D), ACT.Copy, scale=-1.0).then_inc(act_recur, 1)

                act.wait_ge(recur, 1)
                for h in range(Q4):
                    last = nc.scalar.activation(dk[:, :, D * h:D * h + D], rkv[:, :, 32 + D * h:32 + D * h + D],
                                                ACT.Copy, scale=dec[:, h:h + 1])
                last.then_inc(dk_ready, 1)

                def decay(t, u):
                    act.wait_ge(recur, t * STEPS + 1)
                    for h in range(Q4):
                        last = nc.scalar.activation(decayed[:, 64 * h:64 * h + 64],
                                                    state[u][:, 64 * h:64 * h + 64], ACT.Copy,
                                                    scale=dec[:, h:h + 1])
                    last.then_inc(act_recur, 1)
                    minus_v(t + 1, u)

                assert 3 * B <= T and T % 2 == 0
                with act.Fori(0, B // 2) as i:
                    for k in range(6):
                        decay(6 * i + k, k % 2)
                        copy_v(2 * i + k // 3, k // 3, k % 3)
                for t in range(3 * B, T):
                    decay(t, t % 2)
            act.wait_ge(var_ready, 1)
            nc.scalar.activation(small[:, 80:84], small[:, 64:72].rearrange("p (h n) -> p h n", n=2)[:, :, 1],
                                 ACT.Sqrt, bias=eps_s[:]).then_inc(std_ready, 1)
            def scaled_wkv(g, u):
                act.wait_ge(wkvT_posted, g + 1)
                nc.scalar.activation(attT[u][:, :], ps[:, u, 0:GT], ACT.Identity, scale=vecc[:, 0:1],
                                     bias=vecc[:, 1:2]).then_inc(attT_ready, 1)

            def x1_and_q(g, u):
                act.wait_ge(var_ready, g + 2)
                nc.scalar.activation(bst[0:T, 40:44], bst[0:T, 32:40].rearrange("p (h n) -> p h n", n=2)[:, :, 1],
                                     ACT.Sqrt, bias=eps_s[0:T]).then_inc(std_ready, 1)
                act.wait_ge(x1T_posted, g + 1)
                nc.scalar.activation(x1T[u][:, :], ps[:, 4 + u, 0:GT], ACT.Copy).then_inc(x1T_ready, 1)
                act.wait_ge(q_posted, g + 1)
                act.wait_ge(q_out[u], 8 * (g - u) + 16)
                nc.scalar.activation(qpart[u][:, 0, :], ps[:, 6 + u, 0:GT], ACT.Identity, bias=vecc[:, 2:3]
                                     ).then_inc(q_high, 1)

            scaled_wkv(0, 0)
            with act.Fori(0, NG // 2 - 1) as gg:
                for u in range(2):
                    scaled_wkv(gg * 2 + u + 1, 1 - u)
                    x1_and_q(gg * 2 + u, u)
            scaled_wkv(NG - 1, 1)
            x1_and_q(NG - 2, 0)
            x1_and_q(NG - 1, 1)
            def exps(b, u):
                act.wait_ge(flag_ready, b + 1)
                passed(act)
                flag = act.value_load(flags[0:1, 1 + u:2 + u], min_val=0, max_val=1)
                with act.If(flag):
                    for n in range(NU):
                        m = rows_of(n // 2)
                        act.wait_ge(dif_ready, NU * b + n + 1)
                        act.wait_ge(pv_done, NU * b + n + 1)
                        nc.scalar.activation(pexp[n % SS][0:m, :], dif[n % 2][0:m, :], ACT.Exp,
                                             scale=float(D) ** -0.5).then_inc(exp_done, 1)
                with act.Else():
                    for n in range(NU):
                        m = rows_of(n // 2)
                        act.wait_ge(pv_done, NU * b + n + 1)
                        act.wait_ge(scored, NU * b + n + 1)
                        nc.scalar.activation(pexp[n % SS][0:m, :].rearrange("p (a n) -> p a n", a=2),
                                             ps[0:m, 2 * (n % SS):2 * (n % SS) + 2, 0:400], ACT.Exp,
                                             scale=float(D) ** -0.5).then_inc(exp_done, 1)

            with act.Fori(0, B // 2) as i:
                exps(2 * i, 0)
                exps(2 * i + 1, 1)
            def std(o):
                nc.scalar.activation(sm3[:, o + 40:o + 44],
                                     sm3[:, o + 32:o + 40].rearrange("p (h n) -> p h n", n=2)[:, :, 1],
                                     ACT.Sqrt, bias=eps_s[0:T]).then_inc(std3, 1)

            def gate_exps(g, u):
                act.wait_ge(logits_ready, g + 1)
                nc.scalar.activation(pr[u][:, :, :], lg[:, :, :], ACT.Exp).then_inc(gate_exp, 1)

            def relus(g, u, first, last):
                for e in range(E + 1):
                    if e < E:
                        act.wait_ge(h1_posted, g * E + e + 1)
                        nc.scalar.activation(h1[e % 2][:, :], ps[:, 2 + e % 2, 0:GT], ACT.Relu,
                                             bias=b12_s[:, 0, e:e + 1]).then_inc(h1_ready, 1)
                    if e >= 1:
                        act.wait_ge(h2_posted, g * E + e)
                        act.wait_ge(h3_posted, g * E + e - 2 + 2)
                        nc.scalar.activation(h2[(e - 1) % 2][:, :], ps[:, 4 + (e - 1) % 2, 0:GT], ACT.Relu,
                                             bias=b12_s[:, 1, e - 1:e]).then_inc(h2_ready, 1)
                    if e == 2 and not first:
                        act.wait_ge(var3, 2 * g + 1)
                        std(POST)
                    if e == 3 and not last:
                        act.wait_ge(var3, 2 * g + 2)
                        std(PRE)
                if not last:
                    gate_exps(g + 1, 1 - u)

            act.wait_ge(var3, 1)
            std(PRE)
            gate_exps(0, 0)
            relus(0, 0, True, False)
            with act.Fori(0, NG // 2 - 1) as gg:
                relus(gg * 2 + 1, 1, False, False)
                relus(gg * 2 + 2, 0, False, False)
            relus(NG - 1, 1, False, True)
            act.wait_ge(var3, 2 * NG)
            std(POST)

        @block.gpsimd
        def _(pool):
            for u in range(2):
                last = nc.gpsimd.memset(vbuf[u][:, (KT - 1) * C:KT * C], 0.0)
            last.then_inc(vbuf_set, 1)
            for u in range(2):
                nc.gpsimd.memset(qst[u][:, :, :, :], 0.0).then_inc(pool_set, 1)
            for i in (1, 2):
                nc.gpsimd.memset(pexp[i][:, :], 1.0).then_inc(pool_set, 1)

            def clear_v(u, done):
                nc.gpsimd.memset(vst[u][:, :, :, :], 0.0).then_inc(pool_set, 1)
                pool.wait_ge(pool_set, done + 1)
                for e in range(2):
                    nc.gpsimd.memset(vst[u][:, :, :, 16 * e + D:16 * e + D + 1], 1.0).then_inc(pool_set, 1)
                pool.wait_ge(pool_set, done + 3)
                pool.sem_inc(vst_set, 1)

            clear_v(0, 4)
            pool.wait_ge(clip_flag, 1)
            may_clip = pool.value_load(flags[0:1, 0:1], min_val=0, max_val=1)
            with pool.If(may_clip):
                pool.sem_inc(rprod_ready, 1)
            with pool.Else():
                with pool.Fori(0, T // UNROLL) as i:
                    for k in range(UNROLL):
                        t, u = UNROLL * i + k, k % 2
                        pool.wait_ge(recur, (t + 1) * STEPS + 1)
                        nc.gpsimd.tensor_tensor(
                            rprod.rearrange("p (h i j) -> p h i j", h=4, i=D),
                            state[1 - u].rearrange("p (h i j) -> p h i j", h=4, i=D),
                            rkv[:, bass.ds(t, 1), 0:32].rearrange("p o (h d) -> p (o h) d", d=D).unsqueeze(
                                2).broadcast_to([128, 4, D, D]), ALU.mult).then_inc(rprod_ready, 1)

            pool.wait_ge(wkv_ready, 1)
            clear_v(1, 7)

            def maxima(b, u):
                pool.wait_ge(flag_ready, b + 1)
                passed(pool)
                flag = pool.value_load(flags[0:1, 1 + u:2 + u], min_val=0, max_val=1)
                with pool.If(flag):
                    pool.wait_ge(rmax_ready, b + 1)
                    passed(pool)
                    nc.gpsimd.partition_all_reduce(amax[:, :], rmax[:, :], 128, RMAX).then_inc(amax_ready, 1)
                    pool.wait_ge(amax_ready, b + 2)
                    passed(pool)
                with pool.Else():
                    pool.sem_inc(amax_ready, 1)

            with pool.Fori(0, B // 2) as i:
                maxima(2 * i, 0)
                maxima(2 * i + 1, 1)

        @block.vector
        def _(dve):
            V = nc.vector
            for freed in (proj_done, bias_done, bias_done, gated, v_copied, v_copied):
                dve.sem_inc(freed, 1)
            for stored in (*rkv_out, *v_out, *q_out, *out_stored):
                dve.sem_inc(stored, 16)
            for freed in (pv_done, amax_ready, rprod_ready):
                dve.sem_inc(freed, 1)
            dve.sem_inc(exp_done, NU)
            link, n = chained(dve, chain, 0)
            for u in range(2):
                link(V.memset(xg[u][:, :, 0:1], 0.0))
            dve.sem_inc(xg_zero, 1)
            link(V.memset(eps_s[:], 1e-5))
            link(V.memset(rkv[:, T:T + 1, :], 0.0))
            link(V.memset(rprod[:, :], 0.0))
            link(V.memset(x1[:, 0, :], 0.0))
            link(V.memset(qabs[:, B:B + 2], 0.0))
            link(V.memset(state[0][:, :], 0.0))
            dve.wait_ge(wrkvg_in, 16 * 2)
            link(V.tensor_scalar(mixc_s[:], mix_s[:], -1.0, 1.0, ALU.mult, ALU.add))
            V.tensor_tensor(w_now[:, :, :], wrkvg[:, :, :], mix_s[:].unsqueeze(2).broadcast_to([C, 4, C]),
                            ALU.mult).then_inc(mixed_w, 1)
            V.tensor_tensor(w_prev[:, :, :], wrkvg[:, :, :], mixc_s[:].unsqueeze(2).broadcast_to([C, 4, C]),
                            ALU.mult).then_inc(mixed_w, 1)
            dve.wait_ge(consts_in, 16 * 16)
            n_pre = n[0]
            n_a = 3

            def add_bias(g, u):
                dve.wait_ge(proj_done, g + 2)
                V.tensor_tensor(nat[u][:, :, :], ps[0:T, 4 * u:4 * u + 4, :],
                                b_rkvg.unsqueeze(1).broadcast_to([T, G, 512]), ALU.add).then_inc(bias_done, 1)

            def finish(g, u):
                link, n = chained(dve, chain, g * n_a + n_pre)
                kv8 = nat[u][:, :, C:3 * C].rearrange("p b (h d) -> p b h d", d=D)
                dve.wait_ge(kv_squared, g + 1)
                V.tensor_reduce(nrm[:, :, :], kv_sq[:, :, :].rearrange("p b (h d) -> p b h d", d=D), AX.X,
                                ALU.add).then_inc(norm2_ready, 1)
                dve.wait_ge(sig_done, 2 * g + 5)
                V.tensor_tensor(gate[:, bass.ds(g * G, G), :], nat[u][:, :, 3 * C:4 * C], gsig[:, :, :],
                                ALU.mult).then_inc(gated, 1)
                dve.wait_ge(norm_ready, g + 1)
                link(V.tensor_scalar_max(nrm[:, :, :], nrm[:, :, :], 1e-12))
                link(V.reciprocal(nrm[:, :, :], nrm[:, :, :]))
                link(V.tensor_tensor(nrm[:, :, :], nrm[:, :, :],
                                     root_eta[:].unsqueeze(1).broadcast_to([T, G, 2 * H]), ALU.mult))
                dve.wait_ge(rkv_out[u], 8 * (g - u) + 16)
                V.tensor_tensor(rkv_nat[u][:, :, C:3 * C].rearrange("p b (h d) -> p b h d", d=D), kv8, nrm[:, :, :].unsqueeze(3).broadcast_to([T, G, 2 * H, D]),
                                ALU.mult).then_inc(rkv_ready, 1)
                dve.wait_ge(rkv_ready, g + 1)
                assert n[0] == n_a

            add_bias(0, 0)
            with dve.Fori(0, NG // 2 - 1) as gg:
                for u in range(2):
                    g = gg * 2 + u
                    add_bias(g + 1, 1 - u)
                    finish(g, u)
            add_bias(NG - 1, 1)
            finish(NG - 2, 0)
            finish(NG - 1, 1)
            link, n = chained(dve, chain, NG * n_a + n_pre)
            dve.wait_ge(clip_sig, 1)
            hd, he = dec_all[:, 0, :], dec_all[:, 1, :]
            link(V.scalar_tensor_tensor(clip_test[:, 0, :], hd, 2.0, he, ALU.mult, ALU.subtract))
            link(V.tensor_tensor(clip_test[:, 1, :], hd, hd, ALU.mult))
            link(V.tensor_scalar(clip_test[:, 2, :], clip_test[:, 1, :], -1.0, 1.0, ALU.mult, ALU.add))
            link(V.tensor_tensor(clip_test[:, 2, :], clip_test[:, 2, :], clip_test[:, 0, :], ALU.mult))
            link(V.tensor_tensor(clip_test[:, 1, :], clip_test[:, 1, :], he, ALU.mult))
            link(V.scalar_tensor_tensor(clip_test[:, 3, :], clip_test[:, 2, :], 28.0, clip_test[:, 1, :], ALU.mult,
                                        ALU.subtract))
            link(V.tensor_reduce(clip_test[:, 0, 0:1], clip_test[:, 3, :], AX.X, ALU.min))
            V.tensor_scalar(flags[0:1, 0:1], clip_test[:, 0, 0:1], 0.0, None, ALU.is_lt).then_inc(clip_flag, 1)
            n_pre += NG * n_a + n[0]
            n_k, n_bound, n_sums = 2, 1, 2

            def take_k(b, i, posted, base):
                link, n = chained(dve, chain, base)
                o, w = sum(KC[:i]), KC[i]
                first = isinstance(b, int) and b == 0
                if i or not first:
                    dve.wait_ge(kpart_ready, 3 * b + i)
                p = ps[:, 7, 0:w]
                hi, mid, lo = (kpart[:, j, o:o + w] for j in range(3))
                if not first:
                    dve.wait_ge(kpart_out[i], 16 * b)
                dve.wait_ge(chore_posted, posted)
                link(V.tensor_scalar(hi, p, vecc[:, 3:4], None, ALU.add))
                V.scalar_tensor_tensor(kres[:, 0:w], p, vecc[:, 3:4], hi, ALU.add, ALU.subtract
                                       ).then_inc(chore_taken, 1)
                dve.wait_ge(chore_taken, posted)
                link(V.tensor_copy(mid, kres[:, 0:w]))
                V.tensor_tensor(lo, kres[:, 0:w], mid, ALU.subtract).then_inc(kpart_ready, 1)
                assert n[0] == n_k

            def k_max(u, base):
                V.tensor_reduce(kabs[:, u:u + 1], kpart[:, 0, :], AX.X, ALU.max, apply_absolute_value=True
                                ).then_inc(chain, 1)
                dve.wait_ge(chain, base + 3 * n_k + 1)

            def bound_scores(b, u):
                V.tensor_tensor(kbound[:], kabs[:, u:u + 1], qabs[:, bass.ds(b, 1)], ALU.mult
                                ).then_inc(kbound_ready, 1)

            def spread_v(b, u, i):
                dve.wait_ge(v_in[u], 8 * (b - u) + 16)
                if not isinstance(b, int):
                    dve.wait_ge(pv_done, NU * (b - 1) + 4)
                dst = vst[u].rearrange("p k h (e n) -> p (k h e) n", e=2)
                src = vbuf[u][:, :].rearrange("p (k n) -> p k n", n=D)
                if i < 2:
                    V.tensor_copy(dst[:, 64 * i:64 * i + 64, 0:D], src[:, 64 * i:64 * i + 64, :])
                else:
                    V.tensor_copy(dst[:, 128:176, 0:D], src[:, 128:176, :])
                    V.tensor_copy(dst[0:LAST, 176:192, 0:D], src[0:LAST, 176:192, :]).then_inc(v_spread, 1)

            for i in range(3):
                take_k(0, i, i + 1, n_pre + n_k * i)
            n_pre += 3 * n_k
            dve.wait_ge(rkv_in, 16 * NQ * NG)

            def vec_of(tile, t, o):
                return tile[:, bass.ds(t, 1), o:o + 32].rearrange("p o (h d) -> p (o h) d", d=D)

            def over_i(v):
                return v.unsqueeze(2).broadcast_to([128, 4, D, D])

            def over_j(v):
                return v.unsqueeze(3).broadcast_to([128, 4, D, D])

            def head(v):
                return v.unsqueeze(2).broadcast_to([128, 4, D * D])

            st4 = [x.rearrange("p (h i j) -> p h i j", h=4, i=D) for x in state]
            sth = state[0].rearrange("p (h n) -> p h n", h=4)
            up4 = upd.rearrange("p (h i j) -> p h i j", h=4, i=D)
            pred = small[:, 16:48].rearrange("p (h i) -> p h i", h=4)
            dve.sem_inc(recur, 1)
            dve.wait_ge(clip_flag, 1)
            may_clip = dve.value_load(flags[0:1, 0:1], min_val=0, max_val=1)
            with dve.If(may_clip):
                dve.sem_inc(chain, 2)
                pr4 = prod[0][:, :, :, 0:D]
                with dve.Fori(0, T) as t:
                    link, n = chained(dve, recur, t * N_STEP + 1)
                    link(V.tensor_tensor(pr4, st4[0], over_i(vec_of(rkv, t, 32)), ALU.mult))
                    link(V.tensor_reduce(pred, pr4, AX.X, ALU.add))
                    link(V.tensor_tensor(pred, pred, vec_of(rkv, t, 64), ALU.subtract))
                    link(V.tensor_tensor(sth, sth, head(dec[:]), ALU.mult))
                    link(V.tensor_tensor(up4, over_j(pred), over_i(vec_of(rkv, t, 32)), ALU.mult))
                    link(V.tensor_tensor(state[0][:, :], state[0][:, :], upd[:, :], ALU.subtract))
                    link(V.tensor_tensor(upd[:, :], state[0][:, :], state[0][:, :], ALU.mult))
                    link(V.tensor_reduce(small[:, 4:8], upd.rearrange("p (h n) -> p h n", h=4), AX.X, ALU.add))
                    dve.sem_inc(step_ss, 1)
                    dve.wait_ge(step_n, t + 1)
                    link(V.tensor_scalar_max(small[:, 12:16], small[:, 8:12], 1.0))
                    link(V.reciprocal(small[:, 0:4], small[:, 12:16]))
                    link(V.tensor_tensor(sth, sth, head(small[:, 0:4]), ALU.mult))
                    link(V.tensor_tensor(pr4, st4[0], over_i(vec_of(rkv, t, 0)), ALU.mult))
                    link(V.tensor_reduce(vec_of(wkv, t + 1, 0), pr4, AX.X, ALU.add))
                    assert n[0] == N_STEP, n
            with dve.Else():
                link, n = chained(dve, chain, n_pre)
                link(V.tensor_tensor(wkv[:, 0:T, :], rkv[:, 0:T, 32:64], rkv[:, 1:T + 1, 32:64], ALU.mult))
                link(V.tensor_reduce(kk[:, :, :], wkv[:, 0:T, :].rearrange("p t (h d) -> p t h d", d=D), AX.X,
                                     ALU.add))
                V.tensor_scalar(pred, vec_of(rkv, 0, 64), -1.0, None, ALU.mult).then_inc(recur, 1)
                dve.wait_ge(dk_ready, 1)

                def read_out(t):
                    return V.tensor_reduce(vec_of(wkv, t, 0), rprod.rearrange("p (h i j) -> p h i j", h=4, i=D),
                                           AX.X, ALU.add).then_inc(recur, 1)

                with dve.Fori(0, T // UNROLL) as i:
                    for k in range(UNROLL):
                        t, u = UNROLL * i + k, k % 2
                        at_step = t * STEPS + 2
                        dve.wait_ge(recur, at_step - 1)
                        V.tensor_tensor(prod[u][:, :, :, 0:D], st4[u], over_i(vec_of(dk, t + 1, 0)),
                                        ALU.mult).then_inc(recur, 1)
                        dve.wait_ge(recur, at_step)
                        V.tensor_tensor(up4, over_j(pred), over_i(vec_of(rkv, t, 32)), ALU.mult).then_inc(recur, 1)
                        V.scalar_tensor_tensor(prod[u][:, :, :, D + 1], pred, -1.0,
                                               kk[:, bass.ds(t, 1), :].rearrange("p o h -> p (o h)").unsqueeze(
                                                   2).broadcast_to([128, 4, D]), ALU.mult, ALU.mult
                                               ).then_inc(recur, 1)
                        dve.wait_ge(rprod_ready, t + 1)
                        read_out(t)
                        dve.wait_ge(act_recur, 2 * t + 1)
                        dve.wait_ge(recur, at_step + 2)
                        V.tensor_tensor(state[1 - u][:, :], decayed[:, :], upd[:, :], ALU.subtract).then_inc(recur, 1)
                        dve.wait_ge(act_recur, 2 * t + 2)
                        dve.wait_ge(recur, at_step + 3)
                        V.tensor_reduce(pred, prod[u][:, :, :, :], AX.X, ALU.add).then_inc(recur, 1)
                dve.wait_ge(rprod_ready, T + 1)
                read_out(T)
                dve.wait_ge(recur, T * STEPS + 3)
            n_pre += 2
            link, n = chained(dve, chain, n_pre)
            bns = upd[:, 0:48].rearrange("p (h c n) -> p h c n", h=4, c=2)
            for h in range(4):
                for c in range(2):
                    last = V.bn_stats(bns[:, h, c, :], wkv[:, 50 * c + 1:50 * c + 51, 8 * h:8 * h + 8])
            link(last)
            for h in range(4):
                last = V.bn_aggr(small[:, 64 + 2 * h:66 + 2 * h], bns[:, h, :, :].rearrange("p c n -> p (c n)"))
                if h < 3:
                    link(last)
            last.then_inc(var_ready, 1)
            dve.wait_ge(std_ready, 1)
            link(V.reciprocal(small[:, 84:88], small[:, 80:84]))
            for h in range(4):
                w = wkv[:, 1:T + 1, 8 * h:8 * h + 8]
                last = V.tensor_scalar(w, w, small[:, 64 + 2 * h:65 + 2 * h], small[:, 84 + h:85 + h],
                                       ALU.subtract, ALU.mult)
            last.then_inc(wkv_ready, 1)
            n_norm = n[0]
            base_c = n_pre + n_norm
            k_max(0, base_c - 3 * n_k)
            base_c += 1
            for i in range(3):
                take_k(1, i, 4 + i, base_c + n_k * i)
            k_max(1, base_c)
            base_c += 3 * n_k + 1
            dve.wait_ge(vst_set, 1)
            for i in range(3):
                spread_v(0, 0, i)

            n_mix, n_split = 4, 3

            def mix_in(link, g, u):
                dve.wait_ge(o_posted, g + 1)
                link(V.tensor_tensor(osum[u][:, :, :], per_batch(ps[0:T, 2 + u, :]),
                                     bias_s[:, 0, :].unsqueeze(1).broadcast_to([T, G, C]), ALU.add))
                link(V.tensor_tensor(osum[u][:, :, :], osum[u][:, :, :], gate[:, bass.ds(g * G, G), :], ALU.mult))
                V.tensor_tensor(osum[u][:, :, :], osum[u][:, :, :], xin[u][:, :, :], ALU.add).then_inc(x_added, 1)
                dve.wait_ge(x_added, g + 1)
                for b in range(G):
                    last = V.bn_stats(bst[0:T, 6 * b:6 * b + 6], osum[u][:, b, :])
                link(last)
                passed(dve)
                for b in range(G):
                    last = V.bn_aggr(bst[0:T, 32 + 2 * b:34 + 2 * b], bst[0:T, 6 * b:6 * b + 6])
                last.then_inc(var_ready, 1)

            def split_q(link, g, u):
                dve.wait_ge(q_high, g + 1)
                link(V.scalar_tensor_tensor(qres[:, :], ps[:, 6 + u, 0:GT], vecc[:, 2:3], qpart[u][:, 0, :], ALU.add,
                                            ALU.subtract))
                link(V.tensor_copy(qpart[u][:, 1, :], qres[:, :]))
                V.tensor_tensor(qpart[u][:, 2, :], qres[:, :], qpart[u][:, 1, :], ALU.subtract
                                ).then_inc(qpart_ready, 1)
                dve.wait_ge(qpart_ready, g + 1)
                link(V.tensor_reduce(qabs[:, bass.ds(g * G, G)], qpart[u][:, 0, :].rearrange("p (b t) -> p b t", b=G),
                                     AX.X, ALU.max, apply_absolute_value=True))

            def normalise_x1(link, g, u):
                dve.wait_ge(std_ready, g + 2)
                link(V.reciprocal(bst[0:T, 44:48], bst[0:T, 40:44]))
                for b in range(G):
                    last = V.tensor_scalar(osum[u][:, b, :], osum[u][:, b, :], bst[0:T, 32 + 2 * b:33 + 2 * b],
                                           bst[0:T, 44 + b:45 + b], ALU.subtract, ALU.mult)
                last.then_inc(x1_ready, 1)
                dve.wait_ge(x1_ready, g + 1)
                V.tensor_tensor(x1[:, bass.ds(g * G + 1, G), :], osum[u][:, :, :],
                                bias_s[:, 2, :].unsqueeze(1).broadcast_to([T, G, C]), ALU.add)

            def x1_group(g, u, base, split):
                link, n = chained(dve, chain, base)
                mix_in(link, g, u)
                if split:
                    split_q(link, g - 1, 1 - u)
                normalise_x1(link, g, u)
                assert n[0] == n_mix + split * n_split, n

            x1_group(0, 0, base_c, False)
            base_c += n_mix
            n_c = n_mix + n_split
            with dve.Fori(0, NG // 2 - 1) as gg:
                x1_group(gg * 2 + 1, 1, gg * (2 * n_c) + base_c, True)
                x1_group(gg * 2 + 2, 0, gg * (2 * n_c) + base_c + n_c, True)
            x1_group(NG - 1, 1, base_c + (NG - 2) * n_c, True)
            base2 = base_c + (NG - 1) * n_c
            link, n = chained(dve, chain, base2)
            split_q(link, NG - 1, 1)
            base2 += n[0]


            def take_bound(b, u, posted, base):
                dve.wait_ge(chore_posted, posted)
                V.tensor_reduce(clip_test[0:1, 0, 0:1], ps[0:1, 7, 0:H], AX.X, ALU.max).then_inc(chain, 1)
                dve.wait_ge(chain, base + 1)
                if not isinstance(b, int):
                    dve.wait_ge(amax_ready, b)
                V.tensor_scalar(flags[0:1, 1 + u:2 + u], clip_test[0:1, 0, 0:1], SCORE_BOUND * float(D) ** 0.5,
                                None, ALU.is_gt).then_inc(flag_ready, 1)
                dve.wait_ge(flag_ready, b + 1)
                dve.sem_inc(chore_taken, 1)

            def copy_sums(b):
                dve.wait_ge(pv_done, NU * b + 3)
                V.tensor_copy(acc_s[:, :], ps[:, 6, 0:4 * T]).then_inc(acc_copied, 1)

            def take_sums(posted, base):
                link, n = chained(dve, chain, base)
                dve.wait_ge(chore_posted, posted)
                v = ps[0:T, 7, :].rearrange("p (h n) -> p h n", n=32)
                link(V.reciprocal(rden[:, :], v[:, :, D]))
                link(V.tensor_tensor(attn[:, :, :], v[:, :, 0:D], rden[:, :].unsqueeze(2).broadcast_to([T, H, D]),
                                     ALU.mult))
                assert n[0] == n_sums
                V.tensor_tensor(attn[:, :, :], attn[:, :, :], bias_s[:, 1, :].rearrange("p (h d) -> p h d", d=D),
                                ALU.add).then_inc(chore_taken, 1)

            def take_attn(posted):
                dve.wait_ge(chore_posted, posted)
                V.tensor_copy(attnT[:, :], ps[:, 7, 0:T]).then_inc(chore_taken, 1)

            def take_out(b, posted):
                dve.wait_ge(chore_posted, posted)
                xb = x1[:, bass.ds(b, 1), :].rearrange("p o n -> p (o n)")
                V.tensor_tensor(xb, ps[0:T, 7, 0:C], xb, ALU.add).then_inc(chore_taken, 1)

            n_b = 3 * n_k + 1 + n_bound + n_sums

            def chore(b, u, name, base):
                if name[0] == "v":
                    spread_v(b + 1, 1 - u, int(name[1]))
                    return
                posted = PRO + NCH * b + CHORE[name] + 1
                if name[0] == "k":
                    take_k(b + 2, int(name[1]), posted, base + n_k * int(name[1]))
                    if name == "k2":
                        k_max(u, base)
                        bound_scores(b + 2, u)
                elif name == "bound":
                    take_bound(b + 2, u, posted, base + 3 * n_k + 1)
                elif name == "sums":
                    take_sums(posted, base + 3 * n_k + 1 + n_bound)
                elif name == "attn":
                    take_attn(posted)
                else:
                    take_out(b, posted)

            def attention(b, u, base):
                copy_sums(b)
                dve.wait_ge(flag_ready, b + 1)
                passed(dve)
                flag = dve.value_load(flags[0:1, 1 + u:2 + u], min_val=0, max_val=1)
                with dve.If(flag):
                    for q_stored in q_out:
                        dve.wait_ge(q_stored, 8 * NG + 16)
                    for n in range(NU):
                        un, m = n % 2, rows_of(n // 2)
                        dve.wait_ge(score1, NU * b + n + 1)
                        src = ps[0:m, 2 * (n % SS):2 * (n % SS) + 2, 0:400]
                        dst = rmax[0:m, un * UC:(un + 1) * UC].rearrange("p (a n) -> p a n", a=2)
                        if n < UNITS:
                            V.tensor_copy(dst, src).then_inc(score1_read, 1)
                        else:
                            dve.wait_ge(score1_read, NU * b + n - 1)
                            V.tensor_tensor(dst, src, dst, ALU.max).then_inc(score1_read, 1)
                    dve.wait_ge(score1_read, NU * (b + 1))
                    dve.sem_inc(rmax_ready, 1)
                    dve.wait_ge(amax_ready, b + 2)
                    for n in range(NU):
                        un, m = n % 2, rows_of(n // 2)
                        dve.wait_ge(scored, NU * b + n + 1)
                        dve.wait_ge(exp_done, NU * (b + 1) + n - 1)
                        V.tensor_tensor(dif[un][0:m, :].rearrange("p (a n) -> p a n", a=2),
                                        ps[0:m, 2 * (n % SS):2 * (n % SS) + 2, 0:400],
                                        amax[0:m, un * UC:(un + 1) * UC].rearrange("p (a n) -> p a n", a=2),
                                        ALU.subtract).then_inc(dif_ready, 1)
                        for at, name in sorted(CHORES + SPREADS):
                            if at == n:
                                chore(b, u, name, base)
                with dve.Else():
                    dve.sem_inc(score1_read, NU)
                    dve.sem_inc(rmax_ready, 1)
                    dve.sem_inc(dif_ready, NU)
                    for _, name in sorted(CHORES + SPREADS):
                        chore(b, u, name, base)

            for b in range(2):
                bound_scores(b, b)
                take_bound(b, b, PRO - 1 + b, base2)
                base2 += n_bound
            with dve.Fori(0, B // 2) as i:
                attention(2 * i, 0, i * (2 * n_b) + base2)
                attention(2 * i + 1, 1, i * (2 * n_b) + base2 + n_b)
            base2 += B * n_b
            copy_sums(B)
            take_sums(PRO + NCH * B + 1, base2)
            take_attn(PRO + NCH * B + 2)
            take_out(B, PRO + NCH * B + 3)
            dve.wait_ge(chore_taken, PRO + NCH * B + 3)

            def stats(link, src, o):
                for b in range(G):
                    last = V.bn_stats(sm3[:, o + 6 * b:o + 6 * b + 6], src(b))
                link(last)
                passed(dve)
                for b in range(G):
                    last = V.bn_aggr(sm3[:, o + 32 + 2 * b:o + 34 + 2 * b], sm3[:, o + 6 * b:o + 6 * b + 6])
                last.then_inc(var3, 1)

            def normalise(link, src, dst, o, done):
                dve.wait_ge(std3, done)
                link(V.reciprocal(sm3[:, o + 48:o + 52], sm3[:, o + 40:o + 44]))
                for b in range(G):
                    last = V.tensor_scalar(dst[:, b, :], src(b), sm3[:, o + 32 + 2 * b:o + 33 + 2 * b],
                                           sm3[:, o + 48 + b:o + 49 + b], ALU.subtract, ALU.mult)
                return last

            def wide(v, n):
                return v.unsqueeze(2).broadcast_to([T, G, n])

            def prepare(link, g, u, part, done):
                def src(b):
                    return x1[:, bass.ds(g * G + 1 + b, 1), :].rearrange("p o n -> p (o n)")
                if part == 0:
                    stats(link, src, PRE)
                elif part == 1:
                    normalise(link, src, x2[u], PRE, done).then_inc(x2_ready, 1)
                elif part == 2:
                    dve.wait_ge(x2T_posted, g + 1)
                    V.tensor_copy(x2T[u][:, :], ps[:, 0, 0:GT]).then_inc(x2T_ready, 1)
                elif part == 3:
                    dve.wait_ge(logits_posted, g + 1)
                    link(V.tensor_tensor(lg[:, :, :], ps[0:T, 1, 0:G * E].rearrange("p (b e) -> p b e", b=G),
                                         gb_s[:].unsqueeze(1).broadcast_to([T, G, E]), ALU.add))
                    link(V.tensor_reduce(sm3[:, 52:56], lg[:, :, :], AX.X, ALU.max))
                    V.tensor_tensor(lg[:, :, :], lg[:, :, :], wide(sm3[:, 52:56], E), ALU.subtract
                                    ).then_inc(logits_ready, 1)
                elif part == 4:
                    dve.wait_ge(gate_exp, g + 1)
                    link(V.tensor_reduce(sm3[:, 52:56], pr[u][:, :, :], AX.X, ALU.add))
                    link(V.reciprocal(sm3[:, 56:60], sm3[:, 52:56]))
                    link(V.tensor_tensor(pr[u][:, :, :], pr[u][:, :, :], wide(sm3[:, 56:60], E), ALU.mult))
                    passed(dve)
                    for b in range(G):
                        last = V.max(top[:, b, :], pr[u][:, b, :])
                    link(last)
                    passed(dve)
                    for b in range(G):
                        last = V.max_index(topi[:, b, :], top[:, b, :], pr[u][:, b, :])
                    link(last)
                    link(V.tensor_copy(topf[:, :, :], topi[:, :, :]))
                    iob = iota[0:T, :].unsqueeze(1).broadcast_to([T, G, E])
                    for k, dst in enumerate((cw[u], oh)):
                        last = V.tensor_tensor(dst[:, :, :], topf[:, :, k:k + 1].broadcast_to([T, G, E]), iob,
                                               ALU.is_equal)
                    link(last)
                    for k, dst in enumerate((cw[u], oh)):
                        last = V.tensor_tensor(dst[:, :, :], dst[:, :, :], pr[u][:, :, k:k + 1].broadcast_to(
                            [T, G, E]), ALU.mult)
                    link(last)
                    V.tensor_tensor(cw[u][:, :, :], cw[u][:, :, :], oh[:, :, :], ALU.add).then_inc(cw_ready, 1)
                elif part == 5:
                    dve.wait_ge(cwT_posted, g + 1)
                    V.tensor_copy(cwT[u][:, :], ps[0:E, 0, 0:GT]).then_inc(cwT_ready, 1)
                else:
                    dve.wait_ge(base_posted, g + 1)
                    link(V.tensor_tensor(x2[u][:, :, :], ps[0:T, 1, :].rearrange("p (b n) -> p b n", b=G),
                                         x2[u][:, :, :], ALU.add))

            n_3 = 15
            n_pro = 12

            def write_out(link, g, u, done):
                dve.wait_ge(out_stored[u], 8 * (g - u) + 16)
                normalise(link, lambda b: x2[u][:, b, :], fin[u], POST, done).then_inc(out_ready, 1)

            OWN = {1: 5, 3: 6}
            NEXT = {0: 0, 2: 1, 4: 2, 5: 3, 7: 4}

            def group(g, u, base, first, last_one):
                link, n = chained(dve, ch3, base)
                dve.wait_ge(cw_ready, g + 1)
                for e in range(E):
                    dve.wait_ge(h3_posted, g * E + e + 1 + 2)
                    if e:
                        dve.wait_ge(h3_used, g * E + e + 2)
                    for b in range(G):
                        last = V.scalar_tensor_tensor(x2[u][:, b, :], ps[0:T, 6 + e % 2, b * C:(b + 1) * C],
                                                      cw[u][:, b, e:e + 1], x2[u][:, b, :], ALU.mult, ALU.add)
                    last.then_inc(h3_used, 1)
                    if e in OWN:
                        if OWN[e] == 6:
                            dve.wait_ge(h3_used, g * E + e + 3)
                        prepare(link, g, u, OWN[e], 0)
                    if e == 1 and not first:
                        write_out(link, g - 1, 1 - u, 2 * g + 1)
                    if e in NEXT and not last_one:
                        if NEXT[e] == 1 and not first:
                            dve.wait_ge(out_ready, g)
                        prepare(link, g + 1, 1 - u, NEXT[e], 2 * g + 2)
                dve.wait_ge(h3_used, g * E + E + 2)
                stats(link, lambda b: x2[u][:, b, :], POST)
                if not last_one:
                    assert n[0] == n_3 - first, n

            for freed in (h1_ready, h3_used, h3_posted):
                dve.sem_inc(freed, 2)
            dve.wait_ge(experts_in, 16 * 5)
            for i in range(3):
                dve.wait_ge(kpart_out[i], 16 * (B + 2))
            link, n = chained(dve, ch3, 0)
            for part in range(5):
                prepare(link, 0, 0, part, 1)
            assert n[0] == n_pro, n
            group(0, 0, n_pro, True, False)
            n_pro += n_3 - 1
            with dve.Fori(0, NG // 2 - 1) as gg:
                group(gg * 2 + 1, 1, gg * (2 * n_3) + n_pro, False, False)
                group(gg * 2 + 2, 0, gg * (2 * n_3) + n_pro + n_3, False, False)
            n_pro += (NG - 2) * n_3
            group(NG - 1, 1, n_pro, False, True)
            link, n = chained(dve, ch3, n_pro + 3)
            write_out(link, NG - 1, 1, 2 * NG)


def kernel(**inputs):
    import numpy as np
    import concourse.bacc as bacc
    from concourse.bass_utils import run_bass_kernel_spmd

    a = {k: np.asarray(v) for k, v in inputs.items()}
    A, X, F = "L0_attn_", "L0_xattn_", "L0_ffn_"

    def wide(v, n):
        return np.ascontiguousarray(np.broadcast_to(v, (n,) + v.shape))

    order = (2 * (4 * np.arange(2)[:, None, None] + np.arange(4)) + np.arange(2)[:, None]).reshape(H)
    by_head = (D * order[:, None] + np.arange(D)).reshape(C)
    tm = np.stack([a[A + "time_mix_" + c].reshape(C) for c in "rkvg"], 1)
    arrays = {
        "xT": np.ascontiguousarray(a["x"].transpose(2, 0, 1)),
        "xn": a["x"],
        "ctxT": np.ascontiguousarray(a["ctx_1024"].transpose(0, 2, 1)),
        "Wrkvg": np.stack([a[A + "W_" + c].T for c in "rkvg"], 1),
        "brkvg": wide(np.concatenate([a[A + "b_" + c] for c in "rkvg"]), T),
        "mix": tm,
        "WoT": np.ascontiguousarray(a[A + "W_o"].T),
        "vec_c": np.stack([a[A + "gn_weight"], a[A + "gn_bias"], a[X + "bq"], a[X + "bk"]], 1),
        "bias_t": wide(np.stack([a[A + "b_o"], a[X + "bv"][by_head], a[X + "bo"], a[X + "bo"]]), T),
        "dec_in": np.repeat(a[A + "decay"].reshape(NQ, Q4), B, 0),
        "eta_in": wide(np.tile(a[A + "eta"].reshape(H), 2), T),
        "Wq": a[X + "Wq"], "Wk": a[X + "Wk"], "Wv": a[X + "Wv"], "Wxo": a[X + "Wo"][by_head],
        "gate_wT": np.ascontiguousarray(a[F + "gate_w"].T),
        "gate_b": wide(a[F + "gate_b"], T),
        "dec_all_in": np.stack([a[A + "decay"].reshape(H), a[A + "eta"].reshape(H)])[None],
        "headsel_in": np.repeat(np.eye(H, dtype=np.float32), D, 0),
        "w1": a[F + "w1"], "w2": a[F + "w2"], "w3": a[F + "w3"],
        "b12": np.ascontiguousarray(np.stack([a[F + "b1"], a[F + "b2"]]).transpose(2, 0, 1)),
        "b3": a[F + "b3"],
        "ident_in": np.eye(128, dtype=np.float32),
        "iota_in": wide(np.arange(E, dtype=np.float32), 128),
    }
    nc = bacc.Bacc("TRN2", target_bir_lowering=False, num_devices=1)
    args = [nc.dram_tensor(n + "_dram", v.shape, mybir.dt.from_np(v.dtype), kind="ExternalInput").ap()
            for n, v in arrays.items()]
    args.append(nc.dram_tensor("out_dram", (B, T, C), F32, kind="ExternalOutput").ap())
    build(nc, *args)
    r = run_bass_kernel_spmd(nc, [{n + "_dram": v for n, v in arrays.items()}], core_ids=[0])
    return r.results[0]["out_dram"]
```
